# Optimizing a Trainium2 kernel written in Bass

```python
import numpy as np
import jax
import jax.numpy as jnp

def _softmax(x, axis=-1):
    return jax.nn.softmax(x, axis=axis)

def _gelu(x):
    return jax.nn.gelu(x, approximate=True)

def _silu(x):
    return jax.nn.silu(x)

def _sigmoid(x):
    return jax.nn.sigmoid(x)

def _layernorm(x, axis=-1, eps=1e-05):
    m = jnp.mean(x, axis=axis, keepdims=True)
    v = jnp.var(x, axis=axis, keepdims=True)
    return (x - m) / jnp.sqrt(v + eps)

def _scatter_add(tgt, idx, src, axis=0):
    return tgt.at[idx].add(src)

def _segment_sum(src, seg, n):
    return jax.ops.segment_sum(src, seg, n)
kernel_name = 'mk_lm_tower_d1_tok_ids1024_r4_2139ee'

def setup_inputs(seed: int=0):
    np.random.seed(seed)
    _w = jnp.asarray

    def _rec_inputs():
        import jax
        import jax.numpy as jnp
        _rk = jax.random.key(seed)
        x = jax.random.randint(jax.random.fold_in(_rk, 1), (32, 512), 0, 12564, jnp.int32)
        return x
    x = _rec_inputs()

    def _L0_tok_setup():
        import jax, jax.numpy as jnp
        import numpy as np
        N_BUCKETS = 262144
        EDIM = 128
        MODEL_DIM = 256

        def hash_ids(toks, mod):
            t = toks.astype(jnp.int32)
            m = jnp.int32(mod - 1)
            first = jnp.full(t.shape[:-1] + (1,), m, dtype=jnp.int32)
            rest = jnp.mod(jnp.bitwise_xor(jnp.int32(36313) * t[..., 1:], jnp.int32(27191) * t[..., :-1]), m)
            return jnp.concatenate([first, rest], axis=-1)
        key = jax.random.key(seed)
        k1, k2, k3 = jax.random.split(key, 3)
        token_ids = jax.random.randint(k1, (8, 1024), 0, 50257, dtype=jnp.int32).astype(jnp.int64)
        emb_weight = jax.random.normal(k2, (N_BUCKETS, EDIM), dtype=jnp.float32) * 0.02
        proj_weight = jax.random.normal(k3, (MODEL_DIM, EDIM), dtype=jnp.float32) * 0.02
        scale = jnp.float32(0.05)
        return {'token_ids': token_ids, 'emb_weight': emb_weight, 'proj_weight': proj_weight, 'scale': scale}
    _L0_tok_all = _L0_tok_setup()
    _L0_tok_in = {k: v for k, v in _L0_tok_all.items() if k in ('emb_weight', 'proj_weight', 'scale')}
    del _L0_tok_all

    def _L0_attn_setup():
        import jax, jax.numpy as jnp
        import numpy as np
        B, S, D = (2, 256, 256)
        NH = 8
        QK = D // 2
        V = D
        DQK = QK // NH
        DV = V // NH
        CAP = 15.0
        EPS = 1e-06

        def soft_cap(t, cap=CAP):
            return cap * jnp.tanh(t / cap)

        def _mlstm_forward(x, Wq, Wk, Wv, Wog, Wi, bi, Wf, bf, ln_w, ln_b, Wout):
            Bx, Sx, _ = x.shape
            q = (x @ Wq.T).reshape(Bx, Sx, NH, DQK)
            k = (x @ Wk.T).reshape(Bx, Sx, NH, DQK)
            v = (x @ Wv.T).reshape(Bx, Sx, NH, DV)
            o_preact = x @ Wog.T
            i_pre = soft_cap(x @ Wi.T + bi)
            f_pre = soft_cap(x @ Wf.T + bf)
            qT = jnp.moveaxis(q, 1, 0)
            kT = jnp.moveaxis(k, 1, 0)
            vT = jnp.moveaxis(v, 1, 0)
            iT = jnp.moveaxis(i_pre, 1, 0)
            fT = jnp.moveaxis(f_pre, 1, 0)
            qk_scale = DQK ** (-0.5)

            def step(carry, inp):
                C, n, m = carry
                q_t, k_t, v_t, i_t, f_t = inp
                m_new = jnp.maximum(f_t + m, i_t)
                f_act = jnp.exp(f_t + m - m_new)
                i_act = jnp.exp(i_t - m_new)
                C = f_act[..., None, None] * C + i_act[..., None, None] * (k_t[..., :, None] * v_t[..., None, :])
                n = f_act[..., None] * n + i_act[..., None] * k_t
                qs = q_t * qk_scale
                num = jnp.einsum('bhk,bhkv->bhv', qs, C)
                qn = jnp.einsum('bhk,bhk->bh', qs, n)
                denom = jnp.maximum(jnp.abs(qn), jnp.exp(-m_new)) + 1e-06
                h_t = num / denom[..., None]
                return ((C, n, m_new), h_t)
            C0 = jnp.zeros((Bx, NH, DQK, DV), x.dtype)
            n0 = jnp.zeros((Bx, NH, DQK), x.dtype)
            m0 = jnp.zeros((Bx, NH), x.dtype)
            _, hs = jax.lax.scan(step, (C0, n0, m0), (qT, kT, vT, iT, fT))
            h = jnp.moveaxis(hs, 0, 1).reshape(Bx, Sx, NH * DV)
            mu = jnp.mean(h, axis=-1, keepdims=True)
            var = jnp.mean((h - mu) ** 2, axis=-1, keepdims=True)
            h_norm = (h - mu) * jax.lax.rsqrt(var + EPS) * ln_w + ln_b
            h_out = jax.nn.sigmoid(o_preact) * h_norm
            y = h_out @ Wout.T
            return y
        key = jax.random.key(seed)
        ks = jax.random.split(key, 12)
        sc = 0.02
        return {'x': jax.random.normal(ks[0], (B, S, D), jnp.float32), 'Wq': jax.random.normal(ks[1], (QK, D), jnp.float32) * sc, 'Wk': jax.random.normal(ks[2], (QK, D), jnp.float32) * sc, 'Wv': jax.random.normal(ks[3], (V, D), jnp.float32) * sc, 'Wog': jax.random.normal(ks[4], (V, D), jnp.float32) * sc, 'Wi': jax.random.normal(ks[5], (NH, D), jnp.float32) * sc, 'bi': jax.random.normal(ks[6], (NH,), jnp.float32) * sc, 'Wf': jax.random.normal(ks[7], (NH, D), jnp.float32) * sc, 'bf': jax.random.normal(ks[8], (NH,), jnp.float32) * sc + 3.0, 'ln_w': jnp.ones((NH * DV,), jnp.float32), 'ln_b': jnp.zeros((NH * DV,), jnp.float32), 'Wout': jax.random.normal(ks[9], (D, V), jnp.float32) * sc}
    _L0_attn_all = _L0_attn_setup()
    _L0_attn_in = {k: v for k, v in _L0_attn_all.items() if k in ('Wq', 'Wk', 'Wv', 'Wog', 'Wi', 'bi', 'Wf', 'bf', 'ln_w', 'ln_b', 'Wout')}
    del _L0_attn_all

    def _L0_ffn_setup():
        import jax, jax.numpy as jnp
        import numpy as np
        B, S, D, H, M, E, K = (4, 512, 256, 512, 64, 8, 2)

        def _layernorm(x, g, b, eps=1e-05):
            mu = x.mean(-1, keepdims=True)
            var = ((x - mu) ** 2).mean(-1, keepdims=True)
            return (x - mu) * jax.lax.rsqrt(var + eps) * g + b

        def _forward(inputs_embeds, enc_W, enc_b, s2c_W, s2c_b, rW1, rb1, rW2, rb2, We1, be1, We2, be2, c2s_W, c2s_b, dec_W, dec_b, ln_g, ln_b):
            b, s, _ = inputs_embeds.shape
            spikes_enc = jax.nn.sigmoid(inputs_embeds @ enc_W + enc_b)
            flat = spikes_enc.reshape(b * s, H)
            cont = flat @ s2c_W + s2c_b
            logits = jnp.tanh(cont @ rW1 + rb1) @ rW2 + rb2
            probs = jax.nn.softmax(logits, axis=-1)
            topw, topi = jax.lax.top_k(probs, K)
            w = topw / topw.sum(-1, keepdims=True)
            gates = (jax.nn.one_hot(topi, E, dtype=cont.dtype) * w[..., None]).sum(1)
            h = jax.nn.relu(jnp.einsum('nm,emh->enh', cont, We1) + be1[:, None, :])
            expert_out = jnp.einsum('enh,ehm->enm', h, We2) + be2[:, None, :]
            output_flat = jnp.einsum('enm,ne->nm', expert_out, gates)
            spikes_moe = jax.nn.sigmoid(output_flat @ c2s_W + c2s_b).reshape(b, s, H)
            decoded = jax.nn.sigmoid(spikes_moe @ dec_W + dec_b)
            return _layernorm(decoded, ln_g, ln_b)
        key = jax.random.key(seed)
        ks = jax.random.split(key, 10)
        r = lambda k, shape: jax.random.normal(k, shape, dtype=jnp.float32) * 0.02
        return {'inputs_embeds': jax.random.normal(ks[0], (B, S, D), dtype=jnp.float32), 'enc_W': r(ks[1], (D, H)), 'enc_b': jnp.zeros((H,), jnp.float32), 's2c_W': r(ks[2], (H, M)), 's2c_b': jnp.zeros((M,), jnp.float32), 'rW1': r(ks[3], (M, 64)), 'rb1': jnp.zeros((64,), jnp.float32), 'rW2': r(ks[4], (64, E)), 'rb2': jnp.zeros((E,), jnp.float32), 'We1': r(ks[5], (E, M, H // 2)), 'be1': jnp.zeros((E, H // 2), jnp.float32), 'We2': r(ks[6], (E, H // 2, M)), 'be2': jnp.zeros((E, M), jnp.float32), 'c2s_W': r(ks[7], (M, H)), 'c2s_b': jnp.zeros((H,), jnp.float32), 'dec_W': r(ks[8], (H, D)), 'dec_b': jnp.zeros((D,), jnp.float32), 'ln_g': jnp.ones((D,), jnp.float32), 'ln_b': jnp.zeros((D,), jnp.float32)}
    _L0_ffn_all = _L0_ffn_setup()
    _L0_ffn_in = {k: v for k, v in _L0_ffn_all.items() if k in ('enc_W', 'enc_b', 's2c_W', 's2c_b', 'rW1', 'rb1', 'rW2', 'rb2', 'We1', 'be1', 'We2', 'be2', 'c2s_W', 'c2s_b', 'dec_W', 'dec_b', 'ln_g', 'ln_b')}
    del _L0_ffn_all
    return {'x': x, 'L0_tok_emb_weight': _L0_tok_in['emb_weight'], 'L0_tok_proj_weight': _L0_tok_in['proj_weight'], 'L0_tok_scale': _L0_tok_in['scale'], 'L0_attn_Wq': _L0_attn_in['Wq'], 'L0_attn_Wk': _L0_attn_in['Wk'], 'L0_attn_Wv': _L0_attn_in['Wv'], 'L0_attn_Wog': _L0_attn_in['Wog'], 'L0_attn_Wi': _L0_attn_in['Wi'], 'L0_attn_bi': _L0_attn_in['bi'], 'L0_attn_Wf': _L0_attn_in['Wf'], 'L0_attn_bf': _L0_attn_in['bf'], 'L0_attn_ln_w': _L0_attn_in['ln_w'], 'L0_attn_ln_b': _L0_attn_in['ln_b'], 'L0_attn_Wout': _L0_attn_in['Wout'], 'L0_ffn_enc_W': _L0_ffn_in['enc_W'], 'L0_ffn_enc_b': _L0_ffn_in['enc_b'], 'L0_ffn_s2c_W': _L0_ffn_in['s2c_W'], 'L0_ffn_s2c_b': _L0_ffn_in['s2c_b'], 'L0_ffn_rW1': _L0_ffn_in['rW1'], 'L0_ffn_rb1': _L0_ffn_in['rb1'], 'L0_ffn_rW2': _L0_ffn_in['rW2'], 'L0_ffn_rb2': _L0_ffn_in['rb2'], 'L0_ffn_We1': _L0_ffn_in['We1'], 'L0_ffn_be1': _L0_ffn_in['be1'], 'L0_ffn_We2': _L0_ffn_in['We2'], 'L0_ffn_be2': _L0_ffn_in['be2'], 'L0_ffn_c2s_W': _L0_ffn_in['c2s_W'], 'L0_ffn_c2s_b': _L0_ffn_in['c2s_b'], 'L0_ffn_dec_W': _L0_ffn_in['dec_W'], 'L0_ffn_dec_b': _L0_ffn_in['dec_b'], 'L0_ffn_ln_g': _L0_ffn_in['ln_g'], 'L0_ffn_ln_b': _L0_ffn_in['ln_b']}

def reference(x, L0_tok_emb_weight, L0_tok_proj_weight, L0_tok_scale, L0_attn_Wq, L0_attn_Wk, L0_attn_Wv, L0_attn_Wog, L0_attn_Wi, L0_attn_bi, L0_attn_Wf, L0_attn_bf, L0_attn_ln_w, L0_attn_ln_b, L0_attn_Wout, L0_ffn_enc_W, L0_ffn_enc_b, L0_ffn_s2c_W, L0_ffn_s2c_b, L0_ffn_rW1, L0_ffn_rb1, L0_ffn_rW2, L0_ffn_rb2, L0_ffn_We1, L0_ffn_be1, L0_ffn_We2, L0_ffn_be2, L0_ffn_c2s_W, L0_ffn_c2s_b, L0_ffn_dec_W, L0_ffn_dec_b, L0_ffn_ln_g, L0_ffn_ln_b):
    import jax
    import jax.numpy as jnp

    def _L0_tok_ref(token_ids, emb_weight, proj_weight, scale):
        import jax, jax.numpy as jnp
        import numpy as np
        N_BUCKETS = 262144
        EDIM = 128
        MODEL_DIM = 256

        def hash_ids(toks, mod):
            t = toks.astype(jnp.int32)
            m = jnp.int32(mod - 1)
            first = jnp.full(t.shape[:-1] + (1,), m, dtype=jnp.int32)
            rest = jnp.mod(jnp.bitwise_xor(jnp.int32(36313) * t[..., 1:], jnp.int32(27191) * t[..., :-1]), m)
            return jnp.concatenate([first, rest], axis=-1)
        ids = hash_ids(token_ids, N_BUCKETS)
        h = emb_weight[ids]
        h = jnp.einsum('bse,me->bsm', h, proj_weight)
        return h * scale.astype(h.dtype)

    def _L0_attn_ref(x, Wq, Wk, Wv, Wog, Wi, bi, Wf, bf, ln_w, ln_b, Wout):
        import jax, jax.numpy as jnp
        import numpy as np
        B, S, D = (2, 256, 256)
        NH = 8
        QK = D // 2
        V = D
        DQK = QK // NH
        DV = V // NH
        CAP = 15.0
        EPS = 1e-06

        def soft_cap(t, cap=CAP):
            return cap * jnp.tanh(t / cap)

        def _mlstm_forward(x, Wq, Wk, Wv, Wog, Wi, bi, Wf, bf, ln_w, ln_b, Wout):
            Bx, Sx, _ = x.shape
            q = (x @ Wq.T).reshape(Bx, Sx, NH, DQK)
            k = (x @ Wk.T).reshape(Bx, Sx, NH, DQK)
            v = (x @ Wv.T).reshape(Bx, Sx, NH, DV)
            o_preact = x @ Wog.T
            i_pre = soft_cap(x @ Wi.T + bi)
            f_pre = soft_cap(x @ Wf.T + bf)
            qT = jnp.moveaxis(q, 1, 0)
            kT = jnp.moveaxis(k, 1, 0)
            vT = jnp.moveaxis(v, 1, 0)
            iT = jnp.moveaxis(i_pre, 1, 0)
            fT = jnp.moveaxis(f_pre, 1, 0)
            qk_scale = DQK ** (-0.5)

            def step(carry, inp):
                C, n, m = carry
                q_t, k_t, v_t, i_t, f_t = inp
                m_new = jnp.maximum(f_t + m, i_t)
                f_act = jnp.exp(f_t + m - m_new)
                i_act = jnp.exp(i_t - m_new)
                C = f_act[..., None, None] * C + i_act[..., None, None] * (k_t[..., :, None] * v_t[..., None, :])
                n = f_act[..., None] * n + i_act[..., None] * k_t
                qs = q_t * qk_scale
                num = jnp.einsum('bhk,bhkv->bhv', qs, C)
                qn = jnp.einsum('bhk,bhk->bh', qs, n)
                denom = jnp.maximum(jnp.abs(qn), jnp.exp(-m_new)) + 1e-06
                h_t = num / denom[..., None]
                return ((C, n, m_new), h_t)
            C0 = jnp.zeros((Bx, NH, DQK, DV), x.dtype)
            n0 = jnp.zeros((Bx, NH, DQK), x.dtype)
            m0 = jnp.zeros((Bx, NH), x.dtype)
            _, hs = jax.lax.scan(step, (C0, n0, m0), (qT, kT, vT, iT, fT))
            h = jnp.moveaxis(hs, 0, 1).reshape(Bx, Sx, NH * DV)
            mu = jnp.mean(h, axis=-1, keepdims=True)
            var = jnp.mean((h - mu) ** 2, axis=-1, keepdims=True)
            h_norm = (h - mu) * jax.lax.rsqrt(var + EPS) * ln_w + ln_b
            h_out = jax.nn.sigmoid(o_preact) * h_norm
            y = h_out @ Wout.T
            return y
        return _mlstm_forward(x, Wq, Wk, Wv, Wog, Wi, bi, Wf, bf, ln_w, ln_b, Wout)

    def _L0_ffn_ref(inputs_embeds, enc_W, enc_b, s2c_W, s2c_b, rW1, rb1, rW2, rb2, We1, be1, We2, be2, c2s_W, c2s_b, dec_W, dec_b, ln_g, ln_b):
        import jax, jax.numpy as jnp
        import numpy as np
        B, S, D, H, M, E, K = (4, 512, 256, 512, 64, 8, 2)

        def _layernorm(x, g, b, eps=1e-05):
            mu = x.mean(-1, keepdims=True)
            var = ((x - mu) ** 2).mean(-1, keepdims=True)
            return (x - mu) * jax.lax.rsqrt(var + eps) * g + b

        def _forward(inputs_embeds, enc_W, enc_b, s2c_W, s2c_b, rW1, rb1, rW2, rb2, We1, be1, We2, be2, c2s_W, c2s_b, dec_W, dec_b, ln_g, ln_b):
            b, s, _ = inputs_embeds.shape
            spikes_enc = jax.nn.sigmoid(inputs_embeds @ enc_W + enc_b)
            flat = spikes_enc.reshape(b * s, H)
            cont = flat @ s2c_W + s2c_b
            logits = jnp.tanh(cont @ rW1 + rb1) @ rW2 + rb2
            probs = jax.nn.softmax(logits, axis=-1)
            topw, topi = jax.lax.top_k(probs, K)
            w = topw / topw.sum(-1, keepdims=True)
            gates = (jax.nn.one_hot(topi, E, dtype=cont.dtype) * w[..., None]).sum(1)
            h = jax.nn.relu(jnp.einsum('nm,emh->enh', cont, We1) + be1[:, None, :])
            expert_out = jnp.einsum('enh,ehm->enm', h, We2) + be2[:, None, :]
            output_flat = jnp.einsum('enm,ne->nm', expert_out, gates)
            spikes_moe = jax.nn.sigmoid(output_flat @ c2s_W + c2s_b).reshape(b, s, H)
            decoded = jax.nn.sigmoid(spikes_moe @ dec_W + dec_b)
            return _layernorm(decoded, ln_g, ln_b)
        return _forward(inputs_embeds, enc_W, enc_b, s2c_W, s2c_b, rW1, rb1, rW2, rb2, We1, be1, We2, be2, c2s_W, c2s_b, dec_W, dec_b, ln_g, ln_b)
    h = _L0_tok_ref(x, L0_tok_emb_weight, L0_tok_proj_weight, L0_tok_scale)
    h = h + _L0_attn_ref(_layernorm(h, axis=-1), L0_attn_Wq, L0_attn_Wk, L0_attn_Wv, L0_attn_Wog, L0_attn_Wi, L0_attn_bi, L0_attn_Wf, L0_attn_bf, L0_attn_ln_w, L0_attn_ln_b, L0_attn_Wout)
    h = h + _L0_ffn_ref(_layernorm(h, axis=-1), L0_ffn_enc_W, L0_ffn_enc_b, L0_ffn_s2c_W, L0_ffn_s2c_b, L0_ffn_rW1, L0_ffn_rb1, L0_ffn_rW2, L0_ffn_rb2, L0_ffn_We1, L0_ffn_be1, L0_ffn_We2, L0_ffn_be2, L0_ffn_c2s_W, L0_ffn_c2s_b, L0_ffn_dec_W, L0_ffn_dec_b, L0_ffn_ln_g, L0_ffn_ln_b)
    return h

_drawn_inputs = setup_inputs


def setup_inputs(seed=0):
    import zlib

    import numpy as np

    out = dict(_drawn_inputs(seed))
    spreads = {'L0_attn_ln_w': (1.0, 0.6),
     'L0_attn_ln_b': (0.0, 0.51),
     'L0_ffn_enc_b': (0.0, 0.8),
     'L0_ffn_s2c_b': (0.0, 0.8),
     'L0_ffn_rb1': (0.0, 0.8),
     'L0_ffn_rb2': (0.0, 0.8),
     'L0_ffn_be1': (0.0, 0.8),
     'L0_ffn_be2': (0.0, 0.8),
     'L0_ffn_c2s_b': (0.0, 0.375),
     'L0_ffn_dec_b': (0.0, 0.1),
     'L0_ffn_ln_g': (1.0, 0.2),
     'L0_ffn_ln_b': (0.0, 0.1)}
    factors = {'L0_attn_Wog': 8.0,
     'L0_attn_Wi': 64.0,
     'L0_attn_bi': 46.971,
     'L0_attn_Wf': 64.0,
     'L0_attn_bf': 64.0,
     'L0_ffn_enc_W': 8.0,
     'L0_ffn_s2c_W': 8.0,
     'L0_ffn_rW1': 8.0,
     'L0_ffn_rW2': 8.0,
     'L0_ffn_We1': 8.0,
     'L0_ffn_We2': 8.0,
     'L0_ffn_c2s_W': 8.0}
    for name, (base, spread) in spreads.items():
        noise = np.random.default_rng([zlib.crc32(name.encode()), seed]).standard_normal(out[name].shape)
        drawn = base * np.exp(spread * noise) if base else spread * noise
        out[name] = jnp.asarray(drawn.astype(out[name].dtype))
    for name, factor in factors.items():
        out[name] = (out[name] * factor).astype(out[name].dtype)
    return out
```

```python
from contextlib import ExitStack

import concourse.bass as bass
from concourse import mybir

F32 = mybir.dt.float32
I32 = mybir.dt.int32
U32 = mybir.dt.uint32
ACT = mybir.ActivationFunctionType
ALU = mybir.AluOpType

P = 128
NB, S = 32, 512
NT = S // P
TILES = NB * NT
BUCKETS, EDIM, D = 262144, 128, 256
NH, DQK, DV = 8, 16, 32
DV1 = DV + 1
H, M, E, HE = 512, 64, 8, 256
NCH = E * HE // P
CAP = 15.0
HASH_CUR, HASH_PREV, MOD = 36313, 27191, BUCKETS - 1
CH, CV, CO, CF, CI, CK, CQ, CEND = 0, 256, 512, 768, 776, 784, 912, 1040
NKG = CQ - CO


class PerBatch:

    def __init__(self, sem, per):
        self.sem, self.per = sem, per

    def at(self, b, n):
        return b * self.per + n


def bc(ap, shape):
    return ap.unsqueeze(len(ap.shape)).broadcast_to(shape)


def bc1(ap, shape):
    return ap.unsqueeze(1).broadcast_to(shape)


def tower(nc, A, out):
    with ExitStack() as ctx:
        def sb(name, shape, dt=F32):
            return ctx.enter_context(nc.sbuf_tensor(name, shape, dt))

        def sem(name):
            return ctx.enter_context(nc.semaphore(name))

        def per(name, n):
            return PerBatch(sem(name), n)

        gb = sb("gb", [P, E, S])
        W = sb("W", [P, 2, NH * P])
        wall = gb[:, 0:4, :].rearrange("p a b -> p (a b)")[:, 0:2 * (CEND - CV)].rearrange("p (t n) -> p t n", t=2)
        projTc = gb[:, 4, 0:D]
        projc = gb[:, 5, 0:2 * P].rearrange("p (t n) -> p t n", t=2)
        hash_tiles = [W[:, n // 8, (n % 8) * P:(n % 8 + 1) * P] for n in range(10)]
        tok, tokp, mulc, mulp, hx, hlo, hhi = (t.bitcast(I32) for t in hash_tiles[:7])
        hf, hfix, idxf = hash_tiles[7:]
        ident = sb("ident", [P, P])
        headmask = sb("headmask", [P, NH])
        headsel = sb("headsel", [NH, P])
        blockmask = sb("blockmask", [P, NH, DV1])
        notstart = sb("notstart", [NH, S])
        iota8 = sb("iota8", [P, E])
        halves = sb("halves", [P, P])
        mhalf = sb("mhalf", [P, NT])
        scale = sb("scale", [P, 1])
        projT = sb("projT", [P, D])
        wfold = sb("wfold", [P, CEND])
        bfi = sb("bfi", [NH, 2])
        mixw = sb("mixw", [P, D])
        mixb = sb("mixb", [P, D])
        woutT = sb("woutT", [P, 2, D])
        encw = sb("encw", [P, 2, H])
        encb = sb("encb", [P, 4])
        s2cw = sb("s2cw", [P, 4, M])
        s2cwh = sb("s2cwh", [P, 4, M])
        s2cb = sb("s2cb", [M, 1])
        rw1 = sb("rw1", [M, M])
        rb1 = sb("rb1", [M, 1])
        rw2 = sb("rw2", [M, E])
        rb2 = sb("rb2", [P, E])
        we1 = sb("we1", [M, E * HE])
        be1n = sb("be1n", [P, NCH])
        be1pad = sb("be1pad", [P, NCH, E])
        we2 = sb("we2", [P, NCH, M])
        be2 = sb("be2", [E, M])
        biasout = sb("biasout", [E, M])
        c2sw = sb("c2sw", [M, H])
        c2sb = sb("c2sb", [P, 4])
        decw = sb("decw", [P, 4, D])
        decb = sb("decb", [P, D])
        lng = sb("lng", [P, D])
        lnb = sb("lnb", [P, D])
        idx = sb("idx", [P, P], I32)
        idxs = sb("idxs", [P, 2, NT], I32)
        e = sb("e", [P, 2, NT, EDIM])
        eT = sb("eT", [P, S])
        hv = sb("hv", [P, NT, 2 * D])
        kg = sb("kg", [P, NT, NKG])
        bst = sb("bst", [P, NT, 6])
        mv = sb("mv", [P, NT, 2])
        vareps = sb("vareps", [P, NT])
        rs = sb("rs", [P, NT])
        rsh = sb("rsh", [P, NT])
        fi = sb("fi", [P, 2, NT, NH])
        fi8 = sb("fi8", [NH, 2, S])
        fc = sb("fc", [NH, 2, S])
        Fs = sb("Fs", [NH, S])
        ex = sb("ex", [P, S])
        G = sb("G", [NH, S])
        mst = sb("mst", [NH, NT + 1])
        dcin = sb("dcin", [NH, NT])
        dc8 = sb("dc8", [NH, NT])
        exs = sb("exs", [P, NT, 72])
        nega = sb("nega", [P, NT, NH])
        gtm = sb("gtm", [P, NT, NH])
        dcol = sb("dcol", [P, NT])
        qT = sb("qT", [P, S])
        kT = sb("kT", [P, S])
        qbd = sb("qbd", [P, NH, S])
        vh = sb("vh", [P, NT, NH, DV1])
        wv = sb("wv", [P, NT - 1, NH, DV1])
        sg = sb("sg", [P, NT, D])
        num = sb("num", [P, NT, NH, DV1])
        tmpI = sb("tmpI", [P, NH, DV1])
        tmpU = sb("tmpU", [P, NH, DV1])
        cbd = sb("cbd", [P, NH, DV1])
        den = sb("den", [P, NT, NH])
        hm = sb("hm", [P, NT, D])
        hw = sb("hw", [P, NT, D])
        hoT = sb("hoT", [P, 2, S])
        vareps2 = sb("vareps2", [P, NT])
        rs2 = sb("rs2", [P, NT])
        h2 = sb("h2", [P, 2, NT, D])
        vareps3 = sb("vareps3", [P, NT])
        rs3 = sb("rs3", [P, NT])
        xn = sb("xn", [P, NT, D])
        xnT = sb("xnT", [P, 2, S])
        bstf = sb("bstf", [P, NT, 6])
        mvf = sb("mvf", [P, NT, 2])
        sp = sb("sp", [P, 4, S])
        cont = sb("cont", [M, S])
        r1T = sb("r1T", [M, S])
        lg = sb("lg", [P, NT, E])
        mx8 = sb("mx8", [P, NT, 8])
        ix8 = sb("ix8", [P, NT, 8], U32)
        ixf = sb("ixf", [P, NT, 2])
        dl = sb("dl", [P, NT])
        e2 = sb("e2", [P, NT])
        s1 = sb("s1", [P, NT])
        w12 = sb("w12", [P, NT, 2])
        eq0 = sb("eq0", [P, NT, E])
        eq1 = sb("eq1", [P, NT, E])
        g = sb("g", [P, NT, E])
        gT = sb("gT", [E, S])
        hid = sb("hid", [P, 4, S])
        oT = sb("oT", [M, S])
        z = sb("z", [P, NT, D])
        vareps4 = sb("vareps4", [P, NT])
        rs4 = sb("rs4", [P, NT])
        gg = sb("gg", [P, NT, D])

        X = [ctx.enter_context(nc.psum_tensor(f"X{i}", [P, 512], F32)) for i in range(5)]
        Y = [ctx.enter_context(nc.psum_tensor(f"Y{i}", [P, 512], F32)) for i in range(3)]

        passed = sem("passed")
        loaded = sem("loaded")
        tok_in = sem("tok_in")
        pconst = sem("pconst")
        mults = sem("mults")
        hashed = sem("hashed")
        hash_t = sem("hash_t")
        idx_ok = sem("idx_ok")
        prep = sem("prep")
        pprep = sem("pprep")
        gathered = [sem(f"gathered{u}") for u in range(2)]
        idx_copied = per("idx_copied", 1)
        eT_t, eT_ok = per("eT_t", 1), per("eT_ok", 1)
        hv_t, kg_t, hv_ok, kg_ok = per("hv_t", 4), per("kg_t", 4), per("hv_ok", 4), per("kg_ok", 4)
        st1, rs_ok, fi_ok, fiT_t, fi8_ok = per("st1", 3), per("rs_ok", 1), per("fi_ok", 2), per("fiT_t", 1), per("fi8_ok", 1)
        scan, dc_ok, exT_t, exs_ok = per("scan", 15), per("dc_ok", 1), per("exT_t", 1), per("exs_ok", 1)
        qk_t, kT_ok, qT_ok, qbd_ok = per("qk_t", 2), per("kT_ok", 1), per("qT_ok", 1), per("qbd_ok", 1)
        vh_ok, wv_ok, sg_ok = per("vh_ok", 1), per("wv_ok", 3), per("sg_ok", 1)
        gb_t, relu_ok, masked, dm_ok = per("gb_t", 4), per("relu_ok", 4), per("masked", 4), per("dm_ok", 4)
        s_t, p_ok, num_t, int_t, u_t = per("s_t", 4), per("p_ok", 4), per("num_t", 4), per("int_t", 3), per("u_t", 3)
        num_ok, tmpi_ok, tmpu_ok, cbd_ok = per("num_ok", 4), per("tmpi_ok", 3), per("tmpu_ok", 2), per("cbd_ok", 3)
        nrm, rs2_ok, hn_ok, hw_ok, ho_ok = per("nrm", 10), per("rs2_ok", 1), per("hn_ok", 1), per("hw_ok", 2), per("ho_ok", 1)
        hoT_t, hoTa, hoTd = per("hoT_t", 2), per("hoTa", 1), per("hoTd", 1)
        y_t, h2_ok, st3, rs3_ok, xn_ok = per("y_t", 2), per("h2_ok", 2), per("st3", 3), per("rs3_ok", 1), per("xn_ok", 1)
        xnT_t, xnTa, xnTd = per("xnT_t", 2), per("xnTa", 1), per("xnTd", 1)
        enc_t, enc_ok, s2c_t, cont_ok = per("enc_t", 4), per("enc_ok", 4), per("s2c_t", 1), per("cont_ok", 1)
        r1_t, r1_ok, r2_t, top, e2_ok = per("r1_t", 1), per("r1_ok", 1), per("r2_t", 1), per("top", 13), per("e2_ok", 1)
        gT_t, gT_ok, gbc_t, gb_ok = per("gT_t", 1), per("gT_ok", 1), per("gbc_t", 8), per("gb_ok", 8)
        w1_t, hid_ok, w2_t, o_t, oT_ok = per("w1_t", 16), per("hid_ok", 16), per("w2_t", 16), per("o_t", 1), per("oT_ok", 1)
        c2s_t, c2s_ok, dec_t, z_ok, tt_ok = per("c2s_t", 4), per("c2s_ok", 4), per("dec_t", 2), per("z_ok", 2), per("tt_ok", 2)
        st4, rs4_ok, tn_ok, gg_ok, out_ok = per("st4", 3), per("rs4_ok", 1), per("tn_ok", 1), per("gg_ok", 2), per("out_ok", 1)
        stored = [sem(f"stored{u}") for u in range(2)]

        STEP = ["gather",
                "m_eT", ("f_enc", 0), ("f_enc", 1), ("m_proj", 0), ("f_enc", 2), ("m_proj", 1), ("f_enc", 3), "f_s2c",
                "m_gates", "m_qk", "f_r1", "f_r2", "m_scan", "f_top", "m_ex", ("f_bcast", 0), ("m_gb", 0),
                ("f_bcast", 1), ("f_exp", 0), ("f_exp", 1), ("m_s", 0), ("m_gb", 1), ("f_exp", 2), ("m_num", 0), ("f_exp", 3),
                ("m_s", 1), ("m_gb", 2), ("f_exp", 4), ("f_exp", 5), ("m_num", 1), ("f_exp", 6), ("m_s", 2), ("m_gb", 3),
                ("f_exp", 7), ("f_exp", 8), ("m_num", 2), ("f_exp", 9), ("m_s", 3), ("f_exp", 10), ("f_exp", 11),
                ("m_num", 3), "m_norm", ("f_exp", 12), ("f_exp", 13), ("f_exp", 14), ("f_exp", 15), "f_out", "m_hoT",
                ("f_c2s", 0), ("f_c2s", 1), "m_y", ("f_c2s", 2), ("f_c2s", 3), "f_dec", "m_xnT", "f_ln", "f_store"]

        def run_step(parts, b, u, half, mixer, ffn, ahead):
            for part in STEP:
                name, *arg = (part,) if isinstance(part, str) else part
                if name not in parts:
                    continue
                if name == "gather":
                    if ahead:
                        parts[name](b + 2, u, half + 1)
                elif name[0] == "m":
                    if mixer:
                        parts[name](b + 1, 1 - u, half + u, *arg)
                elif ffn:
                    parts[name](b, u, half, *arg)

        def run_all(eng, parts):
            run_step(parts, -1, 1, -1, True, False, False)
            run_step(parts, 0, 0, 0, True, True, True)
            with eng.Fori(0, (NB - 4) // 2) as i:
                run_step(parts, i * 2 + 1, 1, i, True, True, True)
                run_step(parts, i * 2 + 2, 0, i + 1, True, True, True)
            run_step(parts, NB - 3, 1, NB // 2 - 2, True, True, True)
            run_step(parts, NB - 2, 0, NB // 2 - 1, True, True, False)
            run_step(parts, NB - 1, 1, NB // 2 - 1, False, True, False)

        NLOADS = 27
        block = ctx.enter_context(nc.Block())

        @block.sync
        def _(sp_):
            sp_.dma_start(tok[:], A["tok"]).then_inc(tok_in, 16)
            sp_.dma_start(tokp[:], A["tokp"]).then_inc(tok_in, 16)
            loads = [(ident[:], A["ident"]), (headmask[:], A["headmask"]), (headsel[:], A["headsel"]),
                     (notstart[:], A["notstart"].broadcast_to((NH, S))), (iota8[:], A["iota8"].broadcast_to((P, E))),
                     (scale[:], A["scale"].broadcast_to((P, 1))), (projT[:], A["projT"]),
                     (wall[:], A["wall"].rearrange("(t p) n -> p t n", p=P)), (bfi[:], A["bfi"]),
                     (mixw[:], A["mixw"].broadcast_to((P, D))), (mixb[:], A["mixb"].broadcast_to((P, D))),
                     (woutT[:], A["woutT"].rearrange("(t p) n -> p t n", p=P)),
                     (encw[:], A["encw"].rearrange("(t p) n -> p t n", p=P)), (encb[:], A["encb"]),
                     (s2cw[:], A["s2cw"].rearrange("(t p) n -> p t n", p=P)), (s2cb[:], A["s2cb"]),
                     (rw1[:], A["rw1"]), (rb1[:], A["rb1"]), (rw2[:], A["rw2"]), (rb2[:], A["rb2"].broadcast_to((P, E))),
                     (we1[:], A["we1"]), (be1n[:], A["be1"]), (be1pad[:], A["be1pad"].rearrange("p (c e) -> p c e", e=E)),
                     (we2[:], A["we2"].rearrange("p (c m) -> p c m", m=M)), (be2[:], A["be2"]),
                     (c2sw[:], A["c2sw"]), (c2sb[:], A["c2sb"]), (decw[:], A["decw"].rearrange("(t p) n -> p t n", p=P)),
                     (decb[:], A["decb"].broadcast_to((P, D))), (lng[:], A["lng"].broadcast_to((P, D))),
                     (lnb[:], A["lnb"].broadcast_to((P, D)))]
            assert len(loads) == NLOADS + 4
            for dst, src in loads:
                sp_.dma_start(dst, src).then_inc(loaded, 16)

            def f_store(b, u, half):
                sp_.wait_ge(out_ok.sem, out_ok.at(b, 1))
                dst = out[bass.ds(b * S, S), :].rearrange("(c p) d -> p c d", p=P)
                sp_.dma_start(dst, gg[:]).then_inc(stored[u], 16)

            run_all(sp_, {"f_store": f_store})
            for u in range(2):
                sp_.wait_ge(stored[u], 16 * NB // 2)

        LOADED = 16 * (NLOADS + 4)
        PREPARED = 18

        @block.gpsimd
        def _(pool):
            pool.memset(mulc[:], HASH_CUR).then_inc(pconst, 1)
            pool.memset(mulp[:], HASH_PREV).then_inc(pconst, 1)
            pool.memset(halves[:], 0.5).then_inc(pconst, 1)
            pool.memset(mhalf[:], -0.5).then_inc(pconst, 1)
            pool.memset(ex[:], 0.0).then_inc(pconst, 1)
            pool.memset(mst[:], 0.0).then_inc(pconst, 1)
            pool.wait_ge(pconst, 2)
            pool.wait_ge(tok_in, 32)
            pool.tensor_tensor(mulc[:], tok[:], mulc[:], ALU.mult).then_inc(mults, 1)
            pool.tensor_tensor(mulp[:], tokp[:], mulp[:], ALU.mult).then_inc(mults, 1)
            pool.wait_ge(pconst, 4)

            def gather(b, u, half):
                pool.wait_ge(gathered[u], half * 16 * NT)
                pool.tensor_copy(idxs[:, u, :], idx[:, bass.ds(b * NT, NT)]).then_inc(idx_copied.sem, 1)
                pool.wait_ge(idx_copied.sem, idx_copied.at(b, 1))
                if not (isinstance(b, int) and b < 2):
                    pool.wait_ge(eT_t.sem, eT_t.at(b - 1, 0))
                pool.sem_inc(passed, 1)
                for c in range(NT):
                    pool.indirect_dma_start(
                        out=e[:, u, c, :], out_offset=None, in_=A["emb"],
                        in_offset=bass.IndirectOffsetOnAxis(ap=idxs[:, u, c:c + 1].bitcast(U32), axis=0),
                    ).then_inc(gathered[u], 16)

            def m_proj(b, u, half, j):
                if j == 0:
                    return
                pool.wait_ge(st1.sem, st1.at(b, 3))
                pool.wait_ge(nrm.sem, nrm.at(b, 0))
                pool.tensor_tensor(rs[:], vareps[:], mhalf[:], ALU.pow).then_inc(rs_ok.sem, 1)

            def m_qk(b, u, half):
                pool.wait_ge(rs_ok.sem, rs_ok.at(b, 1))
                pool.wait_ge(hv_ok.sem, hv_ok.at(b, 4))
                pool.wait_ge(num_t.sem, num_t.at(b, 0))
                pool.sem_inc(passed, 1)
                for c in range(NT):
                    pool.tensor_scalar(vh[:, c, :, 0:DV], hv[:, c, D:2 * D].rearrange("p (h d) -> p h d", d=DV),
                                       rs[:, c:c + 1], rs[:, c:c + 1], ALU.mult, ALU.mult)
                pool.tensor_copy(vh[:, :, :, DV], bc(rs[:, :], (P, NT, NH))).then_inc(vh_ok.sem, 1)

            def m_ex(b, u, half):
                pool.wait_ge(exs_ok.sem, exs_ok.at(b, 1))
                pool.wait_ge(vh_ok.sem, vh_ok.at(b, 1))
                pool.wait_ge(u_t.sem, u_t.at(b, 0))
                for c in range(NT - 1):
                    pool.tensor_tensor(wv[:, c], vh[:, c], bc(exs[:, c, 64:64 + NH], (P, NH, DV1)),
                                       ALU.mult).then_inc(wv_ok.sem, 1)

            def m_gb(b, u, half, c):
                pool.wait_ge(relu_ok.sem, relu_ok.at(b, c + 1))
                r = W[:, c % 2, :].rearrange("p (h t) -> p h t", t=P)
                pool.sem_inc(passed, 1)
                pool.affine_select(out=r, in_=r, compare_op=ALU.is_ge, fill=far, base=0,
                                   pattern=[[0, NH], [1, P]], channel_multiplier=-1).then_inc(masked.sem, 1)

            def m_norm(b, u, half):
                pool.wait_ge(nrm.sem, nrm.at(b, 10))
                pool.wait_ge(hn_ok.sem, hn_ok.at(b, 0))
                pool.tensor_tensor(rs2[:], vareps2[:], mhalf[:], ALU.pow).then_inc(rs2_ok.sem, 1)
                pool.wait_ge(hn_ok.sem, hn_ok.at(b, 1))
                pool.wait_ge(hoT_t.sem, hoT_t.at(b, 0))
                pool.tensor_tensor(hw[:], hm[:], bc1(mixw[:], (P, NT, D)), ALU.mult).then_inc(hw_ok.sem, 1)
                pool.wait_ge(hw_ok.sem, hw_ok.at(b, 1))
                pool.tensor_tensor(hw[:], hw[:], bc1(mixb[:], (P, NT, D)), ALU.add).then_inc(hw_ok.sem, 1)

            def m_y(b, u, half):
                pool.wait_ge(st3.sem, st3.at(b, 3))
                pool.wait_ge(xn_ok.sem, xn_ok.at(b, 0))
                pool.tensor_tensor(rs3[:], vareps3[:], mhalf[:], ALU.pow).then_inc(rs3_ok.sem, 1)

            def f_ln(b, u, half):
                pool.wait_ge(st4.sem, st4.at(b, 3))
                pool.wait_ge(tn_ok.sem, tn_ok.at(b, 0))
                pool.tensor_tensor(rs4[:], vareps4[:], mhalf[:], ALU.pow).then_inc(rs4_ok.sem, 1)
                pool.wait_ge(tn_ok.sem, tn_ok.at(b, 1))
                pool.wait_ge(stored[1 - u], (half + u) * 16)
                pool.tensor_tensor(gg[:], z[:], bc1(lng[:], (P, NT, D)), ALU.mult).then_inc(gg_ok.sem, 1)
                pool.wait_ge(gg_ok.sem, gg_ok.at(b, 1))
                pool.tensor_tensor(gg[:], gg[:], bc1(lnb[:], (P, NT, D)), ALU.add).then_inc(gg_ok.sem, 1)

            far = pool.to_reg(1e4)
            pool.wait_ge(idx_ok, 1)
            gather(0, 0, 0)
            gather(1, 1, 0)
            pool.wait_ge(loaded, LOADED)
            run_all(pool, {"gather": gather, "m_proj": m_proj, "m_qk": m_qk, "m_ex": m_ex, "m_gb": m_gb,
                           "m_norm": m_norm, "m_y": m_y, "f_ln": f_ln})

        @block.scalar
        def _(act):
            act.wait_ge(prep, 14)

            def m_eT(b, u, half):
                act.wait_ge(eT_t.sem, eT_t.at(b, 1))
                act.wait_ge(qk_t.sem, qk_t.at(b, 0))
                act.activation(eT[:], X[0][:], ACT.Copy).then_inc(eT_ok.sem, 1)

            def m_proj(b, u, half, j):
                if j == 0:
                    act.wait_ge(h2_ok.sem, h2_ok.at(b, 0))
                    act.wait_ge(vh_ok.sem, vh_ok.at(b, 0))
                for c in (2 * j, 2 * j + 1):
                    act.wait_ge(hv_t.sem, hv_t.at(b, c + 1))
                    act.activation(hv[:, c, :], X[1 + 2 * (c % 2)][:], ACT.Copy).then_inc(hv_ok.sem, 1)

            def m_gates(b, u, half):
                act.wait_ge(fiT_t.sem, fiT_t.at(b, 1))
                act.wait_ge(scan.sem, scan.at(b, 0))
                act.activation(fi8[:, 0, :], X[2][0:NH, :], ACT.Tanh, bias=bfi[:, 0:1], scale=1.0 / CAP)
                act.activation(fi8[:, 1, :], X[3][0:NH, :], ACT.Tanh, bias=bfi[:, 1:2],
                               scale=1.0 / CAP).then_inc(fi8_ok.sem, 1)

            def m_qk(b, u, half):
                act.wait_ge(qk_t.sem, qk_t.at(b, 2))
                act.wait_ge(s_t.sem, s_t.at(b, 0))
                act.activation(kT[:], X[1][:], ACT.Copy).then_inc(kT_ok.sem, 1)
                act.wait_ge(fi_ok.sem, fi_ok.at(b, 1))
                act.wait_ge(kg_ok.sem, kg_ok.at(b, 4))
                act.wait_ge(ho_ok.sem, ho_ok.at(b, 0))
                for c in range(NT):
                    ins = act.activation(sg[:, c, :], kg[:, c, 0:D], ACT.Tanh, scale=rsh[:, c:c + 1])
                ins.then_inc(sg_ok.sem, 1)

            def m_ex(b, u, half):
                act.wait_ge(scan.sem, scan.at(b, 15))
                act.activation(dc8[:], dcin[:], ACT.Exp).then_inc(dc_ok.sem, 1)
                act.wait_ge(exT_t.sem, exT_t.at(b, 1))
                act.wait_ge(wv_ok.sem, wv_ok.at(b, 0))
                act.wait_ge(nrm.sem, nrm.at(b, 0))
                act.wait_ge(gb_t.sem, gb_t.at(b, 0))
                x2 = X[2][:, :].rearrange("p (c n) -> p c n", n=P)
                act.activation(exs[:], x2[:, :, 32:104], ACT.Exp)
                act.activation(nega[:], x2[:, :, 0:NH], ACT.Copy, scale=-1.0)
                act.activation(gtm[:], X[3][:, 0:NT * NH].rearrange("p (c n) -> p c n", n=NH), ACT.Copy)
                act.activation(dcol[:], X[4][:, 0:NT], ACT.Copy).then_inc(exs_ok.sem, 1)

            def m_gb(b, u, half, c):
                act.wait_ge(gb_t.sem, gb_t.at(b, c + 1))
                act.wait_ge(exs_ok.sem, exs_ok.at(b, 1))
                act.wait_ge(num_t.sem, num_t.at(b, max(c - 1, 0)))
                for h in range(NH):
                    ins = act.activation(W[:, c % 2, h * P:(h + 1) * P], X[h // 4][:, (h % 4) * P:(h % 4 + 1) * P],
                                         ACT.Relu, bias=nega[:, c, h:h + 1])
                ins.then_inc(relu_ok.sem, 1)
                act.wait_ge(masked.sem, masked.at(b, c + 1))
                act.activation(W[:, c % 2, :], W[:, c % 2, :], ACT.Exp, scale=-1.0).then_inc(dm_ok.sem, 1)

            def m_hoT(b, u, half):
                act.wait_ge(hoT_t.sem, hoT_t.at(b, 1))
                act.wait_ge(y_t.sem, y_t.at(b, 0))
                act.activation(hoT[:, 0, :], X[0][:], ACT.Copy).then_inc(hoTa.sem, 1)

            def m_xnT(b, u, half):
                act.wait_ge(xnT_t.sem, xnT_t.at(b, 1))
                act.wait_ge(enc_t.sem, enc_t.at(b, 0))
                act.activation(xnT[:, 0, :], X[0][:], ACT.Copy).then_inc(xnTa.sem, 1)

            def f_enc(b, u, half, m):
                act.wait_ge(enc_t.sem, enc_t.at(b, m + 1))
                if m == 0:
                    act.wait_ge(dec_t.sem, dec_t.at(b, 0))
                act.activation(sp[:, m, :], Y[m % 2][:], ACT.Tanh, bias=encb[:, m:m + 1],
                               scale=0.5).then_inc(enc_ok.sem, 1)

            def f_r1(b, u, half):
                act.wait_ge(r1_t.sem, r1_t.at(b, 1))
                act.wait_ge(r2_t.sem, r2_t.at(b, 0))
                act.activation(r1T[:], Y[0][0:M, :], ACT.Tanh, bias=rb1[:]).then_inc(r1_ok.sem, 1)

            def f_top(b, u, half):
                act.wait_ge(top.sem, top.at(b, 4))
                act.activation(e2[:], dl[:], ACT.Exp).then_inc(e2_ok.sem, 1)

            def f_bcast(b, u, half, j):
                if j == 0:
                    act.wait_ge(hid_ok.sem, hid_ok.at(b, 0))
                for x in range(4 * j, 4 * j + 4):
                    act.wait_ge(gbc_t.sem, gbc_t.at(b, x + 1))
                    act.activation(gb[:, x, :], Y[x % 2][:], ACT.Copy).then_inc(gb_ok.sem, 1)

            def f_out(b, u, half):
                act.wait_ge(w2_t.sem, w2_t.at(b, NCH))
                act.wait_ge(c2s_t.sem, c2s_t.at(b, 0))
                act.activation(oT[:], Y[2][0:M, :], ACT.Copy).then_inc(oT_ok.sem, 1)

            def f_c2s(b, u, half, m):
                act.wait_ge(c2s_t.sem, c2s_t.at(b, m + 1))
                if m == 0:
                    act.wait_ge(s2c_t.sem, s2c_t.at(b, 1))
                act.activation(sp[:, m, :], Y[m % 2][:], ACT.Tanh, bias=c2sb[:, m:m + 1],
                               scale=0.5).then_inc(c2s_ok.sem, 1)

            def f_dec(b, u, half):
                for j in range(2):
                    act.wait_ge(z_ok.sem, z_ok.at(b, j + 1))
                    act.activation(z[:, 2 * j:2 * j + 2, :], z[:, 2 * j:2 * j + 2, :], ACT.Tanh,
                                   scale=0.5).then_inc(tt_ok.sem, 1)

            run_all(act, {"m_eT": m_eT, "m_proj": m_proj, "m_gates": m_gates, "m_qk": m_qk, "m_ex": m_ex, "m_gb": m_gb,
                          "m_hoT": m_hoT, "m_xnT": m_xnT, "f_enc": f_enc, "f_r1": f_r1, "f_top": f_top,
                          "f_bcast": f_bcast, "f_out": f_out, "f_c2s": f_c2s, "f_dec": f_dec})

        @block.vector
        def _(dve):
            dve.wait_ge(mults, 2)
            dve.tensor_tensor(hx[:], mulc[:], mulp[:], ALU.bitwise_xor).then_inc(hashed, 1)
            dve.wait_ge(hashed, 1)
            dve.tensor_scalar(hlo[:], hx[:], MOD, None, ALU.bitwise_and).then_inc(hashed, 1)
            dve.tensor_scalar(hhi[:], hx[:], 18, None, ALU.arith_shift_right).then_inc(hashed, 1)
            dve.wait_ge(hashed, 3)
            dve.tensor_tensor(hf[:], hlo[:], hhi[:], ALU.add).then_inc(hashed, 1)
            dve.wait_ge(hashed, 4)
            dve.tensor_scalar(hfix[:], hf[:], 0.0, float(MOD), ALU.is_lt, ALU.mult).then_inc(hashed, 1)
            dve.wait_ge(hashed, 5)
            dve.tensor_tensor(hf[:], hf[:], hfix[:], ALU.add).then_inc(hashed, 1)
            dve.wait_ge(hashed, 6)
            dve.tensor_scalar(hfix[:], hf[:], float(MOD), -float(MOD), ALU.is_ge, ALU.mult).then_inc(hashed, 1)
            dve.wait_ge(hashed, 7)
            dve.tensor_tensor(hf[:], hf[:], hfix[:], ALU.add).then_inc(hashed, 1)
            dve.wait_ge(hash_t, 1)
            dve.tensor_copy(idxf[:], X[0][:, 0:P]).then_inc(hashed, 1)
            dve.wait_ge(hashed, 9)
            dve.memset(idxf[0:1, 0:P:NT], float(MOD)).then_inc(hashed, 1)
            dve.wait_ge(hashed, 10)
            dve.tensor_copy(idx[:], idxf[:]).then_inc(idx_ok, 1)
            dve.wait_ge(loaded, LOADED)
            dve.tensor_scalar(wfold[:, CH:CV], projT[:], scale[:, 0:1], None, ALU.mult).then_inc(prep, 1)
            dve.wait_ge(prep, 1)
            dve.bn_stats(bst[:, 0, :], wfold[:, CH:CV]).then_inc(prep, 1)
            dve.wait_ge(prep, 2)
            dve.bn_aggr(mv[:, 0, :], bst[:, 0, :]).then_inc(prep, 1)
            dve.wait_ge(prep, 3)
            dve.tensor_scalar(projTc[:], wfold[:, CH:CV], mv[:, 0, 0:1], None, ALU.subtract).then_inc(prep, 1)
            dve.tensor_copy(blockmask[:], bc(headmask[:], (P, NH, DV1))).then_inc(prep, 1)
            dve.tensor_scalar(encb[:], encb[:], 0.5, None, ALU.mult).then_inc(prep, 1)
            dve.tensor_scalar(c2sb[:], c2sb[:], 0.5, None, ALU.mult).then_inc(prep, 1)
            dve.tensor_scalar(bfi[:], bfi[:], 1.0 / CAP, None, ALU.mult).then_inc(prep, 1)
            dve.tensor_scalar(be1n[:], be1n[:], -1.0, None, ALU.mult).then_inc(prep, 1)
            dve.tensor_scalar(woutT[:], woutT[:], 0.5, None, ALU.mult).then_inc(prep, 1)
            dve.tensor_scalar(s2cwh[:], s2cw[:], 0.5, None, ALU.mult).then_inc(prep, 1)
            dve.wait_ge(pprep, 1)
            dve.tensor_scalar(decw[:], decw[:], 0.5, None, ALU.mult).then_inc(prep, 1)
            dve.tensor_tensor(s2cb[:], X[1][0:M, 0:1], s2cb[:], ALU.add).then_inc(prep, 1)
            dve.tensor_tensor(decb[:], X[2][:, 0:D], decb[:], ALU.add).then_inc(prep, 1)
            dve.tensor_tensor(biasout[:], X[3][0:E, 0:M], be2[:], ALU.add).then_inc(prep, 1)
            dve.wait_ge(pprep, 2)
            dve.tensor_copy(projc[:], X[4][:, 0:2 * P].rearrange("p (t n) -> p t n", n=P)).then_inc(prep, 1)
            dve.wait_ge(pprep, 3)
            half_w = (CEND - CV) // 2
            dve.tensor_copy(wfold[:, CV:CV + half_w], Y[0][:, 0:half_w]).then_inc(prep, 1)
            dve.tensor_copy(wfold[:, CV + half_w:CEND], Y[1][:, 0:half_w]).then_inc(prep, 1)

            def m_proj(b, u, half, j):
                if j == 0:
                    dve.wait_ge(sg_ok.sem, sg_ok.at(b, 0))
                    dve.wait_ge(u_t.sem, u_t.at(b, 0))
                for c in (2 * j, 2 * j + 1):
                    dve.wait_ge(kg_t.sem, kg_t.at(b, c + 1))
                    dve.tensor_copy(kg[:, c, :], X[2 + 2 * (c % 2)][:, 0:NKG]).then_inc(kg_ok.sem, 1)
                if j == 0:
                    return
                dve.wait_ge(hv_ok.sem, hv_ok.at(b, 4))
                for c in range(NT):
                    ins = dve.bn_stats(bst[:, c, :], hv[:, c, 0:D])
                ins.then_inc(st1.sem, 1)
                dve.wait_ge(st1.sem, st1.at(b, 1))
                dve.sem_inc(passed, 1)
                for c in range(NT):
                    ins = dve.bn_aggr(mv[:, c, :], bst[:, c, :])
                ins.then_inc(st1.sem, 1)
                dve.wait_ge(st1.sem, st1.at(b, 2))
                dve.wait_ge(rs_ok.sem, rs_ok.at(b, 0))
                dve.tensor_scalar(vareps[:], mv[:, :, 1], 1e-5, None, ALU.add).then_inc(st1.sem, 1)
                dve.wait_ge(rs_ok.sem, rs_ok.at(b, 1))
                dve.wait_ge(sg_ok.sem, sg_ok.at(b, 0))
                dve.tensor_scalar(rsh[:], rs[:], 0.5, None, ALU.mult).then_inc(fi_ok.sem, 1)
                dve.wait_ge(kg_ok.sem, kg_ok.at(b, 4))
                dve.wait_ge(fiT_t.sem, fiT_t.at(b, 0))
                for k in range(2):
                    ins = dve.tensor_tensor(fi[:, k], kg[:, :, CF - CO + k * NH:CF - CO + (k + 1) * NH],
                                            bc(rs[:, :], (P, NT, NH)), ALU.mult)
                ins.then_inc(fi_ok.sem, 1)

            def m_qk(b, u, half):
                dve.wait_ge(qk_t.sem, qk_t.at(b, 1))
                dve.wait_ge(int_t.sem, int_t.at(b, 0))
                dve.tensor_copy(qT[:], X[0][:]).then_inc(qT_ok.sem, 1)
                dve.wait_ge(qT_ok.sem, qT_ok.at(b, 1))
                dve.wait_ge(s_t.sem, s_t.at(b, 0))
                for h in range(NH):
                    ins = dve.tensor_scalar(qbd[:, h, :], qT[:], headmask[:, h:h + 1], None, ALU.mult)
                ins.then_inc(qbd_ok.sem, 1)

            def m_scan(b, u, half):
                n = 0

                def step(ins):
                    nonlocal n
                    ins.then_inc(scan.sem, 1)
                    n += 1

                dve.wait_ge(fi8_ok.sem, fi8_ok.at(b, 1))
                step(dve.tensor_scalar(fc[:], fi8[:], CAP, None, ALU.mult))
                dve.wait_ge(scan.sem, scan.at(b, 1))
                step(dve.tensor_tensor_scan(Fs[:], notstart[:], fc[:, 0, :], 0.0, ALU.mult, ALU.add))
                dve.wait_ge(scan.sem, scan.at(b, 2))
                dve.wait_ge(exT_t.sem, exT_t.at(b, 0))
                step(dve.tensor_tensor(ex[0:NH, :], fc[:, 1, :], Fs[:], ALU.subtract))
                for c in range(NT):
                    dve.wait_ge(scan.sem, scan.at(b, n))
                    t = slice(c * P, (c + 1) * P)
                    step(dve.tensor_tensor_scan(G[:, t], ex[0:NH, t], ex[0:NH, t], mst[:, c:c + 1], ALU.max, ALU.max))
                    dve.wait_ge(scan.sem, scan.at(b, n))
                    last = (c + 1) * P
                    step(dve.tensor_tensor(mst[:, c + 1:c + 2], G[:, last - 1:last], Fs[:, last - 1:last], ALU.add))
                dve.wait_ge(scan.sem, scan.at(b, n))
                Gv = G[:, :].rearrange("p (c t) -> p c t", t=P)
                exv = ex[:, :].rearrange("p (c t) -> p c t", t=P)
                step(dve.tensor_tensor(exv[64:64 + NH], bc(mst[:, 0:NT], (NH, NT, P)), Gv, ALU.subtract))
                step(dve.tensor_tensor(exv[96:96 + NH], exv[0:NH], bc(Gv[:, :, P - 1], (NH, NT, P)), ALU.subtract))
                step(dve.scalar_tensor_tensor(out=ex[32:32 + NH, :], in0=G[:], scalar=-1.0, in1=Fs[:],
                                              op0=ALU.mult, op1=ALU.subtract))
                dve.wait_ge(dc_ok.sem, dc_ok.at(b, 0))
                step(dve.tensor_tensor(dcin[:], mst[:, 0:NT], Gv[:, :, P - 1], ALU.subtract))
                assert n == scan.per

            def m_s(b, u, half, c):
                dve.wait_ge(s_t.sem, s_t.at(b, c + 1))
                dve.wait_ge(dm_ok.sem, dm_ok.at(b, c + 1))
                for j in range(2):
                    w = slice(j * 512, (j + 1) * 512)
                    ins = dve.tensor_tensor(W[:, c % 2, w], X[2 + j][:], W[:, c % 2, w], ALU.mult)
                ins.then_inc(p_ok.sem, 1)

            def m_num(b, u, half, c):
                flat = "p h d -> p (h d)"
                if c > 0:
                    dve.wait_ge(int_t.sem, int_t.at(b, c))
                    dve.tensor_tensor(tmpI[:], X[2][:, 0:NH * DV1].rearrange("p (h d) -> p h d", d=DV1),
                                      bc(exs[:, c, 32:32 + NH], (P, NH, DV1)), ALU.mult).then_inc(tmpi_ok.sem, 1)
                if c < NT - 1:
                    dve.wait_ge(u_t.sem, u_t.at(b, c + 1))
                    upd = X[3][:, 0:NH * DV1].rearrange("p (h d) -> p h d", d=DV1)
                    if c == 0:
                        dve.wait_ge(int_t.sem, int_t.at(b, 0))
                        dve.tensor_tensor(cbd[:], upd, blockmask[:], ALU.mult).then_inc(cbd_ok.sem, 1)
                    else:
                        dve.tensor_tensor(tmpU[:], upd, blockmask[:], ALU.mult).then_inc(tmpu_ok.sem, 1)
                        dve.wait_ge(tmpu_ok.sem, tmpu_ok.at(b, c))
                        dve.scalar_tensor_tensor(out=cbd[:].rearrange(flat), in0=cbd[:].rearrange(flat),
                                                 scalar=dcol[:, c:c + 1], in1=tmpU[:].rearrange(flat),
                                                 op0=ALU.mult, op1=ALU.add).then_inc(cbd_ok.sem, 1)
                dve.wait_ge(num_t.sem, num_t.at(b, c + 1))
                new = X[4][:, 0:NH * DV1]
                if c == 0:
                    dve.tensor_copy(num[:, c].rearrange(flat), new).then_inc(num_ok.sem, 1)
                else:
                    dve.wait_ge(tmpi_ok.sem, tmpi_ok.at(b, c))
                    dve.tensor_tensor(num[:, c].rearrange(flat), new, tmpI[:].rearrange(flat),
                                      ALU.add).then_inc(num_ok.sem, 1)

            def m_norm(b, u, half):
                n = 0

                def step(ins):
                    nonlocal n
                    ins.then_inc(nrm.sem, 1)
                    n += 1
                    dve.wait_ge(nrm.sem, nrm.at(b, n))

                dve.wait_ge(num_ok.sem, num_ok.at(b, 4))
                rsb = bc(rs[:, :], (P, NT, NH))
                step(dve.tensor_tensor(den[:], num[:, :, :, DV], rsb, ALU.mult))
                step(dve.scalar_tensor_tensor(out=den[:], in0=den[:], scalar=-1.0, in1=den[:],
                                              op0=ALU.mult, op1=ALU.max))
                step(dve.scalar_tensor_tensor(out=den[:], in0=den[:], scalar=DQK ** -0.5, in1=exs[:, :, 0:NH],
                                              op0=ALU.mult, op1=ALU.max))
                step(dve.tensor_scalar(den[:], den[:], 1e-6, None, ALU.add))
                step(dve.reciprocal(den[:], den[:]))
                step(dve.scalar_tensor_tensor(out=den[:], in0=den[:], scalar=DQK ** -0.5, in1=rsb,
                                              op0=ALU.mult, op1=ALU.mult))
                dve.wait_ge(hw_ok.sem, hw_ok.at(b, 0))
                for c in range(NT):
                    ins = dve.tensor_tensor(hm[:, c].rearrange("p (h d) -> p h d", d=DV), num[:, c, :, 0:DV],
                                            bc(den[:, c], (P, NH, DV)), ALU.mult)
                step(ins)
                for c in range(NT):
                    ins = dve.bn_stats(bst[:, c, :], hm[:, c, :])
                step(ins)
                dve.sem_inc(passed, 1)
                for c in range(NT):
                    ins = dve.bn_aggr(mv[:, c, :], bst[:, c, :])
                step(ins)
                step(dve.tensor_scalar(vareps2[:], mv[:, :, 1], 1e-6, None, ALU.add))
                assert n == nrm.per
                dve.wait_ge(rs2_ok.sem, rs2_ok.at(b, 1))
                for c in range(NT):
                    ins = dve.tensor_scalar(hm[:, c, :], hm[:, c, :], mv[:, c, 0:1], rs2[:, c:c + 1],
                                            ALU.subtract, ALU.mult)
                ins.then_inc(hn_ok.sem, 1)

            def m_hoT(b, u, half):
                dve.wait_ge(hw_ok.sem, hw_ok.at(b, 2))
                dve.wait_ge(sg_ok.sem, sg_ok.at(b, 1))
                fl = "p c d -> p (c d)"
                dve.scalar_tensor_tensor(out=hw[:].rearrange(fl), in0=sg[:].rearrange(fl), scalar=1.0,
                                         in1=hw[:].rearrange(fl), op0=ALU.add, op1=ALU.mult).then_inc(ho_ok.sem, 1)
                dve.wait_ge(hoT_t.sem, hoT_t.at(b, 2))
                dve.wait_ge(y_t.sem, y_t.at(b, 0))
                dve.tensor_copy(hoT[:, 1, :], X[1][:]).then_inc(hoTd.sem, 1)

            def m_y(b, u, half):
                for j in range(2):
                    dve.wait_ge(y_t.sem, y_t.at(b, j + 1))
                    dve.tensor_tensor(h2[:, u, 2 * j:2 * j + 2, :], X[2 + j][:, :].rearrange("p (c d) -> p c d", d=D),
                                      hv[:, 2 * j:2 * j + 2, 0:D], ALU.add).then_inc(h2_ok.sem, 1)
                dve.wait_ge(h2_ok.sem, h2_ok.at(b, 2))
                for c in range(NT):
                    ins = dve.bn_stats(bst[:, c, :], h2[:, u, c, :])
                ins.then_inc(st3.sem, 1)
                dve.wait_ge(st3.sem, st3.at(b, 1))
                dve.sem_inc(passed, 1)
                for c in range(NT):
                    ins = dve.bn_aggr(mv[:, c, :], bst[:, c, :])
                ins.then_inc(st3.sem, 1)
                dve.wait_ge(st3.sem, st3.at(b, 2))
                dve.tensor_scalar(vareps3[:], mv[:, :, 1], 1e-5, None, ALU.add).then_inc(st3.sem, 1)
                dve.wait_ge(rs3_ok.sem, rs3_ok.at(b, 1))
                dve.wait_ge(xnT_t.sem, xnT_t.at(b, 0))
                for c in range(NT):
                    ins = dve.tensor_scalar(xn[:, c, :], h2[:, u, c, :], mv[:, c, 0:1], rs3[:, c:c + 1],
                                            ALU.subtract, ALU.mult)
                ins.then_inc(xn_ok.sem, 1)

            def m_xnT(b, u, half):
                dve.wait_ge(xnT_t.sem, xnT_t.at(b, 2))
                dve.wait_ge(enc_t.sem, enc_t.at(b, 0))
                dve.tensor_copy(xnT[:, 1, :], X[1][:]).then_inc(xnTd.sem, 1)

            def f_s2c(b, u, half):
                dve.wait_ge(s2c_t.sem, s2c_t.at(b, 1))
                dve.wait_ge(w1_t.sem, w1_t.at(b, 0))
                dve.tensor_scalar(cont[:], Y[2][0:M, :], s2cb[:, 0:1], None, ALU.add).then_inc(cont_ok.sem, 1)

            def f_top(b, u, half):
                n = 0

                def step(ins):
                    nonlocal n
                    ins.then_inc(top.sem, 1)
                    n += 1

                dve.wait_ge(r2_t.sem, r2_t.at(b, 1))
                step(dve.tensor_tensor(lg[:], Y[1][:, 0:NT * E].rearrange("p (c x) -> p c x", x=E),
                                       bc1(rb2[:], (P, NT, E)), ALU.add))
                dve.wait_ge(top.sem, top.at(b, n))
                dve.sem_inc(passed, 1)
                for c in range(NT):
                    ins = dve.max(mx8[:, c, :], lg[:, c, :])
                step(ins)
                dve.wait_ge(top.sem, top.at(b, n))
                dve.sem_inc(passed, 1)
                for c in range(NT):
                    ins = dve.max_index(ix8[:, c, :], mx8[:, c, :], lg[:, c, :])
                step(ins)
                dve.wait_ge(e2_ok.sem, e2_ok.at(b, 0))
                step(dve.tensor_tensor(dl[:], mx8[:, :, 1], mx8[:, :, 0], ALU.subtract))
                dve.wait_ge(top.sem, top.at(b, 3))
                step(dve.tensor_copy(ixf[:], ix8[:, :, 0:2]))
                dve.wait_ge(e2_ok.sem, e2_ok.at(b, 1))
                step(dve.tensor_scalar(s1[:], e2[:], 1.0, None, ALU.add))
                dve.wait_ge(top.sem, top.at(b, n))
                step(dve.reciprocal(w12[:, :, 0], s1[:]))
                dve.wait_ge(top.sem, top.at(b, n))
                step(dve.tensor_tensor(w12[:, :, 1], e2[:], w12[:, :, 0], ALU.mult))
                iot = bc1(iota8[:], (P, NT, E))
                step(dve.tensor_tensor(eq0[:], iot, bc(ixf[:, :, 0], (P, NT, E)), ALU.is_equal))
                step(dve.tensor_tensor(eq1[:], iot, bc(ixf[:, :, 1], (P, NT, E)), ALU.is_equal))
                dve.wait_ge(top.sem, top.at(b, n))
                step(dve.tensor_tensor(eq0[:], eq0[:], bc(w12[:, :, 0], (P, NT, E)), ALU.mult))
                step(dve.tensor_tensor(eq1[:], eq1[:], bc(w12[:, :, 1], (P, NT, E)), ALU.mult))
                dve.wait_ge(top.sem, top.at(b, n))
                dve.wait_ge(gbc_t.sem, gbc_t.at(b, 0))
                step(dve.tensor_tensor(g[:], eq0[:], eq1[:], ALU.add))
                assert n == top.per

            def f_bcast(b, u, half, j):
                if j == 0:
                    dve.wait_ge(gT_t.sem, gT_t.at(b, 1))
                    dve.wait_ge(o_t.sem, o_t.at(b, 0))
                    dve.tensor_copy(gT[:], Y[2][0:E, :]).then_inc(gT_ok.sem, 1)

            def f_exp(b, u, half, ch):
                dve.wait_ge(w1_t.sem, w1_t.at(b, ch + 1))
                dve.wait_ge(gb_ok.sem, gb_ok.at(b, ch // 2 + 1))
                dve.wait_ge(w2_t.sem, w2_t.at(b, max(ch - 3, 0)))
                dve.scalar_tensor_tensor(out=hid[:, ch % 4, :], in0=Y[ch % 2][:], scalar=be1n[:, ch:ch + 1],
                                         in1=gb[:, ch // 2, :], op0=ALU.max, op1=ALU.mult).then_inc(hid_ok.sem, 1)

            def f_dec(b, u, half):
                for j in range(2):
                    dve.wait_ge(dec_t.sem, dec_t.at(b, j + 1))
                    if j == 0:
                        dve.wait_ge(gg_ok.sem, gg_ok.at(b, 0))
                    dve.tensor_tensor(z[:, 2 * j:2 * j + 2, :], Y[j][:, :].rearrange("p (c d) -> p c d", d=D),
                                      bc1(decb[:], (P, 2, D)), ALU.add).then_inc(z_ok.sem, 1)

            def f_ln(b, u, half):
                dve.wait_ge(tt_ok.sem, tt_ok.at(b, 2))
                for c in range(NT):
                    ins = dve.bn_stats(bstf[:, c, :], z[:, c, :])
                ins.then_inc(st4.sem, 1)
                dve.wait_ge(st4.sem, st4.at(b, 1))
                dve.sem_inc(passed, 1)
                for c in range(NT):
                    ins = dve.bn_aggr(mvf[:, c, :], bstf[:, c, :])
                ins.then_inc(st4.sem, 1)
                dve.wait_ge(st4.sem, st4.at(b, 2))
                dve.tensor_scalar(vareps4[:], mvf[:, :, 1], 4e-5, None, ALU.add).then_inc(st4.sem, 1)
                dve.wait_ge(rs4_ok.sem, rs4_ok.at(b, 1))
                for c in range(NT):
                    ins = dve.tensor_scalar(z[:, c, :], z[:, c, :], mvf[:, c, 0:1], rs4[:, c:c + 1],
                                            ALU.subtract, ALU.mult)
                ins.then_inc(tn_ok.sem, 1)
                dve.wait_ge(gg_ok.sem, gg_ok.at(b, 2))
                dve.tensor_tensor(gg[:], gg[:], h2[:, u], ALU.add).then_inc(out_ok.sem, 1)

            run_all(dve, {"m_proj": m_proj, "m_qk": m_qk, "m_scan": m_scan, "m_s": m_s, "m_num": m_num, "m_norm": m_norm,
                          "m_hoT": m_hoT, "m_y": m_y, "m_xnT": m_xnT, "f_s2c": f_s2c, "f_top": f_top,
                          "f_bcast": f_bcast, "f_exp": f_exp, "f_dec": f_dec, "f_ln": f_ln})

        @block.tensor
        def _(pe):
            mm = pe.matmul
            pe.wait_ge(loaded, LOADED)
            pe.wait_ge(hashed, 8)
            pe.transpose(X[0][:, 0:P], hf[:], ident[:]).then_inc(hash_t, 1)
            pe.wait_ge(pconst, 6)
            for k in range(4):
                mm(X[1][0:M, 0:1], s2cw[:, k, :], halves[:, 0:1], start=k == 0, stop=k == 3)
            for k in range(4):
                mm(X[2][:, 0:D], halves[:], decw[:, k, :], start=k == 0, stop=k == 3)
            pe.wait_ge(prep, 9)
            for ch in range(NCH):
                ins = mm(X[3][0:E, 0:M], be1pad[:, ch, :], we2[:, ch, :], start=ch == 0, stop=ch == NCH - 1)
            ins.then_inc(pprep, 1)
            for t in range(2):
                ins = pe.transpose(X[4][:, t * P:(t + 1) * P], projTc[:, t * P:(t + 1) * P], ident[:])
            ins.then_inc(pprep, 1)
            pe.wait_ge(prep, 16)
            half_w = (CEND - CV) // 2
            for j in range(2):
                for t in range(2):
                    ins = mm(Y[j][:, 0:half_w], projc[:, t, :], wall[:, t, j * half_w:(j + 1) * half_w],
                             start=t == 0, stop=t == 1)
            ins.then_inc(pprep, 1)
            pe.wait_ge(prep, PREPARED)

            def m_eT(b, u, half):
                pe.wait_ge(gathered[u], (half + 1) * 16 * NT)
                pe.wait_ge(xnTa.sem, xnTa.at(b, 0))
                for c in range(NT):
                    ins = pe.transpose(X[0][:, c * P:(c + 1) * P], e[:, u, c, :], ident[:])
                ins.then_inc(eT_t.sem, 1)

            def m_proj(b, u, half, j):
                if j == 0:
                    pe.wait_ge(eT_ok.sem, eT_ok.at(b, 1))
                    pe.wait_ge(xnTd.sem, xnTd.at(b, 0))
                    pe.wait_ge(h2_ok.sem, h2_ok.at(b, 0))
                    pe.wait_ge(num_ok.sem, num_ok.at(b, 0))
                for c in (2 * j, 2 * j + 1):
                    t = eT[:, c * P:(c + 1) * P]
                    if c >= 2:
                        pe.wait_ge(hv_ok.sem, hv_ok.at(b, c - 1))
                        pe.wait_ge(kg_ok.sem, kg_ok.at(b, c - 1))
                    mm(X[1 + 2 * (c % 2)][:], t, wfold[:, CH:CO], start=True, stop=True).then_inc(hv_t.sem, 1)
                    mm(X[2 + 2 * (c % 2)][:, 0:NKG], t, wfold[:, CO:CQ], start=True, stop=True).then_inc(kg_t.sem, 1)

            def m_gates(b, u, half):
                pe.wait_ge(fi_ok.sem, fi_ok.at(b, 2))
                pe.wait_ge(kg_ok.sem, kg_ok.at(b, 3))
                pe.wait_ge(hv_ok.sem, hv_ok.at(b, 4))
                for k in range(2):
                    for c in range(NT):
                        ins = pe.transpose(X[2 + k][0:NH, c * P:(c + 1) * P], fi[:, k, c, :], ident[:])
                ins.then_inc(fiT_t.sem, 1)

            def m_qk(b, u, half):
                pe.wait_ge(hv_ok.sem, hv_ok.at(b, 3))
                mm(X[0][:], wfold[:, CQ:CEND], eT[:], start=True, stop=True).then_inc(qk_t.sem, 1)
                mm(X[1][:], wfold[:, CK:CQ], eT[:], start=True, stop=True).then_inc(qk_t.sem, 1)

            def m_ex(b, u, half):
                pe.wait_ge(scan.sem, scan.at(b, 15))
                pe.wait_ge(fi8_ok.sem, fi8_ok.at(b, 1))
                pe.wait_ge(kg_ok.sem, kg_ok.at(b, 4))
                for c in range(NT):
                    pe.transpose(X[2][:, c * P:c * P + 104], ex[0:104, c * P:(c + 1) * P], ident[0:104, 0:104])
                for c in range(NT):
                    pe.transpose(X[3][:, c * NH:(c + 1) * NH], G[:, c * P:(c + 1) * P], ident[0:NH, 0:NH])
                pe.wait_ge(dc_ok.sem, dc_ok.at(b, 1))
                mm(X[4][:, 0:NT], headsel[:], dc8[:], start=True, stop=True).then_inc(exT_t.sem, 1)

            def m_gb(b, u, half, c):
                if c == 0:
                    pe.wait_ge(exs_ok.sem, exs_ok.at(b, 1))
                    pe.wait_ge(qT_ok.sem, qT_ok.at(b, 1))
                    pe.wait_ge(kT_ok.sem, kT_ok.at(b, 1))
                else:
                    pe.wait_ge(relu_ok.sem, relu_ok.at(b, c))
                for h in range(NH):
                    ins = pe.transpose(X[h // 4][:, (h % 4) * P:(h % 4 + 1) * P],
                                       gtm[:, c, h:h + 1].broadcast_to((P, P)), ident[:])
                ins.then_inc(gb_t.sem, 1)

            def m_s(b, u, half, c):
                if c == 0:
                    pe.wait_ge(qbd_ok.sem, qbd_ok.at(b, 1))
                    pe.wait_ge(exs_ok.sem, exs_ok.at(b, 1))
                else:
                    pe.wait_ge(p_ok.sem, p_ok.at(b, c))
                    if c > 1:
                        pe.wait_ge(tmpi_ok.sem, tmpi_ok.at(b, c - 1))
                    pe.wait_ge(cbd_ok.sem, cbd_ok.at(b, c))
                for j in range(2):
                    ins = mm(X[2 + j][:], kT[:, c * P:(c + 1) * P], qbd[:, 4 * j:4 * j + 4, c * P:(c + 1) * P],
                             start=True, stop=True)
                ins.then_inc(s_t.sem, 1)

            def m_num(b, u, half, c):
                pe.wait_ge(p_ok.sem, p_ok.at(b, c + 1))
                if c > 0:
                    pe.wait_ge(cbd_ok.sem, cbd_ok.at(b, c))
                    mm(X[2][:, 0:NH * DV1], qT[:, c * P:(c + 1) * P], cbd[:].rearrange("p h d -> p (h d)"),
                       start=True, stop=True).then_inc(int_t.sem, 1)
                if c < NT - 1:
                    pe.wait_ge(wv_ok.sem, wv_ok.at(b, c + 1))
                    mm(X[3][:, 0:NH * DV1], kg[:, c, CK - CO:CQ - CO], wv[:, c].rearrange("p h d -> p (h d)"),
                       start=True, stop=True).then_inc(u_t.sem, 1)
                pe.wait_ge(vh_ok.sem, vh_ok.at(b, 1))
                pe.wait_ge(num_ok.sem, num_ok.at(b, c))
                if c == 0:
                    pe.wait_ge(exs_ok.sem, exs_ok.at(b, 1))
                for h in range(NH):
                    ins = mm(X[4][:, h * DV1:(h + 1) * DV1], W[:, c % 2, h * P:(h + 1) * P], vh[:, c, h, :],
                             start=True, stop=True)
                ins.then_inc(num_t.sem, 1)

            def m_hoT(b, u, half):
                pe.wait_ge(ho_ok.sem, ho_ok.at(b, 1))
                pe.wait_ge(relu_ok.sem, relu_ok.at(b, 4))
                for k in range(2):
                    for c in range(NT):
                        ins = pe.transpose(X[k][:, c * P:(c + 1) * P], hw[:, c, k * P:(k + 1) * P], ident[:])
                    ins.then_inc(hoT_t.sem, 1)

            def m_y(b, u, half):
                pe.wait_ge(hoTa.sem, hoTa.at(b, 1))
                pe.wait_ge(hoTd.sem, hoTd.at(b, 1))
                pe.wait_ge(tmpi_ok.sem, tmpi_ok.at(b, 3))
                pe.wait_ge(p_ok.sem, p_ok.at(b, 4))
                for j in range(2):
                    for c in range(2):
                        for k in range(2):
                            ins = mm(X[2 + j][:, c * D:(c + 1) * D], hoT[:, k, (2 * j + c) * P:(2 * j + c + 1) * P],
                                     woutT[:, k, :], start=k == 0, stop=k == 1)
                    ins.then_inc(y_t.sem, 1)

            def m_xnT(b, u, half):
                pe.wait_ge(xn_ok.sem, xn_ok.at(b, 1))
                pe.wait_ge(hoTa.sem, hoTa.at(b, 1))
                pe.wait_ge(hoTd.sem, hoTd.at(b, 1))
                for k in range(2):
                    for c in range(NT):
                        ins = pe.transpose(X[k][:, c * P:(c + 1) * P], xn[:, c, k * P:(k + 1) * P], ident[:])
                    ins.then_inc(xnT_t.sem, 1)

            def f_enc(b, u, half, m):
                if m == 0:
                    pe.wait_ge(xnTa.sem, xnTa.at(b, 1))
                    pe.wait_ge(xnTd.sem, xnTd.at(b, 1))
                    pe.wait_ge(z_ok.sem, z_ok.at(b, 0))
                if m >= 2:
                    pe.wait_ge(enc_ok.sem, enc_ok.at(b, m - 1))
                for k in range(2):
                    ins = mm(Y[m % 2][:], encw[:, k, m * P:(m + 1) * P], xnT[:, k, :], start=k == 0, stop=k == 1)
                ins.then_inc(enc_t.sem, 1)

            def f_s2c(b, u, half):
                pe.wait_ge(enc_ok.sem, enc_ok.at(b, 4))
                pe.wait_ge(oT_ok.sem, oT_ok.at(b, 0))
                for k in range(4):
                    ins = mm(Y[2][0:M, :], s2cwh[:, k, :], sp[:, k, :], start=k == 0, stop=k == 3)
                ins.then_inc(s2c_t.sem, 1)

            def f_r1(b, u, half):
                pe.wait_ge(cont_ok.sem, cont_ok.at(b, 1))
                pe.sem_inc(passed, 1)
                mm(Y[0][0:M, :], rw1[:], cont[:], start=True, stop=True).then_inc(r1_t.sem, 1)

            def f_r2(b, u, half):
                pe.wait_ge(r1_ok.sem, r1_ok.at(b, 1))
                for c in range(NT):
                    ins = mm(Y[1][:, c * E:(c + 1) * E], r1T[:, c * P:(c + 1) * P], rw2[:], start=True, stop=True)
                ins.then_inc(r2_t.sem, 1)

            def f_bcast(b, u, half, j):
                if j == 0:
                    pe.wait_ge(cont_ok.sem, cont_ok.at(b, 1))
                    pe.wait_ge(top.sem, top.at(b, 13))
                    for c in range(NT):
                        ins = pe.transpose(Y[2][0:E, c * P:(c + 1) * P], g[:, c, :], ident[:])
                    ins.then_inc(gT_t.sem, 1)
                for x in range(4 * j, 4 * j + 4):
                    if x >= 2:
                        pe.wait_ge(gb_ok.sem, gb_ok.at(b, x - 1))
                    for c in range(NT):
                        ins = pe.transpose(Y[x % 2][:, c * P:(c + 1) * P], g[:, c, x:x + 1].broadcast_to((P, P)), ident[:])
                    ins.then_inc(gbc_t.sem, 1)

            def second(b, ch):
                pe.wait_ge(hid_ok.sem, hid_ok.at(b, ch + 1))
                mm(Y[2][0:M, :], we2[:, ch, :], hid[:, ch % 4, :], start=False, stop=ch == NCH - 1).then_inc(w2_t.sem, 1)

            def f_exp(b, u, half, ch):
                if ch < 2:
                    pe.wait_ge(gb_ok.sem, gb_ok.at(b, 7 + ch))
                else:
                    pe.wait_ge(hid_ok.sem, hid_ok.at(b, ch - 1))
                mm(Y[ch % 2][:], we1[:, ch * P:(ch + 1) * P], cont[:], start=True, stop=True).then_inc(w1_t.sem, 1)
                if ch == 0:
                    pe.wait_ge(gT_ok.sem, gT_ok.at(b, 1))
                    mm(Y[2][0:M, :], biasout[:], gT[:], start=True, stop=False).then_inc(o_t.sem, 1)
                else:
                    second(b, ch - 1)

            def f_out(b, u, half):
                second(b, NCH - 1)

            def f_c2s(b, u, half, m):
                if m == 0:
                    pe.wait_ge(oT_ok.sem, oT_ok.at(b, 1))
                if m >= 2:
                    pe.wait_ge(c2s_ok.sem, c2s_ok.at(b, m - 1))
                mm(Y[m % 2][:], c2sw[:, m * P:(m + 1) * P], oT[:], start=True, stop=True).then_inc(c2s_t.sem, 1)

            def f_dec(b, u, half):
                pe.wait_ge(c2s_ok.sem, c2s_ok.at(b, 4))
                for j in range(2):
                    for c in range(2):
                        for k in range(4):
                            t = (2 * j + c) * P
                            ins = mm(Y[j][:, c * D:(c + 1) * D], sp[:, k, t:t + P], decw[:, k, :], start=k == 0, stop=k == 3)
                    ins.then_inc(dec_t.sem, 1)

            run_all(pe, {"m_eT": m_eT, "m_proj": m_proj, "m_gates": m_gates, "m_qk": m_qk, "m_ex": m_ex, "m_gb": m_gb,
                         "m_s": m_s, "m_num": m_num, "m_hoT": m_hoT, "m_y": m_y, "m_xnT": m_xnT, "f_enc": f_enc,
                         "f_s2c": f_s2c, "f_r1": f_r1, "f_r2": f_r2, "f_bcast": f_bcast, "f_exp": f_exp, "f_out": f_out,
                         "f_c2s": f_c2s, "f_dec": f_dec})


def kernel(**inputs):
    import numpy as np
    import concourse.bacc as bacc
    from concourse.bass_utils import run_bass_kernel_spmd

    a = {k: np.ascontiguousarray(v) for k, v in inputs.items()}
    f = np.float32

    def attn(n):
        return a["L0_attn_" + n]

    def ffn(n):
        return a["L0_ffn_" + n]

    x = a["x"].reshape(-1)
    be1 = ffn("be1").reshape(NCH, P)
    be1pad = np.zeros((P, NCH, E), f)
    for ch in range(NCH):
        be1pad[:, ch, ch // (HE // P)] = be1[ch]
    heads = np.repeat(np.eye(NH, dtype=f), DQK, axis=1)
    notstart = np.ones((1, S), f)
    notstart[:, ::P] = 0
    arrays = {
        "tok": x.reshape(TILES, P), "tokp": np.roll(x, 1).reshape(TILES, P),
        "emb": a["L0_tok_emb_weight"], "projT": a["L0_tok_proj_weight"].T, "scale": a["L0_tok_scale"].reshape(1, 1),
        "ident": np.eye(P, dtype=f), "headmask": heads.T, "headsel": heads, "notstart": notstart,
        "iota8": np.arange(E, dtype=f)[None],
        "wall": np.concatenate([attn(n) for n in ("Wv", "Wog", "Wf", "Wi", "Wk", "Wq")], axis=0).T,
        "bfi": np.stack([attn("bf"), attn("bi")], axis=1), "mixw": attn("ln_w")[None], "mixb": attn("ln_b")[None],
        "woutT": attn("Wout").T, "encw": ffn("enc_W"), "encb": ffn("enc_b").reshape(4, P).T,
        "s2cw": ffn("s2c_W"), "s2cb": ffn("s2c_b")[:, None], "rw1": ffn("rW1"), "rb1": ffn("rb1")[:, None],
        "rw2": ffn("rW2"), "rb2": ffn("rb2")[None], "we1": ffn("We1").transpose(1, 0, 2).reshape(M, E * HE),
        "be1": be1.T, "be1pad": be1pad.reshape(P, NCH * E),
        "we2": ffn("We2").reshape(NCH, P, M).transpose(1, 0, 2).reshape(P, NCH * M), "be2": ffn("be2"),
        "c2sw": ffn("c2s_W"), "c2sb": ffn("c2s_b").reshape(4, P).T, "decw": ffn("dec_W"), "decb": ffn("dec_b")[None],
        "lng": ffn("ln_g")[None], "lnb": ffn("ln_b")[None],
    }
    nc = bacc.Bacc("TRN2", target_bir_lowering=False, num_devices=1)
    feed, aps = {}, {}
    for name, arr in arrays.items():
        arr = np.ascontiguousarray(arr)
        feed["in_" + name] = arr
        aps[name] = nc.dram_tensor("in_" + name, arr.shape, mybir.dt.from_np(arr.dtype), kind="ExternalInput").ap()
    out = nc.dram_tensor("out", (NB * S, D), F32, kind="ExternalOutput").ap()
    tower(nc, aps, out)
    r = run_bass_kernel_spmd(nc, [feed], core_ids=[0])
    return r.results[0]["out"].reshape(NB, S, D)
```

```python
from contextlib import ExitStack

import concourse.bass as bass
from concourse import mybir

F32 = mybir.dt.float32
F32R = mybir.dt.float32r
I32 = mybir.dt.int32
U32 = mybir.dt.uint32
ACT = mybir.ActivationFunctionType
ALU = mybir.AluOpType

P = 128
NB, S = 32, 512
NT = S // P
TILES = NB * NT
BUCKETS, EDIM, D = 262144, 128, 256
NH, DQK, DV = 8, 16, 32
DV1 = DV + 1
H, M, E, HE = 512, 64, 8, 256
NCH = E * HE // P
CAP = 15.0
HASH_CUR, HASH_PREV, MOD = 36313, 27191, BUCKETS - 1
CH, CV, CO, CF, CI, CK, CQ, CEND = 0, 256, 512, 768, 776, 784, 912, 1040
NKG = CQ - CO


class PerBatch:

    def __init__(self, sem, per):
        self.sem, self.per = sem, per

    def at(self, b, n):
        return b * self.per + n


def bc(ap, shape):
    return ap.unsqueeze(len(ap.shape)).broadcast_to(shape)


def bc1(ap, shape):
    return ap.unsqueeze(1).broadcast_to(shape)


def tower(nc, A, out):
    with ExitStack() as ctx:
        def sb(name, shape, dt=F32):
            return ctx.enter_context(nc.sbuf_tensor(name, shape, dt))

        def sem(name):
            return ctx.enter_context(nc.semaphore(name))

        def per(name, n):
            return PerBatch(sem(name), n)

        gb = sb("gb", [P, E, S])
        W = sb("W", [P, 2, NH * P])
        wall = gb[:, 0:4, :].rearrange("p a b -> p (a b)")[:, 0:2 * (CEND - CV)].rearrange("p (t n) -> p t n", t=2)
        we1raw = W[:, :, :].rearrange("p a b -> p (a b)")
        rw1raw = gb[:, 6, 0:M]
        projTc = gb[:, 4, 0:D]
        projT = gb[:, 7, 0:D]
        s2cw = gb[:, 7, D:2 * D].rearrange("p (k m) -> p k m", m=M)
        projc = gb[:, 5, 0:2 * P].rearrange("p (t n) -> p t n", t=2)
        qbd = sb("qbd", [P, NH, S])
        hash_tiles = [qbd[:, n // 4, (n % 4) * P:(n % 4 + 1) * P] for n in range(10)]
        tok, tokp, mulc, mulp, hx, hlo, hhi = (t.bitcast(I32) for t in hash_tiles[:7])
        hf, hfix, idxf = hash_tiles[7:]
        ident = sb("ident", [P, P])
        headmask = sb("headmask", [P, NH])
        headsel = sb("headsel", [NH, P])
        blockmask = sb("blockmask", [P, NH, DV1])
        notstart = sb("notstart", [NH, S])
        iota8 = sb("iota8", [P, E])
        halves = sb("halves", [P, P])
        mhalf = sb("mhalf", [P, NT])
        scale = sb("scale", [P, 1])
        wfold = sb("wfold", [P, CEND])
        bfi = sb("bfi", [NH, 2])
        mixw = sb("mixw", [P, 2])
        mixb = sb("mixb", [P, 2])
        woutT = sb("woutT", [P, 2, D])
        encw = sb("encw", [P, 2, H])
        encb = sb("encb", [P, 4])
        s2cwh = sb("s2cwh", [P, 4, 2 * M])
        s2cb = sb("s2cb", [2 * M, 1])
        rw1 = sb("rw1", [2 * M, M], F32R)
        rb1 = sb("rb1", [M, 1])
        rw2 = sb("rw2", [M, E])
        rb2 = sb("rb2", [P, E])
        we1 = sb("we1", [2 * M, E * HE], F32R)
        be1n = sb("be1n", [P, NCH])
        be1pad = sb("be1pad", [P, NCH, E])
        we2 = sb("we2", [P, NCH, M])
        be2 = sb("be2", [E, M])
        biasout = sb("biasout", [E, M])
        c2sw = sb("c2sw", [2 * M, H])
        c2sb = sb("c2sb", [P, 4])
        decw = sb("decw", [P, 4, D])
        decb = sb("decb", [P, D])
        lng = sb("lng", [P, D])
        lnb = sb("lnb", [P, D])
        idx = sb("idx", [P, P], I32)
        idxs = sb("idxs", [P, 2, NT], I32)
        e = sb("e", [P, 2, NT, EDIM])
        eT = sb("eT", [P, S])
        hv = sb("hv", [P, 2, NT, 2 * D])
        kg = sb("kg", [P, NT, NKG])
        bst, bst2, bst3 = (sb(f"bst{n}", [P, NT, 6]) for n in range(3))
        mv, mv2, mv3 = (sb(f"mv{n}", [P, NT, 2]) for n in range(3))
        vareps = sb("vareps", [P, NT])
        rs = sb("rs", [P, 2, NT])
        rsh = sb("rsh", [P, NT])
        fi = sb("fi", [P, 2, NT, NH])
        fi8 = sb("fi8", [NH, 2, S])
        Fs = sb("Fs", [NH, S])
        ex = sb("ex", [P, S])
        G = sb("G", [NH, S])
        mst = sb("mst", [NH, NT + 1])
        dcin = sb("dcin", [NH, NT])
        dc8 = sb("dc8", [NH, NT])
        exs = sb("exs", [P, NT, 72])
        nega = sb("nega", [P, NT, NH])
        gtm = sb("gtm", [P, NT, NH])
        dcol = sb("dcol", [P, NT])
        qT = sb("qT", [P, S])
        kT = sb("kT", [P, S])
        vh = sb("vh", [P, NT, NH, DV1])
        wv = sb("wv", [P, NT - 1, NH, DV1])
        sg = sb("sg", [P, NT, D])
        sgT = sb("sgT", [P, 2, S])
        num = sb("num", [P, NT, NH, DV1])
        tmpI = sb("tmpI", [P, NH, DV1])
        tmpU = sb("tmpU", [P, NH, DV1])
        cbd = sb("cbd", [P, NH, DV1])
        den = sb("den", [P, NT, NH])
        hm = sb("hm", [P, NT, D])
        hoT = sb("hoT", [P, 2, S])
        vareps2 = sb("vareps2", [P, NT])
        rs2 = sb("rs2", [P, NT])
        h2 = sb("h2", [P, 2, NT, D])
        vareps3 = sb("vareps3", [P, NT])
        rs3 = sb("rs3", [P, NT])
        xn = sb("xn", [P, NT, D])
        xnT = sb("xnT", [P, 2, S])
        bstf = sb("bstf", [P, NT, 6])
        mvf = sb("mvf", [P, NT, 2])
        sp = sb("sp", [P, 4, S])
        conth = sb("conth", [2 * M, S], F32R)
        contl = sb("contl", [2 * M, S], F32R)
        r1T = sb("r1T", [M, S])
        lg = sb("lg", [P, NT, E])
        mx8 = sb("mx8", [P, NT, 8])
        ix8 = sb("ix8", [P, NT, 8], U32)
        ixf = sb("ixf", [P, NT, 2])
        dl = sb("dl", [P, NT])
        e2 = sb("e2", [P, NT])
        s1 = sb("s1", [P, NT])
        w12 = sb("w12", [P, NT, 2])
        eq0 = sb("eq0", [P, NT, E])
        eq1 = sb("eq1", [P, NT, E])
        g = sb("g", [P, NT, E])
        gT = sb("gT", [E, S])
        hid = sb("hid", [P, 4, S])
        oT = sb("oT", [2 * M, S])
        z = sb("z", [P, NT, D])
        vareps4 = sb("vareps4", [P, NT])
        rs4 = sb("rs4", [P, NT])
        gg = sb("gg", [P, NT, D])

        X = [ctx.enter_context(nc.psum_tensor(f"X{i}", [P, 512], F32)) for i in range(5)]
        Y = [ctx.enter_context(nc.psum_tensor(f"Y{i}", [P, 512], F32)) for i in range(3)]

        passed = sem("passed")
        loaded = sem("loaded")
        tok_in = sem("tok_in")
        pconst = sem("pconst")
        mults = sem("mults")
        hashed = sem("hashed")
        hash_t = sem("hash_t")
        idx_ok = sem("idx_ok")
        prep = sem("prep")
        pprep = sem("pprep")
        gathered = [sem(f"gathered{u}") for u in range(2)]
        idx_copied = per("idx_copied", 1)
        eT_t, eT_ok = per("eT_t", 1), per("eT_ok", 1)
        hv_t, kg_t, hv_ok, kg_ok = per("hv_t", 4), per("kg_t", 4), per("hv_ok", 4), per("kg_ok", 4)
        st1, rs_ok, fi_ok, fiT_t, fi8_ok = per("st1", 3), per("rs_ok", 1), per("fi_ok", 2), per("fiT_t", 1), per("fi8_ok", 1)
        scan, dc_ok, exT_t, exs_ok = per("scan", 15), per("dc_ok", 1), per("exT_t", 1), per("exs_ok", 1)
        qk_t, kT_ok, qT_ok, qbd_ok = per("qk_t", 2), per("kT_ok", 1), per("qT_ok", 1), per("qbd_ok", 4)
        vh_ok, wv_ok, sg_ok, sgT_t, sgT_ok = per("vh_ok", 1), per("wv_ok", 3), per("sg_ok", 1), per("sgT_t", 1), per("sgT_ok", 1)
        gb_t, relu_ok, masked, dm_ok = per("gb_t", 4), per("relu_ok", 4), per("masked", 4), per("dm_ok", 4)
        s_t, p_ok, num_t, int_t, u_t = per("s_t", 4), per("p_ok", 4), per("num_t", 4), per("int_t", 3), per("u_t", 3)
        num_ok, tmpi_ok, tmpu_ok, cbd_ok = per("num_ok", 4), per("tmpi_ok", 3), per("tmpu_ok", 2), per("cbd_ok", 3)
        nrm, rs2_ok, hn_ok, ho_ok = per("nrm", 10), per("rs2_ok", 1), per("hn_ok", 1), per("ho_ok", 2)
        hoT_t, hwT_ok = per("hoT_t", 2), per("hwT_ok", 2)
        y_t, h2_ok, st3, rs3_ok, xn_ok = per("y_t", 2), per("h2_ok", 2), per("st3", 3), per("rs3_ok", 1), per("xn_ok", 1)
        xnT_t, xnTa, xnTd = per("xnT_t", 2), per("xnTa", 1), per("xnTd", 1)
        enc_t, enc_ok, s2c_t, cont_ok = per("enc_t", 4), per("enc_ok", 4), per("s2c_t", 1), per("cont_ok", 2)
        r1_t, r1_ok, r2_t, top, e2_ok = per("r1_t", 1), per("r1_ok", 1), per("r2_t", 1), per("top", 13), per("e2_ok", 1)
        gT_t, gT_ok, gbc_t, gb_ok = per("gT_t", 1), per("gT_ok", 1), per("gbc_t", 8), per("gb_ok", 8)
        w1_t, hid_ok, w2_t, o_t, oT_ok = per("w1_t", 16), per("hid_ok", 16), per("w2_t", 16), per("o_t", 1), per("oT_ok", 1)
        c2s_t, c2s_ok, dec_t, z_ok, tt_ok = per("c2s_t", 4), per("c2s_ok", 4), per("dec_t", 2), per("z_ok", 2), per("tt_ok", 2)
        st4, rs4_ok, tn_ok, gg_ok, out_ok = per("st4", 3), per("rs4_ok", 1), per("tn_ok", 1), per("gg_ok", 2), per("out_ok", 1)
        stored = [sem(f"stored{u}") for u in range(2)]

        def order(names):
            return [(n.rstrip("0123456789"), *(int(d) for d in (n[len(n.rstrip("0123456789")):],) if d)) for n in names.split()]

        ORDER = {
            "pe": order(
                "c_gb0 f_enc0 f_enc1 c_gb1 c_s0 f_enc2 f_enc3 c_int0 c_num0 c_gb2 c_s1 f_s2c c_int1 c_gb3 c_num1 "
                "c_s2 f_route c_int2 f_logit h_eT c_s3 c_num2 f_bcast0 f_gT c_int3 c_num3 h_proj0 f_bcast1 f_bcast2 "
                "f_bcast3 h_proj1 f_bcast4 f_bcast5 f_bcast6 f_bcast7 f_exp0 f_exp1 h_proj2 f_exp2 f_exp3 f_sec0 "
                "h_proj3 f_exp4 f_exp5 f_sec1 f_exp6 f_exp7 f_sec2 f_exp8 f_exp9 f_sec3 t_hoT h_q f_exp10 f_exp11 "
                "h_gates f_sec4 f_exp12 f_exp13 h_k f_sec5 t_y0 h_sg f_exp14 f_exp15 t_y1 f_sec6 f_sec7 f_c2s0 "
                "f_c2s1 f_c2s2 f_c2s3 f_dec0 f_dec1 h_ex t_xnT"),
            "act": order(
                "c_gb0 f_enc0 f_enc1 c_exp0 c_gb1 f_enc2 f_enc3 c_exp1 c_gb2 c_exp2 c_gb3 f_route f_top c_exp3 "
                "f_bcast0 h_eT f_bcast1 f_bcast2 f_bcast3 f_bcast4 f_bcast5 f_bcast6 f_bcast7 h_proj0 h_proj1 "
                "h_proj2 h_proj3 t_hoT0 t_hoT1 h_og h_gates h_k h_sg f_out f_c2s0 f_c2s1 f_c2s2 f_c2s3 h_dc h_ex "
                "f_dec0 t_xnT f_dec1"),
            "dve": order(
                "l_st c_p0 c_int0 c_num0 l_norm c_p1 c_int1 f_s2c c_p2 c_num1 c_int2 f_top f_gate c_p3 c_num2 "
                "c_int3 c_num3 f_gT t_den h_proj0 t_hm h_proj1 f_exp0 f_exp1 f_exp2 f_exp3 h_proj2 t_norm f_exp4 "
                "f_exp5 h_proj3 f_exp6 f_exp7 h_st f_exp8 f_exp9 h_fi f_exp10 h_q f_exp11 t_hoT0 t_hoT1 f_exp12 "
                "f_exp13 h_F f_exp14 h_G0 f_exp15 h_G1 l_sum t_y0 h_G2 t_y1 h_G3 t_st h_ex t_xn f_dec0 f_dec1 "
                "h_qbd0 t_xnT h_qbd1 h_qbd2 h_qbd3"),
            "pool": order(
                "c_mask0 l_st c_mask1 c_mask2 c_mask3 g_rows t_norm l_gain h_st t_st h_vh h_wv"),
            "sync": order(
                "l_store"),
        }

        def run_step(name, parts, b, u, half):
            stages = {"l": (b - 1, 1 - u, half - 1 + u), "f": (b, u, half), "c": (b + 1, 1 - u, half + u),
                      "t": (b + 1, 1 - u, half + u), "h": (b + 2, u, half + 1), "g": (b + 3, 1 - u, half + 1 + u)}
            for part, *arg in ORDER[name]:
                at = stages[part[0]]
                if not (isinstance(at[0], int) and not 0 <= at[0] < NB):
                    parts[part](*at, *arg)

        def run_all(name, eng, parts):
            for b in range(-3, 3):
                run_step(name, parts, b, b % 2, b // 2)
            with eng.Fori(0, (NB - 6) // 2) as i:
                run_step(name, parts, i * 2 + 3, 1, i + 1)
                run_step(name, parts, i * 2 + 4, 0, i + 2)
            for b in range(NB - 3, NB + 1):
                run_step(name, parts, b, b % 2, b // 2)

        NLOADS = 31
        block = ctx.enter_context(nc.Block())

        @block.sync
        def _(sp_):
            sp_.dma_start(tok[:], A["tok"]).then_inc(tok_in, 16)
            sp_.dma_start(tokp[:], A["tokp"]).then_inc(tok_in, 16)
            loads = [(ident[:], A["ident"]), (headmask[:], A["headmask"]), (headsel[:], A["headsel"]),
                     (notstart[:], A["notstart"].broadcast_to((NH, S))), (iota8[:], A["iota8"].broadcast_to((P, E))),
                     (scale[:], A["scale"].broadcast_to((P, 1))), (projT[:], A["projT"]),
                     (wall[:], A["wall"].rearrange("(t p) n -> p t n", p=P)), (bfi[:], A["bfi"]),
                     (mixw[:], A["mixw"]), (mixb[:], A["mixb"]),
                     (woutT[:], A["woutT"].rearrange("(t p) n -> p t n", p=P)),
                     (encw[:], A["encw"].rearrange("(t p) n -> p t n", p=P)), (encb[:], A["encb"]),
                     (s2cw[:], A["s2cw"].rearrange("(t p) n -> p t n", p=P)), (s2cb[0:M], A["s2cb"]), (s2cb[M:2 * M], A["s2cb"]),
                     (rw1raw[0:M], A["rw1"]), (rw1raw[M:2 * M], A["rw1"]), (rb1[:], A["rb1"]), (rw2[:], A["rw2"]), (rb2[:], A["rb2"].broadcast_to((P, E))),
                     (we1raw[0:M], A["we1"]), (we1raw[M:2 * M], A["we1"]), (be1n[:], A["be1"]), (be1pad[:], A["be1pad"].rearrange("p (c e) -> p c e", e=E)),
                     (we2[:], A["we2"].rearrange("p (c m) -> p c m", m=M)), (be2[:], A["be2"]),
                     (c2sw[0:M], A["c2sw"]), (c2sw[M:2 * M], A["c2sw"]), (c2sb[:], A["c2sb"]), (decw[:], A["decw"].rearrange("(t p) n -> p t n", p=P)),
                     (decb[:], A["decb"].broadcast_to((P, D))), (lng[:], A["lng"].broadcast_to((P, D))),
                     (lnb[:], A["lnb"].broadcast_to((P, D)))]
            assert len(loads) == NLOADS + 4
            for dst, src in loads:
                sp_.dma_start(dst, src).then_inc(loaded, 16)

            def l_store(b, u, half):
                sp_.wait_ge(out_ok.sem, out_ok.at(b, 1))
                dst = out[bass.ds(b * S, S), :].rearrange("(c p) d -> p c d", p=P)
                sp_.dma_start(dst, gg[:]).then_inc(stored[u], 16)

            run_all("sync", sp_, {"l_store": l_store})
            for u in range(2):
                sp_.wait_ge(stored[u], 16 * NB // 2)

        LOADED = 16 * (NLOADS + 4)
        PREPARED = 22

        @block.gpsimd
        def _(pool):
            pool.memset(mulc[:], HASH_CUR).then_inc(pconst, 1)
            pool.memset(mulp[:], HASH_PREV).then_inc(pconst, 1)
            pool.memset(halves[:], 0.5).then_inc(pconst, 1)
            pool.memset(mhalf[:], -0.5).then_inc(pconst, 1)
            pool.memset(ex[:], 0.0).then_inc(pconst, 1)
            pool.memset(mst[:], 0.0).then_inc(pconst, 1)
            pool.wait_ge(pconst, 2)
            pool.wait_ge(tok_in, 32)
            pool.tensor_tensor(mulc[:], tok[:], mulc[:], ALU.mult).then_inc(mults, 1)
            pool.tensor_tensor(mulp[:], tokp[:], mulp[:], ALU.mult).then_inc(mults, 1)
            pool.wait_ge(pconst, 4)

            def g_rows(b, u, half):
                pool.wait_ge(gathered[u], half * 16 * NT)
                pool.tensor_copy(idxs[:, u, :], idx[:, bass.ds(b * NT, NT)]).then_inc(idx_copied.sem, 1)
                pool.wait_ge(idx_copied.sem, idx_copied.at(b, 1))
                if not (isinstance(b, int) and b < 2):
                    pool.wait_ge(eT_t.sem, eT_t.at(b - 1, 0))
                pool.sem_inc(passed, 1)
                for c in range(NT):
                    pool.indirect_dma_start(
                        out=e[:, u, c, :], out_offset=None, in_=A["emb"],
                        in_offset=bass.IndirectOffsetOnAxis(ap=idxs[:, u, c:c + 1].bitcast(U32), axis=0),
                    ).then_inc(gathered[u], 16)

            def h_st(b, u, half):
                pool.wait_ge(st1.sem, st1.at(b, 3))
                if not (isinstance(b, int) and b < 2):
                    pool.wait_ge(nrm.sem, nrm.at(b - 1, 0))
                pool.tensor_tensor(rs[:, u], vareps[:], mhalf[:], ALU.pow).then_inc(rs_ok.sem, 1)

            def h_vh(b, u, half):
                pool.wait_ge(rs_ok.sem, rs_ok.at(b, 1))
                pool.wait_ge(hv_ok.sem, hv_ok.at(b, 4))
                pool.wait_ge(num_t.sem, num_t.at(b, 0))
                pool.sem_inc(passed, 1)
                for c in range(NT):
                    pool.tensor_scalar(vh[:, c, :, 0:DV], hv[:, u, c, D:2 * D].rearrange("p (h d) -> p h d", d=DV),
                                       rs[:, u, c:c + 1], rs[:, u, c:c + 1], ALU.mult, ALU.mult)
                pool.tensor_copy(vh[:, :, :, DV], bc(rs[:, u, :], (P, NT, NH))).then_inc(vh_ok.sem, 1)

            def h_wv(b, u, half):
                pool.wait_ge(exs_ok.sem, exs_ok.at(b, 1))
                pool.wait_ge(vh_ok.sem, vh_ok.at(b, 1))
                pool.wait_ge(u_t.sem, u_t.at(b, 0))
                for c in range(NT - 1):
                    pool.tensor_tensor(wv[:, c], vh[:, c], bc(exs[:, c, 64:64 + NH], (P, NH, DV1)),
                                       ALU.mult).then_inc(wv_ok.sem, 1)

            def c_mask(b, u, half, c):
                pool.wait_ge(relu_ok.sem, relu_ok.at(b, c + 1))
                r = W[:, c % 2, :].rearrange("p (h t) -> p h t", t=P)
                pool.sem_inc(passed, 1)
                pool.affine_select(out=r, in_=r, compare_op=ALU.is_ge, fill=far, base=0,
                                   pattern=[[0, NH], [1, P]], channel_multiplier=-1).then_inc(masked.sem, 1)

            def t_norm(b, u, half):
                pool.wait_ge(nrm.sem, nrm.at(b, 10))
                pool.wait_ge(hn_ok.sem, hn_ok.at(b, 0))
                pool.tensor_tensor(rs2[:], vareps2[:], mhalf[:], ALU.pow).then_inc(rs2_ok.sem, 1)

            def t_st(b, u, half):
                pool.wait_ge(st3.sem, st3.at(b, 3))
                pool.wait_ge(xn_ok.sem, xn_ok.at(b, 0))
                pool.tensor_tensor(rs3[:], vareps3[:], mhalf[:], ALU.pow).then_inc(rs3_ok.sem, 1)

            def l_st(b, u, half):
                pool.wait_ge(st4.sem, st4.at(b, 3))
                pool.wait_ge(tn_ok.sem, tn_ok.at(b, 0))
                pool.tensor_tensor(rs4[:], vareps4[:], mhalf[:], ALU.pow).then_inc(rs4_ok.sem, 1)

            def l_gain(b, u, half):
                pool.wait_ge(tn_ok.sem, tn_ok.at(b, 1))
                pool.wait_ge(stored[1 - u], (half + u) * 16)
                pool.tensor_tensor(gg[:], z[:], bc1(lng[:], (P, NT, D)), ALU.mult).then_inc(gg_ok.sem, 1)
                pool.wait_ge(gg_ok.sem, gg_ok.at(b, 1))
                pool.tensor_tensor(gg[:], gg[:], bc1(lnb[:], (P, NT, D)), ALU.add).then_inc(gg_ok.sem, 1)

            far = pool.to_reg(1e4)
            pool.wait_ge(idx_ok, 1)
            run_all("pool", pool, {"g_rows": g_rows, "h_st": h_st, "h_vh": h_vh, "h_wv": h_wv, "c_mask": c_mask,
                                   "t_norm": t_norm, "t_st": t_st, "l_st": l_st, "l_gain": l_gain})

        @block.scalar
        def _(act):
            act.wait_ge(prep, PREPARED)

            def h_eT(b, u, half):
                act.wait_ge(eT_t.sem, eT_t.at(b, 1))
                act.wait_ge(qk_t.sem, qk_t.at(b, 0))
                act.activation(eT[:], X[0][:], ACT.Copy).then_inc(eT_ok.sem, 1)

            def h_proj(b, u, half, c):
                if c == 0:
                    if not (isinstance(b, int) and b < 2):
                        act.wait_ge(h2_ok.sem, h2_ok.at(b - 1, 0))
                    act.wait_ge(vh_ok.sem, vh_ok.at(b, 0))
                act.wait_ge(hv_t.sem, hv_t.at(b, c + 1))
                act.activation(hv[:, u, c, :], X[1 - c % 2][:], ACT.Copy).then_inc(hv_ok.sem, 1)

            def h_gates(b, u, half):
                act.wait_ge(fiT_t.sem, fiT_t.at(b, 1))
                act.wait_ge(scan.sem, scan.at(b, 0))
                act.activation(fi8[:, 0, :], X[0][0:NH, :], ACT.Tanh, bias=bfi[:, 0:1], scale=1.0 / CAP)
                act.activation(fi8[:, 1, :], X[1][0:NH, :], ACT.Tanh, bias=bfi[:, 1:2],
                               scale=1.0 / CAP).then_inc(fi8_ok.sem, 1)

            def h_k(b, u, half):
                act.wait_ge(qk_t.sem, qk_t.at(b, 2))
                act.wait_ge(s_t.sem, s_t.at(b, 0))
                act.activation(kT[:], X[0][:], ACT.Copy).then_inc(kT_ok.sem, 1)

            def h_og(b, u, half):
                act.wait_ge(fi_ok.sem, fi_ok.at(b, 1))
                act.wait_ge(kg_ok.sem, kg_ok.at(b, 4))
                act.wait_ge(sgT_t.sem, sgT_t.at(b, 0))
                for c in range(NT):
                    ins = act.activation(sg[:, c, :], kg[:, c, 0:D], ACT.Tanh, scale=rsh[:, c:c + 1])
                ins.then_inc(sg_ok.sem, 1)

            def h_sg(b, u, half):
                act.wait_ge(sgT_t.sem, sgT_t.at(b, 1))
                act.wait_ge(ho_ok.sem, ho_ok.at(b, 0))
                act.activation(sgT[:, 0, :], X[0][:], ACT.Copy)
                act.activation(sgT[:, 1, :], X[1][:], ACT.Copy).then_inc(sgT_ok.sem, 1)

            def h_dc(b, u, half):
                act.wait_ge(scan.sem, scan.at(b, 15))
                act.activation(dc8[:], dcin[:], ACT.Exp).then_inc(dc_ok.sem, 1)

            def h_ex(b, u, half):
                act.wait_ge(exT_t.sem, exT_t.at(b, 1))
                act.wait_ge(wv_ok.sem, wv_ok.at(b, 0))
                act.wait_ge(nrm.sem, nrm.at(b, 0))
                act.wait_ge(gb_t.sem, gb_t.at(b, 0))
                x2 = X[2][:, :].rearrange("p (c n) -> p c n", n=P)
                act.activation(exs[:], x2[:, :, 32:104], ACT.Exp)
                act.activation(nega[:], x2[:, :, 0:NH], ACT.Copy, scale=-1.0)
                act.activation(gtm[:], X[1][:, 0:NT * NH].rearrange("p (c n) -> p c n", n=NH), ACT.Copy)
                act.activation(dcol[:], X[0][:, 0:NT], ACT.Copy).then_inc(exs_ok.sem, 1)

            def c_gb(b, u, half, c):
                act.wait_ge(gb_t.sem, gb_t.at(b, c + 1))
                act.wait_ge(exs_ok.sem, exs_ok.at(b, 1))
                act.wait_ge(num_t.sem, num_t.at(b, max(c - 1, 0)))
                for h in range(NH):
                    ins = act.activation(W[:, c % 2, h * P:(h + 1) * P], X[h // 4][:, (h % 4) * P:(h % 4 + 1) * P],
                                         ACT.Relu, bias=nega[:, c, h:h + 1])
                ins.then_inc(relu_ok.sem, 1)

            def c_exp(b, u, half, c):
                act.wait_ge(masked.sem, masked.at(b, c + 1))
                act.activation(W[:, c % 2, :], W[:, c % 2, :], ACT.Exp, scale=-1.0).then_inc(dm_ok.sem, 1)

            def t_hoT(b, u, half, k):
                act.wait_ge(y_t.sem, y_t.at(b, 0))
                act.wait_ge(hoT_t.sem, hoT_t.at(b, k + 1))
                act.activation(hoT[:, k, :], X[3 + k][:], ACT.Identity, bias=mixb[:, k:k + 1],
                               scale=mixw[:, k:k + 1]).then_inc(hwT_ok.sem, 1)

            def t_xnT(b, u, half):
                act.wait_ge(xnT_t.sem, xnT_t.at(b, 1))
                act.wait_ge(enc_t.sem, enc_t.at(b, 0))
                act.activation(xnT[:, 0, :], X[3][:], ACT.Copy).then_inc(xnTa.sem, 1)

            def f_enc(b, u, half, m):
                act.wait_ge(enc_t.sem, enc_t.at(b, m + 1))
                if m == 0:
                    act.wait_ge(dec_t.sem, dec_t.at(b, 0))
                act.activation(sp[:, m, :], Y[m % 2][:], ACT.Tanh, bias=encb[:, m:m + 1],
                               scale=0.5).then_inc(enc_ok.sem, 1)

            def f_route(b, u, half):
                act.wait_ge(r1_t.sem, r1_t.at(b, 1))
                act.wait_ge(r2_t.sem, r2_t.at(b, 0))
                act.activation(r1T[:], Y[0][0:M, :], ACT.Tanh, bias=rb1[:]).then_inc(r1_ok.sem, 1)

            def f_top(b, u, half):
                act.wait_ge(top.sem, top.at(b, 3))
                act.activation(e2[:], dl[:], ACT.Exp).then_inc(e2_ok.sem, 1)

            def f_bcast(b, u, half, x):
                act.wait_ge(hid_ok.sem, hid_ok.at(b, 0))
                act.wait_ge(gbc_t.sem, gbc_t.at(b, x + 1))
                act.activation(gb[:, x, :], Y[x % 2][:], ACT.Copy).then_inc(gb_ok.sem, 1)

            def f_out(b, u, half):
                act.wait_ge(w2_t.sem, w2_t.at(b, NCH))
                act.wait_ge(c2s_t.sem, c2s_t.at(b, 0))
                act.activation(oT[:], Y[2][:], ACT.Copy).then_inc(oT_ok.sem, 1)

            def f_c2s(b, u, half, m):
                act.wait_ge(c2s_t.sem, c2s_t.at(b, m + 1))
                if m == 0:
                    act.wait_ge(s2c_t.sem, s2c_t.at(b, 1))
                act.activation(sp[:, m, :], Y[m % 2][:], ACT.Tanh, bias=c2sb[:, m:m + 1],
                               scale=0.5).then_inc(c2s_ok.sem, 1)

            def f_dec(b, u, half, j):
                act.wait_ge(z_ok.sem, z_ok.at(b, j + 1))
                act.activation(z[:, 2 * j:2 * j + 2, :], z[:, 2 * j:2 * j + 2, :], ACT.Tanh,
                               scale=0.5).then_inc(tt_ok.sem, 1)

            run_all("act", act, {"h_eT": h_eT, "h_proj": h_proj, "h_gates": h_gates, "h_k": h_k, "h_og": h_og,
                                 "h_sg": h_sg, "h_dc": h_dc, "h_ex": h_ex, "c_gb": c_gb, "c_exp": c_exp, "t_hoT": t_hoT,
                                 "t_xnT": t_xnT, "f_enc": f_enc, "f_route": f_route, "f_top": f_top, "f_bcast": f_bcast,
                                 "f_out": f_out, "f_c2s": f_c2s, "f_dec": f_dec})

        @block.vector
        def _(dve):
            dve.wait_ge(mults, 2)
            dve.tensor_tensor(hx[:], mulc[:], mulp[:], ALU.bitwise_xor).then_inc(hashed, 1)
            dve.wait_ge(hashed, 1)
            dve.tensor_scalar(hlo[:], hx[:], MOD, None, ALU.bitwise_and).then_inc(hashed, 1)
            dve.tensor_scalar(hhi[:], hx[:], 18, None, ALU.arith_shift_right).then_inc(hashed, 1)
            dve.wait_ge(hashed, 3)
            dve.tensor_tensor(hf[:], hlo[:], hhi[:], ALU.add).then_inc(hashed, 1)
            dve.wait_ge(hashed, 4)
            dve.tensor_scalar(hfix[:], hf[:], 0.0, float(MOD), ALU.is_lt, ALU.mult).then_inc(hashed, 1)
            dve.wait_ge(hashed, 5)
            dve.tensor_tensor(hf[:], hf[:], hfix[:], ALU.add).then_inc(hashed, 1)
            dve.wait_ge(hashed, 6)
            dve.tensor_scalar(hfix[:], hf[:], float(MOD), -float(MOD), ALU.is_ge, ALU.mult).then_inc(hashed, 1)
            dve.wait_ge(hashed, 7)
            dve.tensor_tensor(hf[:], hf[:], hfix[:], ALU.add).then_inc(hashed, 1)
            dve.wait_ge(hash_t, 1)
            dve.tensor_copy(idxf[:], X[0][:, 0:P]).then_inc(hashed, 1)
            dve.wait_ge(hashed, 9)
            dve.memset(idxf[0:1, 0:P:NT], float(MOD)).then_inc(hashed, 1)
            dve.wait_ge(hashed, 10)
            dve.tensor_copy(idx[:], idxf[:]).then_inc(idx_ok, 1)
            dve.wait_ge(loaded, LOADED)
            dve.tensor_scalar(wfold[:, CH:CV], projT[:], scale[:, 0:1], None, ALU.mult).then_inc(prep, 1)
            dve.wait_ge(prep, 1)
            dve.bn_stats(bst[:, 0, :], wfold[:, CH:CV]).then_inc(prep, 1)
            dve.wait_ge(prep, 2)
            dve.bn_aggr(mv[:, 0, :], bst[:, 0, :]).then_inc(prep, 1)
            dve.wait_ge(prep, 3)
            dve.tensor_scalar(projTc[:], wfold[:, CH:CV], mv[:, 0, 0:1], None, ALU.subtract).then_inc(prep, 1)
            dve.tensor_copy(blockmask[:], bc(headmask[:], (P, NH, DV1))).then_inc(prep, 1)
            dve.tensor_scalar(encb[:], encb[:], 0.5, None, ALU.mult).then_inc(prep, 1)
            dve.tensor_scalar(c2sb[:], c2sb[:], 0.5, None, ALU.mult).then_inc(prep, 1)
            dve.tensor_scalar(bfi[:], bfi[:], 1.0 / CAP, None, ALU.mult).then_inc(prep, 1)
            dve.tensor_scalar(be1n[:], be1n[:], -1.0, None, ALU.mult).then_inc(prep, 1)
            dve.tensor_scalar(woutT[:], woutT[:], 0.5, None, ALU.mult).then_inc(prep, 1)
            dve.tensor_scalar(s2cwh[:, :, 0:M], s2cw[:], 0.5, None, ALU.mult)
            dve.tensor_scalar(s2cwh[:, :, M:2 * M], s2cw[:], 0.5, None, ALU.mult).then_inc(prep, 1)
            dve.wait_ge(pprep, 1)
            dve.tensor_scalar(decw[:], decw[:], 0.5, None, ALU.mult).then_inc(prep, 1)
            dve.tensor_tensor(s2cb[:], X[1][:, 0:1], s2cb[:], ALU.add).then_inc(prep, 1)
            dve.tensor_tensor(decb[:], X[2][:, 0:D], decb[:], ALU.add).then_inc(prep, 1)
            dve.tensor_tensor(biasout[:], X[3][0:E, 0:M], be2[:], ALU.add).then_inc(prep, 1)
            dve.wait_ge(pprep, 2)
            dve.tensor_copy(projc[:], X[4][:, 0:2 * P].rearrange("p (t n) -> p t n", n=P)).then_inc(prep, 1)
            dve.wait_ge(pprep, 3)
            for dst, src in ((we1, we1raw), (rw1, rw1raw)):
                dve.tensor_copy(dst[:], src).then_inc(prep, 1)
            dve.wait_ge(prep, 18)
            for dst, src in ((we1, we1raw), (rw1, rw1raw)):
                dve.tensor_tensor(dst[M:2 * M], src[M:2 * M], dst[M:2 * M].bitcast(F32), ALU.subtract).then_inc(prep, 1)
            half_w = (CEND - CV) // 2
            dve.tensor_copy(wfold[:, CV:CV + half_w], Y[0][:, 0:half_w]).then_inc(prep, 1)
            dve.tensor_copy(wfold[:, CV + half_w:CEND], Y[1][:, 0:half_w]).then_inc(prep, 1)

            def h_proj(b, u, half, c):
                if c == 0:
                    dve.wait_ge(sg_ok.sem, sg_ok.at(b, 0))
                    dve.wait_ge(u_t.sem, u_t.at(b, 0))
                dve.wait_ge(kg_t.sem, kg_t.at(b, c + 1))
                dve.tensor_copy(kg[:, c, :], X[2][:, 0:NKG]).then_inc(kg_ok.sem, 1)

            def h_st(b, u, half):
                dve.wait_ge(hv_ok.sem, hv_ok.at(b, 4))
                for c in range(NT):
                    ins = dve.bn_stats(bst[:, c, :], hv[:, u, c, 0:D])
                ins.then_inc(st1.sem, 1)
                dve.wait_ge(st1.sem, st1.at(b, 1))
                dve.sem_inc(passed, 1)
                for c in range(NT):
                    ins = dve.bn_aggr(mv[:, c, :], bst[:, c, :])
                ins.then_inc(st1.sem, 1)
                dve.wait_ge(st1.sem, st1.at(b, 2))
                dve.wait_ge(rs_ok.sem, rs_ok.at(b, 0))
                dve.tensor_scalar(vareps[:], mv[:, :, 1], 1e-5, None, ALU.add).then_inc(st1.sem, 1)

            def h_fi(b, u, half):
                dve.wait_ge(rs_ok.sem, rs_ok.at(b, 1))
                dve.wait_ge(sg_ok.sem, sg_ok.at(b, 0))
                dve.tensor_scalar(rsh[:], rs[:, u], 0.5, None, ALU.mult).then_inc(fi_ok.sem, 1)
                dve.wait_ge(kg_ok.sem, kg_ok.at(b, 4))
                dve.wait_ge(fiT_t.sem, fiT_t.at(b, 0))
                for k in range(2):
                    ins = dve.tensor_tensor(fi[:, k], kg[:, :, CF - CO + k * NH:CF - CO + (k + 1) * NH],
                                            bc(rs[:, u, :], (P, NT, NH)), ALU.mult)
                ins.then_inc(fi_ok.sem, 1)

            def h_q(b, u, half):
                dve.wait_ge(qk_t.sem, qk_t.at(b, 1))
                dve.wait_ge(int_t.sem, int_t.at(b, 0))
                dve.tensor_copy(qT[:], X[2][:]).then_inc(qT_ok.sem, 1)

            def h_qbd(b, u, half, j):
                dve.wait_ge(qT_ok.sem, qT_ok.at(b, 1))
                dve.wait_ge(s_t.sem, s_t.at(b, 0))
                for h in range(2 * j, 2 * j + 2):
                    ins = dve.tensor_scalar(qbd[:, h, :], qT[:], headmask[:, h:h + 1], None, ALU.mult)
                ins.then_inc(qbd_ok.sem, 1)

            Gv = G[:, :].rearrange("p (c t) -> p c t", t=P)
            exv = ex[:, :].rearrange("p (c t) -> p c t", t=P)

            def h_F(b, u, half):
                dve.wait_ge(fi8_ok.sem, fi8_ok.at(b, 1))
                dve.tensor_scalar(fi8[:], fi8[:], CAP, None, ALU.mult).then_inc(scan.sem, 1)
                dve.wait_ge(scan.sem, scan.at(b, 1))
                dve.tensor_tensor_scan(Fs[:], notstart[:], fi8[:, 0, :], 0.0, ALU.mult, ALU.add).then_inc(scan.sem, 1)
                dve.wait_ge(scan.sem, scan.at(b, 2))
                dve.wait_ge(exT_t.sem, exT_t.at(b, 0))
                dve.tensor_tensor(ex[0:NH, :], fi8[:, 1, :], Fs[:], ALU.subtract).then_inc(scan.sem, 1)

            def h_G(b, u, half, c):
                t, last = slice(c * P, (c + 1) * P), (c + 1) * P
                dve.wait_ge(scan.sem, scan.at(b, 3 + 2 * c))
                dve.tensor_tensor_scan(G[:, t], ex[0:NH, t], ex[0:NH, t], mst[:, c:c + 1], ALU.max,
                                       ALU.max).then_inc(scan.sem, 1)
                dve.wait_ge(scan.sem, scan.at(b, 4 + 2 * c))
                dve.tensor_tensor(mst[:, c + 1:c + 2], G[:, last - 1:last], Fs[:, last - 1:last],
                                  ALU.add).then_inc(scan.sem, 1)

            def h_ex(b, u, half):
                dve.wait_ge(scan.sem, scan.at(b, 11))
                dve.wait_ge(dc_ok.sem, dc_ok.at(b, 0))
                dve.tensor_tensor(dcin[:], mst[:, 0:NT], Gv[:, :, P - 1], ALU.subtract).then_inc(scan.sem, 1)
                dve.tensor_tensor(exv[64:64 + NH], bc(mst[:, 0:NT], (NH, NT, P)), Gv,
                                  ALU.subtract).then_inc(scan.sem, 1)
                dve.tensor_tensor(exv[96:96 + NH], exv[0:NH], bc(Gv[:, :, P - 1], (NH, NT, P)),
                                  ALU.subtract).then_inc(scan.sem, 1)
                dve.scalar_tensor_tensor(out=ex[32:32 + NH, :], in0=G[:], scalar=-1.0, in1=Fs[:],
                                         op0=ALU.mult, op1=ALU.subtract).then_inc(scan.sem, 1)

            def c_p(b, u, half, c):
                dve.wait_ge(s_t.sem, s_t.at(b, c + 1))
                dve.wait_ge(dm_ok.sem, dm_ok.at(b, c + 1))
                for j in range(2):
                    w = slice(j * 512, (j + 1) * 512)
                    ins = dve.tensor_tensor(W[:, c % 2, w], X[2 + j][:], W[:, c % 2, w], ALU.mult)
                ins.then_inc(p_ok.sem, 1)

            flat = "p h d -> p (h d)"

            def c_int(b, u, half, c):
                if c > 0:
                    dve.wait_ge(int_t.sem, int_t.at(b, c))
                    dve.wait_ge(num_ok.sem, num_ok.at(b, c))
                    dve.tensor_tensor(tmpI[:], X[2][:, 0:NH * DV1].rearrange("p (h d) -> p h d", d=DV1),
                                      bc(exs[:, c, 32:32 + NH], (P, NH, DV1)), ALU.mult).then_inc(tmpi_ok.sem, 1)
                if c < NT - 1:
                    dve.wait_ge(u_t.sem, u_t.at(b, c + 1))
                    upd = X[3][:, 0:NH * DV1].rearrange("p (h d) -> p h d", d=DV1)
                    if c == 0:
                        dve.wait_ge(int_t.sem, int_t.at(b, 0))
                        dve.tensor_tensor(cbd[:], upd, blockmask[:], ALU.mult).then_inc(cbd_ok.sem, 1)
                    else:
                        dve.tensor_tensor(tmpU[:], upd, blockmask[:], ALU.mult).then_inc(tmpu_ok.sem, 1)
                        dve.wait_ge(tmpu_ok.sem, tmpu_ok.at(b, c))
                        dve.scalar_tensor_tensor(out=cbd[:].rearrange(flat), in0=cbd[:].rearrange(flat),
                                                 scalar=dcol[:, c:c + 1], in1=tmpU[:].rearrange(flat),
                                                 op0=ALU.mult, op1=ALU.add).then_inc(cbd_ok.sem, 1)

            def c_num(b, u, half, c):
                dve.wait_ge(num_t.sem, num_t.at(b, c + 1))
                new = X[4][:, 0:NH * DV1]
                if c == 0:
                    dve.tensor_copy(num[:, c].rearrange(flat), new).then_inc(num_ok.sem, 1)
                else:
                    dve.wait_ge(tmpi_ok.sem, tmpi_ok.at(b, c))
                    dve.tensor_tensor(num[:, c].rearrange(flat), new, tmpI[:].rearrange(flat),
                                      ALU.add).then_inc(num_ok.sem, 1)

            def t_den(b, u, half):
                n = 0

                def step(ins):
                    nonlocal n
                    ins.then_inc(nrm.sem, 1)
                    n += 1
                    if n < 6:
                        dve.wait_ge(nrm.sem, nrm.at(b, n))

                dve.wait_ge(num_ok.sem, num_ok.at(b, 4))
                rsb = bc(rs[:, u, :], (P, NT, NH))
                step(dve.tensor_tensor(den[:], num[:, :, :, DV], rsb, ALU.mult))
                step(dve.scalar_tensor_tensor(out=den[:], in0=den[:], scalar=-1.0, in1=den[:],
                                              op0=ALU.mult, op1=ALU.max))
                step(dve.scalar_tensor_tensor(out=den[:], in0=den[:], scalar=DQK ** -0.5, in1=exs[:, :, 0:NH],
                                              op0=ALU.mult, op1=ALU.max))
                step(dve.tensor_scalar(den[:], den[:], 1e-6, None, ALU.add))
                step(dve.reciprocal(den[:], den[:]))
                step(dve.scalar_tensor_tensor(out=den[:], in0=den[:], scalar=DQK ** -0.5, in1=rsb,
                                              op0=ALU.mult, op1=ALU.mult))

            def t_hm(b, u, half):
                dve.wait_ge(nrm.sem, nrm.at(b, 6))
                dve.wait_ge(hoT_t.sem, hoT_t.at(b, 0))
                for c in range(NT):
                    ins = dve.tensor_tensor(hm[:, c].rearrange("p (h d) -> p h d", d=DV), num[:, c, :, 0:DV],
                                            bc(den[:, c], (P, NH, DV)), ALU.mult)
                ins.then_inc(nrm.sem, 1)
                dve.wait_ge(nrm.sem, nrm.at(b, 7))
                for c in range(NT):
                    ins = dve.bn_stats(bst2[:, c, :], hm[:, c, :])
                ins.then_inc(nrm.sem, 1)
                dve.wait_ge(nrm.sem, nrm.at(b, 8))
                dve.sem_inc(passed, 1)
                for c in range(NT):
                    ins = dve.bn_aggr(mv2[:, c, :], bst2[:, c, :])
                ins.then_inc(nrm.sem, 1)
                dve.wait_ge(nrm.sem, nrm.at(b, 9))
                dve.tensor_scalar(vareps2[:], mv2[:, :, 1], 1e-6, None, ALU.add).then_inc(nrm.sem, 1)

            def t_norm(b, u, half):
                dve.wait_ge(rs2_ok.sem, rs2_ok.at(b, 1))
                for c in range(NT):
                    ins = dve.tensor_scalar(hm[:, c, :], hm[:, c, :], mv2[:, c, 0:1], rs2[:, c:c + 1],
                                            ALU.subtract, ALU.mult)
                ins.then_inc(hn_ok.sem, 1)

            def t_hoT(b, u, half, k):
                dve.wait_ge(hwT_ok.sem, hwT_ok.at(b, k + 1))
                dve.wait_ge(sgT_ok.sem, sgT_ok.at(b, 1))
                dve.scalar_tensor_tensor(out=hoT[:, k, :], in0=sgT[:, k, :], scalar=1.0, in1=hoT[:, k, :],
                                         op0=ALU.add, op1=ALU.mult).then_inc(ho_ok.sem, 1)

            def t_y(b, u, half, j):
                dve.wait_ge(y_t.sem, y_t.at(b, j + 1))
                if not (isinstance(b, int) and b < 2):
                    dve.wait_ge(out_ok.sem, out_ok.at(b - 1, 0))
                dve.tensor_tensor(h2[:, u, 2 * j:2 * j + 2, :], X[3 + j][:, :].rearrange("p (c d) -> p c d", d=D),
                                  hv[:, u, 2 * j:2 * j + 2, 0:D], ALU.add).then_inc(h2_ok.sem, 1)

            def t_st(b, u, half):
                dve.wait_ge(h2_ok.sem, h2_ok.at(b, 2))
                for c in range(NT):
                    ins = dve.bn_stats(bst3[:, c, :], h2[:, u, c, :])
                ins.then_inc(st3.sem, 1)
                dve.wait_ge(st3.sem, st3.at(b, 1))
                dve.sem_inc(passed, 1)
                for c in range(NT):
                    ins = dve.bn_aggr(mv3[:, c, :], bst3[:, c, :])
                ins.then_inc(st3.sem, 1)
                dve.wait_ge(st3.sem, st3.at(b, 2))
                dve.tensor_scalar(vareps3[:], mv3[:, :, 1], 1e-5, None, ALU.add).then_inc(st3.sem, 1)

            def t_xn(b, u, half):
                dve.wait_ge(rs3_ok.sem, rs3_ok.at(b, 1))
                dve.wait_ge(xnT_t.sem, xnT_t.at(b, 0))
                for c in range(NT):
                    ins = dve.tensor_scalar(xn[:, c, :], h2[:, u, c, :], mv3[:, c, 0:1], rs3[:, c:c + 1],
                                            ALU.subtract, ALU.mult)
                ins.then_inc(xn_ok.sem, 1)

            def t_xnT(b, u, half):
                dve.wait_ge(xnT_t.sem, xnT_t.at(b, 2))
                dve.wait_ge(enc_t.sem, enc_t.at(b, 0))
                dve.tensor_copy(xnT[:, 1, :], X[4][:]).then_inc(xnTd.sem, 1)

            def f_s2c(b, u, half):
                dve.wait_ge(s2c_t.sem, s2c_t.at(b, 1))
                dve.wait_ge(w1_t.sem, w1_t.at(b, 0))
                dve.tensor_scalar(conth[:], Y[2][:], s2cb[:, 0:1], None, ALU.add).then_inc(cont_ok.sem, 1)
                dve.wait_ge(cont_ok.sem, cont_ok.at(b, 1))
                dve.scalar_tensor_tensor(out=contl[:], in0=Y[2][:], scalar=s2cb[:, 0:1], in1=conth[:].bitcast(F32),
                                         op0=ALU.add, op1=ALU.subtract).then_inc(cont_ok.sem, 1)

            def f_top(b, u, half):
                dve.wait_ge(r2_t.sem, r2_t.at(b, 1))
                dve.tensor_tensor(lg[:], Y[1][:, 0:NT * E].rearrange("p (c x) -> p c x", x=E),
                                  bc1(rb2[:], (P, NT, E)), ALU.add).then_inc(top.sem, 1)
                dve.wait_ge(top.sem, top.at(b, 1))
                dve.sem_inc(passed, 1)
                for c in range(NT):
                    ins = dve.max(mx8[:, c, :], lg[:, c, :])
                ins.then_inc(top.sem, 1)
                dve.wait_ge(top.sem, top.at(b, 2))
                dve.wait_ge(e2_ok.sem, e2_ok.at(b, 0))
                dve.tensor_tensor(dl[:], mx8[:, :, 1], mx8[:, :, 0], ALU.subtract).then_inc(top.sem, 1)
                dve.sem_inc(passed, 1)
                for c in range(NT):
                    ins = dve.max_index(ix8[:, c, :], mx8[:, c, :], lg[:, c, :])
                ins.then_inc(top.sem, 1)
                dve.wait_ge(top.sem, top.at(b, 4))
                dve.tensor_copy(ixf[:], ix8[:, :, 0:2]).then_inc(top.sem, 1)
                dve.wait_ge(top.sem, top.at(b, 5))
                iot = bc1(iota8[:], (P, NT, E))
                dve.tensor_tensor(eq0[:], iot, bc(ixf[:, :, 0], (P, NT, E)), ALU.is_equal).then_inc(top.sem, 1)
                dve.tensor_tensor(eq1[:], iot, bc(ixf[:, :, 1], (P, NT, E)), ALU.is_equal).then_inc(top.sem, 1)

            def f_gate(b, u, half):
                dve.wait_ge(e2_ok.sem, e2_ok.at(b, 1))
                dve.tensor_scalar(s1[:], e2[:], 1.0, None, ALU.add).then_inc(top.sem, 1)
                dve.wait_ge(top.sem, top.at(b, 8))
                dve.reciprocal(w12[:, :, 0], s1[:]).then_inc(top.sem, 1)
                dve.wait_ge(top.sem, top.at(b, 9))
                dve.tensor_tensor(w12[:, :, 1], e2[:], w12[:, :, 0], ALU.mult).then_inc(top.sem, 1)
                dve.tensor_tensor(eq0[:], eq0[:], bc(w12[:, :, 0], (P, NT, E)), ALU.mult).then_inc(top.sem, 1)
                dve.wait_ge(top.sem, top.at(b, 10))
                dve.tensor_tensor(eq1[:], eq1[:], bc(w12[:, :, 1], (P, NT, E)), ALU.mult).then_inc(top.sem, 1)
                dve.wait_ge(top.sem, top.at(b, 12))
                dve.wait_ge(gbc_t.sem, gbc_t.at(b, 0))
                dve.tensor_tensor(g[:], eq0[:], eq1[:], ALU.add).then_inc(top.sem, 1)

            def f_gT(b, u, half):
                dve.wait_ge(gT_t.sem, gT_t.at(b, 1))
                dve.wait_ge(o_t.sem, o_t.at(b, 0))
                dve.tensor_copy(gT[:], Y[2][0:E, :]).then_inc(gT_ok.sem, 1)

            def f_exp(b, u, half, ch):
                dve.wait_ge(w1_t.sem, w1_t.at(b, ch + 1))
                dve.wait_ge(gb_ok.sem, gb_ok.at(b, ch // 2 + 1))
                dve.wait_ge(w2_t.sem, w2_t.at(b, max(ch - 3, 0)))
                dve.scalar_tensor_tensor(out=hid[:, ch % 4, :], in0=Y[ch % 2][:], scalar=be1n[:, ch:ch + 1],
                                         in1=gb[:, ch // 2, :], op0=ALU.max, op1=ALU.mult).then_inc(hid_ok.sem, 1)

            def f_dec(b, u, half, j):
                dve.wait_ge(dec_t.sem, dec_t.at(b, j + 1))
                if j == 0:
                    dve.wait_ge(gg_ok.sem, gg_ok.at(b, 0))
                dve.tensor_tensor(z[:, 2 * j:2 * j + 2, :], Y[j][:, :].rearrange("p (c d) -> p c d", d=D),
                                  bc1(decb[:], (P, 2, D)), ALU.add).then_inc(z_ok.sem, 1)

            def l_st(b, u, half):
                dve.wait_ge(tt_ok.sem, tt_ok.at(b, 2))
                for c in range(NT):
                    ins = dve.bn_stats(bstf[:, c, :], z[:, c, :])
                ins.then_inc(st4.sem, 1)
                dve.wait_ge(st4.sem, st4.at(b, 1))
                dve.sem_inc(passed, 1)
                for c in range(NT):
                    ins = dve.bn_aggr(mvf[:, c, :], bstf[:, c, :])
                ins.then_inc(st4.sem, 1)
                dve.wait_ge(st4.sem, st4.at(b, 2))
                dve.tensor_scalar(vareps4[:], mvf[:, :, 1], 4e-5, None, ALU.add).then_inc(st4.sem, 1)

            def l_norm(b, u, half):
                dve.wait_ge(rs4_ok.sem, rs4_ok.at(b, 1))
                for c in range(NT):
                    ins = dve.tensor_scalar(z[:, c, :], z[:, c, :], mvf[:, c, 0:1], rs4[:, c:c + 1],
                                            ALU.subtract, ALU.mult)
                ins.then_inc(tn_ok.sem, 1)

            def l_sum(b, u, half):
                dve.wait_ge(gg_ok.sem, gg_ok.at(b, 2))
                dve.tensor_tensor(gg[:], gg[:], h2[:, u], ALU.add).then_inc(out_ok.sem, 1)

            run_all("dve", dve, {"h_proj": h_proj, "h_st": h_st, "h_fi": h_fi, "h_q": h_q, "h_qbd": h_qbd, "h_F": h_F,
                                 "h_G": h_G, "h_ex": h_ex, "c_p": c_p, "c_int": c_int, "c_num": c_num, "t_den": t_den,
                                 "t_hm": t_hm, "t_norm": t_norm, "t_hoT": t_hoT, "t_y": t_y, "t_st": t_st, "t_xn": t_xn,
                                 "t_xnT": t_xnT, "f_s2c": f_s2c, "f_top": f_top, "f_gate": f_gate, "f_gT": f_gT,
                                 "f_exp": f_exp, "f_dec": f_dec, "l_st": l_st, "l_norm": l_norm, "l_sum": l_sum})

        @block.tensor
        def _(pe):
            mm = pe.matmul
            pe.wait_ge(loaded, LOADED)
            pe.wait_ge(hashed, 8)
            pe.transpose(X[0][:, 0:P], hf[:], ident[:]).then_inc(hash_t, 1)
            pe.wait_ge(pconst, 6)
            for k in range(4):
                for x in range(2):
                    mm(X[1][x * M:(x + 1) * M, 0:1], s2cw[:, k, :], halves[:, 0:1], start=k == 0, stop=k == 3)
            for k in range(4):
                mm(X[2][:, 0:D], halves[:], decw[:, k, :], start=k == 0, stop=k == 3)
            pe.wait_ge(prep, 9)
            for ch in range(NCH):
                ins = mm(X[3][0:E, 0:M], be1pad[:, ch, :], we2[:, ch, :], start=ch == 0, stop=ch == NCH - 1)
            ins.then_inc(pprep, 1)
            for t in range(2):
                ins = pe.transpose(X[4][:, t * P:(t + 1) * P], projTc[:, t * P:(t + 1) * P], ident[:])
            ins.then_inc(pprep, 1)
            pe.wait_ge(prep, 16)
            half_w = (CEND - CV) // 2
            for j in range(2):
                for t in range(2):
                    ins = mm(Y[j][:, 0:half_w], projc[:, t, :], wall[:, t, j * half_w:(j + 1) * half_w],
                             start=t == 0, stop=t == 1)
            ins.then_inc(pprep, 1)
            pe.wait_ge(prep, PREPARED)

            def h_eT(b, u, half):
                pe.wait_ge(gathered[u], (half + 1) * 16 * NT)
                pe.wait_ge(relu_ok.sem, relu_ok.at(b, 0))
                for c in range(NT):
                    ins = pe.transpose(X[0][:, c * P:(c + 1) * P], e[:, u, c, :], ident[:])
                ins.then_inc(eT_t.sem, 1)

            def h_proj(b, u, half, c):
                if c == 0:
                    pe.wait_ge(eT_ok.sem, eT_ok.at(b, 1))
                    pe.wait_ge(tmpi_ok.sem, tmpi_ok.at(b, 0))
                t = eT[:, c * P:(c + 1) * P]
                if c >= 2:
                    pe.wait_ge(hv_ok.sem, hv_ok.at(b, c - 1))
                mm(X[1 - c % 2][:], t, wfold[:, CH:CO], start=True, stop=True).then_inc(hv_t.sem, 1)
                if c >= 1:
                    pe.wait_ge(kg_ok.sem, kg_ok.at(b, c))
                mm(X[2][:, 0:NKG], t, wfold[:, CO:CQ], start=True, stop=True).then_inc(kg_t.sem, 1)

            def h_gates(b, u, half):
                pe.wait_ge(fi_ok.sem, fi_ok.at(b, 2))
                pe.wait_ge(hv_ok.sem, hv_ok.at(b, 4))
                for k in range(2):
                    for c in range(NT):
                        ins = pe.transpose(X[k][0:NH, c * P:(c + 1) * P], fi[:, k, c, :], ident[:])
                ins.then_inc(fiT_t.sem, 1)

            def h_q(b, u, half):
                pe.wait_ge(kg_ok.sem, kg_ok.at(b, 4))
                mm(X[2][:], wfold[:, CQ:CEND], eT[:], start=True, stop=True).then_inc(qk_t.sem, 1)

            def h_k(b, u, half):
                pe.wait_ge(fi8_ok.sem, fi8_ok.at(b, 1))
                mm(X[0][:], wfold[:, CK:CQ], eT[:], start=True, stop=True).then_inc(qk_t.sem, 1)

            def h_sg(b, u, half):
                pe.wait_ge(sg_ok.sem, sg_ok.at(b, 1))
                pe.wait_ge(kT_ok.sem, kT_ok.at(b, 1))
                for k in range(2):
                    for c in range(NT):
                        ins = pe.transpose(X[k][:, c * P:(c + 1) * P], sg[:, c, k * P:(k + 1) * P], ident[:])
                ins.then_inc(sgT_t.sem, 1)

            def h_ex(b, u, half):
                pe.wait_ge(scan.sem, scan.at(b, 15))
                pe.wait_ge(qT_ok.sem, qT_ok.at(b, 1))
                pe.wait_ge(sgT_ok.sem, sgT_ok.at(b, 1))
                for c in range(NT):
                    pe.transpose(X[2][:, c * P:c * P + 104], ex[0:104, c * P:(c + 1) * P], ident[0:104, 0:104])
                for c in range(NT):
                    pe.transpose(X[1][:, c * NH:(c + 1) * NH], G[:, c * P:(c + 1) * P], ident[0:NH, 0:NH])
                pe.wait_ge(dc_ok.sem, dc_ok.at(b, 1))
                mm(X[0][:, 0:NT], headsel[:], dc8[:], start=True, stop=True).then_inc(exT_t.sem, 1)

            def c_gb(b, u, half, c):
                if c == 0:
                    pe.wait_ge(exs_ok.sem, exs_ok.at(b, 1))
                else:
                    pe.wait_ge(relu_ok.sem, relu_ok.at(b, c))
                for h in range(NH):
                    ins = pe.transpose(X[h // 4][:, (h % 4) * P:(h % 4 + 1) * P],
                                       gtm[:, c, h:h + 1].broadcast_to((P, P)), ident[:])
                ins.then_inc(gb_t.sem, 1)

            def c_s(b, u, half, c):
                if c == 0:
                    pe.wait_ge(qbd_ok.sem, qbd_ok.at(b, 4))
                    pe.wait_ge(exs_ok.sem, exs_ok.at(b, 1))
                    pe.wait_ge(xnTa.sem, xnTa.at(b, 0))
                else:
                    pe.wait_ge(p_ok.sem, p_ok.at(b, c))
                    if c > 1:
                        pe.wait_ge(tmpi_ok.sem, tmpi_ok.at(b, c - 1))
                    pe.wait_ge(cbd_ok.sem, cbd_ok.at(b, c))
                for j in range(2):
                    ins = mm(X[2 + j][:], kT[:, c * P:(c + 1) * P], qbd[:, 4 * j:4 * j + 4, c * P:(c + 1) * P],
                             start=True, stop=True)
                ins.then_inc(s_t.sem, 1)

            def c_int(b, u, half, c):
                pe.wait_ge(p_ok.sem, p_ok.at(b, c + 1))
                if c > 0:
                    pe.wait_ge(cbd_ok.sem, cbd_ok.at(b, c))
                    mm(X[2][:, 0:NH * DV1], qT[:, c * P:(c + 1) * P], cbd[:].rearrange("p h d -> p (h d)"),
                       start=True, stop=True).then_inc(int_t.sem, 1)
                if c < NT - 1:
                    pe.wait_ge(wv_ok.sem, wv_ok.at(b, c + 1))
                    mm(X[3][:, 0:NH * DV1], kg[:, c, CK - CO:CQ - CO], wv[:, c].rearrange("p h d -> p (h d)"),
                       start=True, stop=True).then_inc(u_t.sem, 1)

            def c_num(b, u, half, c):
                pe.wait_ge(vh_ok.sem, vh_ok.at(b, 1))
                pe.wait_ge(num_ok.sem, num_ok.at(b, c))
                if c == 0:
                    pe.wait_ge(xnTd.sem, xnTd.at(b, 0))
                for h in range(NH):
                    ins = mm(X[4][:, h * DV1:(h + 1) * DV1], W[:, c % 2, h * P:(h + 1) * P], vh[:, c, h, :],
                             start=True, stop=True)
                ins.then_inc(num_t.sem, 1)

            def t_hoT(b, u, half):
                pe.wait_ge(hn_ok.sem, hn_ok.at(b, 1))
                for k in range(2):
                    for c in range(NT):
                        ins = pe.transpose(X[3 + k][:, c * P:(c + 1) * P], hm[:, c, k * P:(k + 1) * P], ident[:])
                    ins.then_inc(hoT_t.sem, 1)

            def t_y(b, u, half, j):
                pe.wait_ge(ho_ok.sem, ho_ok.at(b, 2))
                for c in range(2):
                    for k in range(2):
                        ins = mm(X[3 + j][:, c * D:(c + 1) * D], hoT[:, k, (2 * j + c) * P:(2 * j + c + 1) * P],
                                 woutT[:, k, :], start=k == 0, stop=k == 1)
                ins.then_inc(y_t.sem, 1)

            def t_xnT(b, u, half):
                pe.wait_ge(xn_ok.sem, xn_ok.at(b, 1))
                for k in range(2):
                    for c in range(NT):
                        ins = pe.transpose(X[3 + k][:, c * P:(c + 1) * P], xn[:, c, k * P:(k + 1) * P], ident[:])
                    ins.then_inc(xnT_t.sem, 1)

            def f_enc(b, u, half, m):
                if m == 0:
                    pe.wait_ge(xnTa.sem, xnTa.at(b, 1))
                    pe.wait_ge(xnTd.sem, xnTd.at(b, 1))
                    pe.wait_ge(z_ok.sem, z_ok.at(b, 0))
                if m >= 2:
                    pe.wait_ge(enc_ok.sem, enc_ok.at(b, m - 1))
                for k in range(2):
                    ins = mm(Y[m % 2][:], encw[:, k, m * P:(m + 1) * P], xnT[:, k, :], start=k == 0, stop=k == 1)
                ins.then_inc(enc_t.sem, 1)

            def f_s2c(b, u, half):
                pe.wait_ge(enc_ok.sem, enc_ok.at(b, 4))
                pe.wait_ge(oT_ok.sem, oT_ok.at(b, 0))
                for k in range(4):
                    ins = mm(Y[2][:], s2cwh[:, k, :], sp[:, k, :], start=k == 0, stop=k == 3)
                ins.then_inc(s2c_t.sem, 1)

            def f_route(b, u, half):
                pe.wait_ge(cont_ok.sem, cont_ok.at(b, 2))
                mm(Y[0][0:M, :], rw1[:], conth[:], start=True, stop=False)
                mm(Y[0][0:M, :], rw1[:], contl[:], start=False, stop=True).then_inc(r1_t.sem, 1)

            def f_logit(b, u, half):
                pe.wait_ge(r1_ok.sem, r1_ok.at(b, 1))
                for c in range(NT):
                    ins = mm(Y[1][:, c * E:(c + 1) * E], r1T[:, c * P:(c + 1) * P], rw2[:], start=True, stop=True)
                ins.then_inc(r2_t.sem, 1)

            def f_gT(b, u, half):
                pe.wait_ge(cont_ok.sem, cont_ok.at(b, 2))
                pe.wait_ge(top.sem, top.at(b, 13))
                for c in range(NT):
                    ins = pe.transpose(Y[2][0:E, c * P:(c + 1) * P], g[:, c, :], ident[:])
                ins.then_inc(gT_t.sem, 1)

            def f_bcast(b, u, half, x):
                pe.wait_ge(top.sem, top.at(b, 13))
                if x >= 2:
                    pe.wait_ge(gb_ok.sem, gb_ok.at(b, x - 1))
                for c in range(NT):
                    ins = pe.transpose(Y[x % 2][:, c * P:(c + 1) * P], g[:, c, x:x + 1].broadcast_to((P, P)), ident[:])
                ins.then_inc(gbc_t.sem, 1)

            def f_exp(b, u, half, ch):
                if ch < 2:
                    pe.wait_ge(gb_ok.sem, gb_ok.at(b, 7 + ch))
                else:
                    pe.wait_ge(hid_ok.sem, hid_ok.at(b, ch - 1))
                w = we1[:, ch * P:(ch + 1) * P]
                mm(Y[ch % 2][:], w, conth[:], start=True, stop=False)
                mm(Y[ch % 2][:], w, contl[:], start=False, stop=True).then_inc(w1_t.sem, 1)

            def f_sec(b, u, half, j):
                if j == 0:
                    pe.wait_ge(gT_ok.sem, gT_ok.at(b, 1))
                    mm(Y[2][0:M, :], biasout[:], gT[:], start=True, stop=False).then_inc(o_t.sem, 1)
                pe.wait_ge(hid_ok.sem, hid_ok.at(b, 2 * j + 2))
                for ch in (2 * j, 2 * j + 1):
                    x = ch % 2 * M
                    mm(Y[2][x:x + M, :], we2[:, ch, :], hid[:, ch % 4, :], start=ch == 1,
                       stop=j == NCH // 2 - 1).then_inc(w2_t.sem, 1)

            def f_c2s(b, u, half, m):
                if m == 0:
                    pe.wait_ge(oT_ok.sem, oT_ok.at(b, 1))
                if m >= 2:
                    pe.wait_ge(c2s_ok.sem, c2s_ok.at(b, m - 1))
                mm(Y[m % 2][:], c2sw[:, m * P:(m + 1) * P], oT[:], start=True, stop=True).then_inc(c2s_t.sem, 1)

            def f_dec(b, u, half, j):
                pe.wait_ge(c2s_ok.sem, c2s_ok.at(b, 4))
                for c in range(2):
                    for k in range(4):
                        t = (2 * j + c) * P
                        ins = mm(Y[j][:, c * D:(c + 1) * D], sp[:, k, t:t + P], decw[:, k, :], start=k == 0, stop=k == 3)
                ins.then_inc(dec_t.sem, 1)

            run_all("pe", pe, {"h_eT": h_eT, "h_proj": h_proj, "h_gates": h_gates, "h_q": h_q, "h_k": h_k, "h_sg": h_sg,
                               "h_ex": h_ex, "c_gb": c_gb, "c_s": c_s, "c_int": c_int, "c_num": c_num, "t_hoT": t_hoT,
                               "t_y": t_y, "t_xnT": t_xnT, "f_enc": f_enc, "f_s2c": f_s2c, "f_route": f_route, "f_logit": f_logit,
                               "f_gT": f_gT, "f_bcast": f_bcast, "f_exp": f_exp, "f_sec": f_sec, "f_c2s": f_c2s,
                               "f_dec": f_dec})


def kernel(**inputs):
    import numpy as np
    import concourse.bacc as bacc
    from concourse.bass_utils import run_bass_kernel_spmd

    a = {k: np.ascontiguousarray(v) for k, v in inputs.items()}
    f = np.float32

    def attn(n):
        return a["L0_attn_" + n]

    def ffn(n):
        return a["L0_ffn_" + n]

    x = a["x"].reshape(-1)
    be1 = ffn("be1").reshape(NCH, P)
    be1pad = np.zeros((P, NCH, E), f)
    for ch in range(NCH):
        be1pad[:, ch, ch // (HE // P)] = be1[ch]
    heads = np.repeat(np.eye(NH, dtype=f), DQK, axis=1)
    notstart = np.ones((1, S), f)
    notstart[:, ::P] = 0
    arrays = {
        "tok": x.reshape(TILES, P), "tokp": np.roll(x, 1).reshape(TILES, P),
        "emb": a["L0_tok_emb_weight"], "projT": a["L0_tok_proj_weight"].T, "scale": a["L0_tok_scale"].reshape(1, 1),
        "ident": np.eye(P, dtype=f), "headmask": heads.T, "headsel": heads, "notstart": notstart,
        "iota8": np.arange(E, dtype=f)[None],
        "wall": np.concatenate([attn(n) for n in ("Wv", "Wog", "Wf", "Wi", "Wk", "Wq")], axis=0).T,
        "bfi": np.stack([attn("bf"), attn("bi")], axis=1), "mixw": attn("ln_w").reshape(2, P).T,
        "mixb": attn("ln_b").reshape(2, P).T,
        "woutT": attn("Wout").T, "encw": ffn("enc_W"), "encb": ffn("enc_b").reshape(4, P).T,
        "s2cw": ffn("s2c_W"), "s2cb": ffn("s2c_b")[:, None], "rw1": ffn("rW1"), "rb1": ffn("rb1")[:, None],
        "rw2": ffn("rW2"), "rb2": ffn("rb2")[None], "we1": ffn("We1").transpose(1, 0, 2).reshape(M, E * HE),
        "be1": be1.T, "be1pad": be1pad.reshape(P, NCH * E),
        "we2": ffn("We2").reshape(NCH, P, M).transpose(1, 0, 2).reshape(P, NCH * M), "be2": ffn("be2"),
        "c2sw": ffn("c2s_W"), "c2sb": ffn("c2s_b").reshape(4, P).T, "decw": ffn("dec_W"), "decb": ffn("dec_b")[None],
        "lng": ffn("ln_g")[None], "lnb": ffn("ln_b")[None],
    }
    nc = bacc.Bacc("TRN2", target_bir_lowering=False, num_devices=1)
    feed, aps = {}, {}
    for name, arr in arrays.items():
        arr = np.ascontiguousarray(arr)
        feed["in_" + name] = arr
        aps[name] = nc.dram_tensor("in_" + name, arr.shape, mybir.dt.from_np(arr.dtype), kind="ExternalInput").ap()
    out = nc.dram_tensor("out", (NB * S, D), F32, kind="ExternalOutput").ap()
    tower(nc, aps, out)
    r = run_bass_kernel_spmd(nc, [feed], core_ids=[0])
    return r.results[0]["out"].reshape(NB, S, D)
```

```python
from contextlib import ExitStack

import concourse.bass as bass
from concourse import mybir

F32 = mybir.dt.float32
F32R = mybir.dt.float32r
I32 = mybir.dt.int32
U32 = mybir.dt.uint32
ACT = mybir.ActivationFunctionType
ALU = mybir.AluOpType

P = 128
NB, S = 32, 512
NT = S // P
TILES = NB * NT
BUCKETS, EDIM, D = 262144, 128, 256
NH, DQK, DV = 8, 16, 32
DV1 = DV + 1
H, M, E, HE = 512, 64, 8, 256
NCH = E * HE // P
CAP = 15.0
HASH_CUR, HASH_PREV, MOD = 36313, 27191, BUCKETS - 1
CH, CV, CO, CF, CI, CK, CQ, CEND = 0, 256, 512, 768, 776, 784, 912, 1040
NKG = CQ - CO


class PerBatch:

    def __init__(self, sem, per):
        self.sem, self.per = sem, per

    def at(self, b, n):
        return b * self.per + n


def bc(ap, shape):
    return ap.unsqueeze(len(ap.shape)).broadcast_to(shape)


def bc1(ap, shape):
    return ap.unsqueeze(1).broadcast_to(shape)


def tower(nc, A, out):
    with ExitStack() as ctx:
        def sb(name, shape, dt=F32):
            return ctx.enter_context(nc.sbuf_tensor(name, shape, dt))

        def sem(name):
            return ctx.enter_context(nc.semaphore(name))

        def per(name, n):
            return PerBatch(sem(name), n)

        gb = sb("gb", [P, E, S])
        W = sb("W", [P, 2, NH * P])
        z = sb("z", [P, NT, D])
        hm = sb("hm", [P, NT, D])
        wall = gb[:, 0:4, :].rearrange("p a b -> p (a b)")[:, 0:2 * (CEND - CV)].rearrange("p (t n) -> p t n", t=2)
        we1raw = W[:, :, :].rearrange("p a b -> p (a b)")
        rw1raw = gb[:, 6, 0:M]
        projTc = gb[:, 4, 0:D]
        projT = gb[:, 7, 0:D]
        s2cw = gb[:, 7, D:2 * D].rearrange("p (k m) -> p k m", m=M)
        projc = gb[:, 5, 0:2 * P].rearrange("p (t n) -> p t n", t=2)
        qbd = sb("qbd", [P, NH, S])
        spare = qbd[:, 3:8, :].rearrange("p h s -> p (h s)")
        wfold = spare[:, 0:CEND]
        encwr = spare[:, CEND:CEND + 2 * H].rearrange("p (t n) -> p t n", n=H)
        be1pad = spare[:, CEND + 2 * H:CEND + 2 * H + NCH * E].rearrange("p (c e) -> p c e", e=E)
        c2swr = z[:, 0:2, :].rearrange("p c d -> p (c d)")
        hash_tiles = [qbd[:, n // 4, (n % 4) * P:(n % 4 + 1) * P] for n in range(10)]
        tok, tokp, mulc, mulp, hx, hlo, hhi = (t.bitcast(I32) for t in hash_tiles[:7])
        hf, hfix, idxf = hash_tiles[7:]
        ident = sb("ident", [P, P])
        headmask = sb("headmask", [P, NH])
        headsel = sb("headsel", [NH, P])
        blockmask = sb("blockmask", [P, NH, DV1])
        notstart = sb("notstart", [NH, S])
        iota8 = sb("iota8", [P, E])
        halves = sb("halves", [P, P])
        mhalf = sb("mhalf", [P, NT])
        scale = sb("scale", [P, 1])
        wfh, wfl = sb("wfh", [P, CEND], F32R), sb("wfl", [P, CEND], F32R)
        bfi = sb("bfi", [NH, 2])
        mixw = sb("mixw", [P, 2])
        mixb = sb("mixb", [P, 2])
        woutT = sb("woutT", [P, 2, D])
        encwh, encwl = sb("encwh", [P, 2, H], F32R), sb("encwl", [P, 2, H], F32R)
        encb = sb("encb", [P, 4])
        s2cwh = sb("s2cwh", [P, 4, 2 * M])
        s2cb = sb("s2cb", [2 * M, 1])
        rw1 = sb("rw1", [2 * M, M], F32R)
        rb1 = sb("rb1", [M, 1])
        rw2 = sb("rw2", [M, E])
        rb2 = sb("rb2", [P, E])
        we1 = sb("we1", [2 * M, E * HE], F32R)
        be1n = sb("be1n", [P, NCH])
        we2 = sb("we2", [P, NCH, M])
        be2 = sb("be2", [E, M])
        biasout = sb("biasout", [E, M])
        c2swh, c2swl = sb("c2swh", [2 * M, H], F32R), sb("c2swl", [2 * M, H], F32R)
        c2sb = sb("c2sb", [P, 4])
        decw = sb("decw", [P, 4, D])
        decb = sb("decb", [P, D])
        lng = sb("lng", [P, D])
        lnb = sb("lnb", [P, D])
        idx = sb("idx", [P, P], I32)
        idxs = sb("idxs", [P, 2, NT], I32)
        e = sb("e", [P, 2, NT, EDIM])
        eTh, eTl = sb("eTh", [P, S], F32R), sb("eTl", [P, S], F32R)
        hh = sb("hh", [P, 2, NT, D])
        v = sb("v", [P, NT, D])
        kg = sb("kg", [P, NT, NKG])
        bst, bst2, bst3 = (sb(f"bst{n}", [P, NT, 6]) for n in range(3))
        mv, mv2, mv3 = (sb(f"mv{n}", [P, NT, 2]) for n in range(3))
        vareps = sb("vareps", [P, NT])
        rs = sb("rs", [P, 2, NT])
        rsh = sb("rsh", [P, NT])
        fi = sb("fi", [P, 2, NT, NH])
        fi8 = sb("fi8", [NH, 2, S])
        Fs = sb("Fs", [NH, S])
        ex = sb("ex", [P, S])
        G = sb("G", [NH, S])
        mst = sb("mst", [NH, NT + 1])
        dcin = sb("dcin", [NH, NT])
        dc8 = sb("dc8", [NH, NT])
        exs = sb("exs", [P, NT, 72])
        nega = sb("nega", [P, NT, NH])
        dcol = sb("dcol", [P, NT])
        qT = sb("qT", [P, S])
        kT = sb("kT", [P, S])
        vh = sb("vh", [P, NT, NH, DV1])
        wv = sb("wv", [P, NT - 1, NH, DV1])
        sgT = sb("sgT", [P, 2, S])
        num = sb("num", [P, NT, NH, DV1])
        tmpI = sb("tmpI", [P, NH, DV1])
        tmpU = sb("tmpU", [P, NH, DV1])
        cbd = sb("cbd", [P, NH, DV1])
        den = sb("den", [P, NT, NH])
        hoT = sb("hoT", [P, 2, S])
        vareps2 = sb("vareps2", [P, NT])
        rs2 = sb("rs2", [P, NT])
        h2 = sb("h2", [P, 2, NT, D])
        vareps3 = sb("vareps3", [P, NT])
        rs3 = sb("rs3", [P, NT])
        xnTh, xnTl = sb("xnTh", [P, 2, S], F32R), sb("xnTl", [P, 2, S], F32R)
        bstf = sb("bstf", [P, NT, 6])
        mvf = sb("mvf", [P, NT, 2])
        sp = sb("sp", [P, 4, S])
        conth = sb("conth", [2 * M, S], F32R)
        contl = sb("contl", [2 * M, S], F32R)
        lg = sb("lg", [P, NT, E])
        mx8 = sb("mx8", [P, NT, 8])
        ix8 = sb("ix8", [P, NT, 8], U32)
        ixf = sb("ixf", [P, NT, 2])
        dl = sb("dl", [P, NT])
        e2 = sb("e2", [P, NT])
        s1 = sb("s1", [P, NT])
        w12 = sb("w12", [P, NT, 2])
        eq0 = sb("eq0", [P, NT, E])
        eq1 = sb("eq1", [P, NT, E])
        g = sb("g", [P, NT, E])
        gT = sb("gT", [E, S])
        hid = sb("hid", [P, 4, S])
        oTh, oTl = sb("oTh", [2 * M, S], F32R), sb("oTl", [2 * M, S], F32R)
        r1T = sb("r1T", [M, S])
        vareps4 = sb("vareps4", [P, NT])
        rs4 = sb("rs4", [P, NT])
        gd = nc.dram_tensor("gd", (NT, NH, P), F32, kind="Internal").ap()
        gs = nc.dram_tensor("gs", (E, S), F32, kind="Internal").ap()

        X = [ctx.enter_context(nc.psum_tensor(f"X{i}", [P, 512], F32)) for i in range(5)]
        Y = [ctx.enter_context(nc.psum_tensor(f"Y{i}", [P, 512], F32)) for i in range(3)]

        passed = sem("passed")
        loaded = sem("loaded")
        tok_in = sem("tok_in")
        pconst = sem("pconst")
        mults = sem("mults")
        hashed = sem("hashed")
        hash_t = sem("hash_t")
        idx_ok = sem("idx_ok")
        prep = sem("prep")
        pprep = sem("pprep")
        gathered = [sem(f"gathered{u}") for u in range(2)]
        idx_copied = per("idx_copied", 1)
        eT_t, eT_ok = per("eT_t", 1), per("eT_ok", 2)
        hv_t, kg_t, hv_ok, kg_ok = per("hv_t", 4), per("kg_t", 4), per("hv_ok", 4), per("kg_ok", 4)
        st1, rs_ok, fi_ok, fiT_t, fi8_ok = per("st1", 3), per("rs_ok", 1), per("fi_ok", 2), per("fiT_t", 1), per("fi8_ok", 1)
        scan, dc_ok, exT_t, exs_ok = per("scan", 15), per("dc_ok", 1), per("exT_t", 1), per("exs_ok", 1)
        qk_t, kT_ok, qT_ok, qbd_ok = per("qk_t", 2), per("kT_ok", 1), per("qT_ok", 1), per("qbd_ok", 4)
        vh_ok, wv_ok, sg_ok, sgT_t, sgT_ok = per("vh_ok", 1), per("wv_ok", 3), per("sg_ok", 1), per("sgT_t", 1), per("sgT_ok", 1)
        gd_in, gw_in, relu_ok, masked, dm_ok = per("gd_in", 16), per("gw_in", 64), per("relu_ok", 4), per("masked", 4), per("dm_ok", 4)
        s_t, p_ok, num_t, int_t, u_t = per("s_t", 8), per("p_ok", 8), per("num_t", 4), per("int_t", 3), per("u_t", 3)
        num_ok, tmpi_ok, tmpu_ok, cbd_ok = per("num_ok", 4), per("tmpi_ok", 3), per("tmpu_ok", 2), per("cbd_ok", 3)
        nrm, rs2_ok, hn_ok, ho_ok = per("nrm", 10), per("rs2_ok", 1), per("hn_ok", 1), per("ho_ok", 2)
        hoT_t, hwT_ok = per("hoT_t", 2), per("hwT_ok", 2)
        y_t, h2_ok, st3, rs3_ok, xn_ok = per("y_t", 2), per("h2_ok", 2), per("st3", 3), per("rs3_ok", 1), per("xn_ok", 1)
        xnT_t, xnTa, xnTd = per("xnT_t", 2), per("xnTa", 2), per("xnTd", 2)
        enc_t, enc_ok, s2c_t, cont_ok = per("enc_t", 4), per("enc_ok", 4), per("s2c_t", 1), per("cont_ok", 2)
        r1_t, r1_ok, r2_t, top, e2_ok = per("r1_t", 1), per("r1_ok", 1), per("r2_t", 1), per("top", 13), per("e2_ok", 1)
        gT_t, gT_ok, gs_in, gb_in = per("gT_t", 1), per("gT_ok", 1), per("gs_in", 16), per("gb_in", 16)
        w1_t, hid_ok, w2_t, o_t, oT_ok = per("w1_t", 16), per("hid_ok", 16), per("w2_t", 16), per("o_t", 1), per("oT_ok", 2)
        c2s_t, c2s_ok, dec_t, z_ok, tt_ok = per("c2s_t", 4), per("c2s_ok", 4), per("dec_t", 2), per("z_ok", 2), per("tt_ok", 2)
        st4, rs4_ok, tn_ok, gg_ok, out_ok = per("st4", 3), per("rs4_ok", 1), per("tn_ok", 1), per("gg_ok", 2), per("out_ok", 1)
        stored = [sem(f"stored{u}") for u in range(2)]

        def mm3(mm, dst, wh, wl, xh, xl, start, stop):
            mm(dst, wh, xh, start=start, stop=False)
            mm(dst, wh, xl, start=False, stop=False)
            return mm(dst, wl, xh, start=False, stop=stop)

        AHEAD = {"g": 3, "h": 2, "c": 1, "t": 0, "f": 0, "x": -1, "l": -2}

        def order(names):
            return [(n.rstrip("0123456789"), *(int(d) for d in (n[len(n.rstrip("0123456789")):],) if d)) for n in names.split()]

        ORDER = {
            "pe": order(
                "t_y0 x_exp0 x_exp1 t_y1 x_exp2 x_sec0 x_exp3 x_exp4 c_s0 x_exp5 c_s1 x_sec1 c_u0 c_head0 c_head1 "
                "x_exp6 c_head2 c_head3 x_exp7 c_head4 c_head5 c_head6 x_exp8 c_head7 c_s2 c_s3 c_int1 x_sec2 c_u1 "
                "c_head8 x_exp9 c_head9 c_head10 c_head11 c_head12 x_sec3 c_head13 x_exp10 c_head14 x_exp11 "
                "c_head15 c_s4 x_sec4 c_s5 c_int2 x_sec5 c_u2 c_head16 c_head17 c_head18 c_head19 c_head20 c_head21 "
                "x_exp12 c_head22 c_head23 c_s6 c_int3 c_s7 t_xnT x_exp13 c_head24 c_head25 h_eT c_head26 c_head27 "
                "x_exp14 c_head28 c_head29 f_enc0 c_head30 c_head31 f_enc1 h_proj0 x_exp15 h_proj1 f_enc2 f_enc3 "
                "h_proj2 f_s2c h_proj3 x_sec6 f_route x_sec7 h_q f_logit x_c2s0 x_c2s1 h_gates x_c2s2 f_gT x_c2s3 "
                "h_k c_hoT x_dec0 h_sg x_dec1 h_ex"),
            "act": order(
                "c_relu0 c_exp0 c_relu1 c_exp1 c_relu2 c_exp2 c_relu3 c_exp3 t_xnT0 t_xnT1 h_eT h_proj0 f_enc0 "
                "f_enc1 f_enc2 f_enc3 h_proj1 h_proj2 h_proj3 f_route x_out f_top x_c2s0 x_c2s1 h_gates x_c2s2 "
                "x_c2s3 h_og h_k c_hoT0 c_hoT1 h_qbd0 h_qbd1 h_sg h_dc h_qbd2 x_dec0 x_dec1 h_ex h_qbd3"),
            "dve": order(
                "l_st x_exp0 x_exp1 l_norm x_exp2 x_exp3 x_exp4 x_exp5 c_p0 c_p1 c_u0 x_exp6 x_exp7 l_sum c_num0 "
                "t_y0 c_p2 c_p3 c_int1 t_y1 x_exp8 x_exp9 c_u1 t_st x_exp10 c_num1 x_exp11 c_p4 c_int2 c_p5 t_xn "
                "c_u2 c_num2 c_int3 c_p6 c_p7 x_exp12 t_xnT0 t_xnT1 x_exp13 h_eT x_exp14 c_num3 h_proj0 c_den "
                "h_proj1 c_hm h_proj2 x_exp15 c_norm f_s2c h_proj3 h_st x_out h_fi f_top f_gate h_q f_gT h_F h_G0 "
                "h_G1 h_G2 h_G3 c_hoT0 c_hoT1 h_ex x_dec0 x_dec1"),
            "pool": order(
                "l_st c_mask0 l_gain c_mask1 c_mask2 t_st c_mask3 c_norm h_st h_vh g_rows h_wv"),
            "sync": order(
                "c_gw0 c_gw1 c_gw2 c_gw3 f_gs l_store f_gates h_gd"),
        }

        def run_step(name, parts, b, u, half):
            for part, *arg in ORDER[name]:
                n = AHEAD[part[0]]
                if not (isinstance(b, int) and not 0 <= b + n < NB):
                    parts[part](b + n, (u + n) % 2, half + (u + n) // 2, *arg)

        def run_all(name, eng, parts):
            for b in range(-3, 3):
                run_step(name, parts, b, b % 2, b // 2)
            with eng.Fori(0, (NB - 6) // 2) as i:
                run_step(name, parts, i * 2 + 3, 1, i + 1)
                run_step(name, parts, i * 2 + 4, 0, i + 2)
            for b in range(NB - 3, NB + 2):
                run_step(name, parts, b, b % 2, b // 2)

        NLOADS = 31
        block = ctx.enter_context(nc.Block())

        @block.sync
        def _(sp_):
            sp_.dma_start(tok[:], A["tok"]).then_inc(tok_in, 16)
            sp_.dma_start(tokp[:], A["tokp"]).then_inc(tok_in, 16)
            loads = [(ident[:], A["ident"]), (headmask[:], A["headmask"]), (headsel[:], A["headsel"]),
                     (notstart[:], A["notstart"].broadcast_to((NH, S))), (iota8[:], A["iota8"].broadcast_to((P, E))),
                     (scale[:], A["scale"].broadcast_to((P, 1))), (projT[:], A["projT"]),
                     (wall[:], A["wall"].rearrange("(t p) n -> p t n", p=P)), (bfi[:], A["bfi"]),
                     (mixw[:], A["mixw"]), (mixb[:], A["mixb"]),
                     (woutT[:], A["woutT"].rearrange("(t p) n -> p t n", p=P)),
                     (encwr, A["encw"].rearrange("(t p) n -> p t n", p=P)), (encb[:], A["encb"]),
                     (s2cw[:], A["s2cw"].rearrange("(t p) n -> p t n", p=P)), (s2cb[0:M], A["s2cb"]), (s2cb[M:2 * M], A["s2cb"]),
                     (rw1raw[0:M], A["rw1"]), (rw1raw[M:2 * M], A["rw1"]), (rb1[:], A["rb1"]), (rw2[:], A["rw2"]), (rb2[:], A["rb2"].broadcast_to((P, E))),
                     (we1raw[0:M], A["we1"]), (we1raw[M:2 * M], A["we1"]), (be1n[:], A["be1"]), (be1pad, A["be1pad"].rearrange("p (c e) -> p c e", e=E)),
                     (we2[:], A["we2"].rearrange("p (c m) -> p c m", m=M)), (be2[:], A["be2"]),
                     (c2swr[0:M], A["c2sw"]), (c2swr[M:2 * M], A["c2sw"]), (c2sb[:], A["c2sb"]), (decw[:], A["decw"].rearrange("(t p) n -> p t n", p=P)),
                     (decb[:], A["decb"].broadcast_to((P, D))), (lng[:], A["lng"].broadcast_to((P, D))),
                     (lnb[:], A["lnb"].broadcast_to((P, D)))]
            assert len(loads) == NLOADS + 4
            for dst, src in loads:
                sp_.dma_start(dst, src).then_inc(loaded, 16)

            def h_gd(b, u, half):
                sp_.wait_ge(scan.sem, scan.at(b, 11))
                sp_.sem_inc(passed, 1)
                sp_.wait_ge(gw_in.sem, gw_in.at(b, 0))
                sp_.sem_inc(passed, 1)
                sp_.dma_start(gd.rearrange("c h t -> h c t"), G[:].rearrange("h (c t) -> h c t", t=P)).then_inc(gd_in.sem, 16)

            def c_gw(b, u, half, c):
                if c == 0:
                    sp_.wait_ge(gd_in.sem, gd_in.at(b, 16))
                    sp_.sem_inc(passed, 1)
                else:
                    sp_.wait_ge(gw_in.sem, gw_in.at(b, 16 * c))
                    sp_.sem_inc(passed, 1)
                sp_.wait_ge(num_t.sem, num_t.at(b, max(c - 1, 0)))
                sp_.sem_inc(passed, 1)
                sp_.dma_start(W[:, c % 2, :], gd[c].rearrange("h t -> (h t)").unsqueeze(0).broadcast_to((P, NH * P))).then_inc(gw_in.sem, 16)

            def f_gs(b, u, half):
                sp_.wait_ge(gT_ok.sem, gT_ok.at(b, 1))
                sp_.sem_inc(passed, 1)
                sp_.wait_ge(gb_in.sem, gb_in.at(b, 0))
                sp_.sem_inc(passed, 1)
                sp_.dma_start(gs, gT[:]).then_inc(gs_in.sem, 16)

            def f_gates(b, u, half):
                sp_.wait_ge(gs_in.sem, gs_in.at(b, 16))
                sp_.sem_inc(passed, 1)
                sp_.wait_ge(hid_ok.sem, hid_ok.at(b, 0))
                sp_.sem_inc(passed, 1)
                sp_.dma_start(gb[:], gs.unsqueeze(0).broadcast_to((P, E, S))).then_inc(gb_in.sem, 16)

            def l_store(b, u, half):
                sp_.wait_ge(out_ok.sem, out_ok.at(b, 1))
                dst = out[bass.ds(b * S, S), :].rearrange("(c p) d -> p c d", p=P)
                sp_.dma_start(dst, z[:]).then_inc(stored[u], 16)

            run_all("sync", sp_, {"h_gd": h_gd, "c_gw": c_gw, "f_gs": f_gs, "f_gates": f_gates, "l_store": l_store})
            for u in range(2):
                sp_.wait_ge(stored[u], 16 * NB // 2)

        LOADED = 16 * (NLOADS + 4)
        PREPARED = 28

        @block.gpsimd
        def _(pool):
            pool.memset(mulc[:], HASH_CUR).then_inc(pconst, 1)
            pool.memset(mulp[:], HASH_PREV).then_inc(pconst, 1)
            pool.memset(halves[:], 0.5).then_inc(pconst, 1)
            pool.memset(mhalf[:], -0.5).then_inc(pconst, 1)
            pool.memset(ex[:], 0.0).then_inc(pconst, 1)
            pool.memset(mst[:], 0.0).then_inc(pconst, 1)
            pool.wait_ge(pconst, 2)
            pool.wait_ge(tok_in, 32)
            pool.tensor_tensor(mulc[:], tok[:], mulc[:], ALU.mult).then_inc(mults, 1)
            pool.tensor_tensor(mulp[:], tokp[:], mulp[:], ALU.mult).then_inc(mults, 1)
            pool.wait_ge(pconst, 4)

            def g_rows(b, u, half):
                pool.wait_ge(gathered[u], half * 16 * NT)
                pool.tensor_copy(idxs[:, u, :], idx[:, bass.ds(b * NT, NT)]).then_inc(idx_copied.sem, 1)
                pool.wait_ge(idx_copied.sem, idx_copied.at(b, 1))
                if not (isinstance(b, int) and b < 2):
                    pool.wait_ge(eT_t.sem, eT_t.at(b - 1, 0))
                pool.sem_inc(passed, 1)
                for c in range(NT):
                    pool.indirect_dma_start(
                        out=e[:, u, c, :], out_offset=None, in_=A["emb"],
                        in_offset=bass.IndirectOffsetOnAxis(ap=idxs[:, u, c:c + 1].bitcast(U32), axis=0),
                    ).then_inc(gathered[u], 16)

            def h_st(b, u, half):
                pool.wait_ge(st1.sem, st1.at(b, 3))
                if not (isinstance(b, int) and b < 2):
                    pool.wait_ge(nrm.sem, nrm.at(b - 1, 0))
                pool.tensor_tensor(rs[:, u], vareps[:], mhalf[:], ALU.pow).then_inc(rs_ok.sem, 1)

            def h_vh(b, u, half):
                pool.wait_ge(rs_ok.sem, rs_ok.at(b, 1))
                pool.wait_ge(hv_ok.sem, hv_ok.at(b, 4))
                pool.wait_ge(num_t.sem, num_t.at(b, 0))
                pool.sem_inc(passed, 1)
                for c in range(NT):
                    pool.tensor_scalar(vh[:, c, :, 0:DV], v[:, c, :].rearrange("p (h d) -> p h d", d=DV),
                                       rs[:, u, c:c + 1], rs[:, u, c:c + 1], ALU.mult, ALU.mult)
                pool.tensor_copy(vh[:, :, :, DV], bc(rs[:, u, :], (P, NT, NH))).then_inc(vh_ok.sem, 1)

            def h_wv(b, u, half):
                pool.wait_ge(exs_ok.sem, exs_ok.at(b, 1))
                pool.wait_ge(vh_ok.sem, vh_ok.at(b, 1))
                pool.wait_ge(u_t.sem, u_t.at(b, 0))
                for c in range(NT - 1):
                    pool.tensor_tensor(wv[:, c], vh[:, c], bc(exs[:, c, 64:64 + NH], (P, NH, DV1)),
                                       ALU.mult).then_inc(wv_ok.sem, 1)

            def c_mask(b, u, half, c):
                pool.wait_ge(relu_ok.sem, relu_ok.at(b, c + 1))
                r = W[:, c % 2, :].rearrange("p (h t) -> p h t", t=P)
                pool.sem_inc(passed, 1)
                pool.affine_select(out=r, in_=r, compare_op=ALU.is_ge, fill=far, base=0,
                                   pattern=[[0, NH], [1, P]], channel_multiplier=-1).then_inc(masked.sem, 1)

            def c_norm(b, u, half):
                pool.wait_ge(nrm.sem, nrm.at(b, 10))
                pool.wait_ge(hn_ok.sem, hn_ok.at(b, 0))
                pool.tensor_tensor(rs2[:], vareps2[:], mhalf[:], ALU.pow).then_inc(rs2_ok.sem, 1)

            def t_st(b, u, half):
                pool.wait_ge(st3.sem, st3.at(b, 3))
                pool.wait_ge(xn_ok.sem, xn_ok.at(b, 0))
                pool.tensor_tensor(rs3[:], vareps3[:], mhalf[:], ALU.pow).then_inc(rs3_ok.sem, 1)

            def l_st(b, u, half):
                pool.wait_ge(st4.sem, st4.at(b, 3))
                pool.wait_ge(tn_ok.sem, tn_ok.at(b, 0))
                pool.tensor_tensor(rs4[:], vareps4[:], mhalf[:], ALU.pow).then_inc(rs4_ok.sem, 1)

            def l_gain(b, u, half):
                pool.wait_ge(tn_ok.sem, tn_ok.at(b, 1))
                pool.tensor_tensor(z[:], z[:], bc1(lng[:], (P, NT, D)), ALU.mult).then_inc(gg_ok.sem, 1)
                pool.wait_ge(gg_ok.sem, gg_ok.at(b, 1))
                pool.tensor_tensor(z[:], z[:], bc1(lnb[:], (P, NT, D)), ALU.add).then_inc(gg_ok.sem, 1)

            far = pool.to_reg(1e4)
            pool.wait_ge(idx_ok, 1)
            run_all("pool", pool, {"g_rows": g_rows, "h_st": h_st, "h_vh": h_vh, "h_wv": h_wv, "c_mask": c_mask,
                                   "c_norm": c_norm, "t_st": t_st, "l_st": l_st, "l_gain": l_gain})

        @block.scalar
        def _(act):
            act.wait_ge(prep, PREPARED)

            def h_eT(b, u, half):
                act.wait_ge(eT_t.sem, eT_t.at(b, 1))
                act.wait_ge(qk_t.sem, qk_t.at(b, 0))
                act.activation(eTh[:], X[0][:], ACT.Copy).then_inc(eT_ok.sem, 1)

            def h_proj(b, u, half, c):
                if c == 0:
                    if not (isinstance(b, int) and b < 2):
                        act.wait_ge(h2_ok.sem, h2_ok.at(b - 1, 0))
                    act.wait_ge(vh_ok.sem, vh_ok.at(b, 0))
                act.wait_ge(hv_t.sem, hv_t.at(b, c + 1))
                act.activation(hh[:, u, c, :], X[1 - c % 2][:, 0:D], ACT.Copy)
                act.activation(v[:, c, :], X[1 - c % 2][:, D:2 * D], ACT.Copy).then_inc(hv_ok.sem, 1)

            def h_gates(b, u, half):
                act.wait_ge(fiT_t.sem, fiT_t.at(b, 1))
                act.wait_ge(scan.sem, scan.at(b, 0))
                act.activation(fi8[:, 0, :], X[0][0:NH, :], ACT.Tanh, bias=bfi[:, 0:1], scale=1.0 / CAP)
                act.activation(fi8[:, 1, :], X[1][0:NH, :], ACT.Tanh, bias=bfi[:, 1:2],
                               scale=1.0 / CAP).then_inc(fi8_ok.sem, 1)

            def h_k(b, u, half):
                act.wait_ge(qk_t.sem, qk_t.at(b, 2))
                act.wait_ge(s_t.sem, s_t.at(b, 0))
                act.activation(kT[:], X[0][:], ACT.Copy).then_inc(kT_ok.sem, 1)

            def h_og(b, u, half):
                act.wait_ge(fi_ok.sem, fi_ok.at(b, 1))
                act.wait_ge(kg_ok.sem, kg_ok.at(b, 4))
                for c in range(NT):
                    ins = act.activation(kg[:, c, 0:D], kg[:, c, 0:D], ACT.Tanh, scale=rsh[:, c:c + 1])
                ins.then_inc(sg_ok.sem, 1)

            def h_qbd(b, u, half, j):
                act.wait_ge(qT_ok.sem, qT_ok.at(b, 1))
                act.wait_ge(s_t.sem, s_t.at(b, 0))
                for h in range(2 * j, 2 * j + 2):
                    ins = act.activation(qbd[:, h, :], qT[:], ACT.Copy, scale=headmask[:, h:h + 1])
                ins.then_inc(qbd_ok.sem, 1)

            def h_sg(b, u, half):
                act.wait_ge(sgT_t.sem, sgT_t.at(b, 1))
                act.wait_ge(ho_ok.sem, ho_ok.at(b, 0))
                act.activation(sgT[:, 0, :], X[0][:], ACT.Copy)
                act.activation(sgT[:, 1, :], X[1][:], ACT.Copy).then_inc(sgT_ok.sem, 1)

            def h_dc(b, u, half):
                act.wait_ge(scan.sem, scan.at(b, 15))
                act.activation(dc8[:], dcin[:], ACT.Exp).then_inc(dc_ok.sem, 1)

            def h_ex(b, u, half):
                act.wait_ge(exT_t.sem, exT_t.at(b, 1))
                act.wait_ge(wv_ok.sem, wv_ok.at(b, 0))
                act.wait_ge(nrm.sem, nrm.at(b, 0))
                x2 = X[2][:, :].rearrange("p (c n) -> p c n", n=P)
                act.activation(exs[:], x2[:, :, 32:104], ACT.Exp)
                act.activation(nega[:], x2[:, :, 0:NH], ACT.Copy, scale=-1.0)
                act.activation(dcol[:], X[0][:, 0:NT], ACT.Copy).then_inc(exs_ok.sem, 1)

            def c_relu(b, u, half, c):
                act.wait_ge(gw_in.sem, gw_in.at(b, 16 * c + 16))
                act.wait_ge(exs_ok.sem, exs_ok.at(b, 1))
                for h in range(NH):
                    ins = act.activation(W[:, c % 2, h * P:(h + 1) * P], W[:, c % 2, h * P:(h + 1) * P],
                                         ACT.Relu, bias=nega[:, c, h:h + 1])
                ins.then_inc(relu_ok.sem, 1)

            def c_exp(b, u, half, c):
                act.wait_ge(masked.sem, masked.at(b, c + 1))
                act.activation(W[:, c % 2, :], W[:, c % 2, :], ACT.Exp, scale=-1.0).then_inc(dm_ok.sem, 1)

            def c_hoT(b, u, half, k):
                act.wait_ge(y_t.sem, y_t.at(b, 0))
                act.wait_ge(hoT_t.sem, hoT_t.at(b, k + 1))
                act.activation(hoT[:, k, :], X[3 + k][:], ACT.Identity, bias=mixb[:, k:k + 1],
                               scale=mixw[:, k:k + 1]).then_inc(hwT_ok.sem, 1)

            def t_xnT(b, u, half, k):
                act.wait_ge(xnT_t.sem, xnT_t.at(b, k + 1))
                act.wait_ge(enc_t.sem, enc_t.at(b, 0))
                act.activation(xnTh[:, k, :], X[3 + k][:], ACT.Copy).then_inc(xnTa.sem, 1)

            def f_enc(b, u, half, m):
                act.wait_ge(enc_t.sem, enc_t.at(b, m + 1))
                act.wait_ge(s2c_t.sem, s2c_t.at(b, 0))
                act.activation(sp[:, m, :], X[3 + m % 2][:], ACT.Tanh, bias=encb[:, m:m + 1],
                               scale=0.5).then_inc(enc_ok.sem, 1)

            def f_route(b, u, half):
                act.wait_ge(r1_t.sem, r1_t.at(b, 1))
                act.wait_ge(r2_t.sem, r2_t.at(b, 0))
                act.activation(r1T[:], X[4][0:M, :], ACT.Tanh, bias=rb1[:]).then_inc(r1_ok.sem, 1)

            def f_top(b, u, half):
                act.wait_ge(top.sem, top.at(b, 3))
                act.activation(e2[:], dl[:], ACT.Exp).then_inc(e2_ok.sem, 1)

            def x_out(b, u, half):
                act.wait_ge(w2_t.sem, w2_t.at(b, NCH))
                act.wait_ge(c2s_t.sem, c2s_t.at(b, 0))
                act.activation(oTh[:], Y[2][:], ACT.Copy).then_inc(oT_ok.sem, 1)

            def x_c2s(b, u, half, m):
                act.wait_ge(c2s_t.sem, c2s_t.at(b, m + 1))
                act.activation(hid[:, m, :], Y[m % 2][:], ACT.Tanh, bias=c2sb[:, m:m + 1],
                               scale=0.5).then_inc(c2s_ok.sem, 1)

            def x_dec(b, u, half, j):
                act.wait_ge(z_ok.sem, z_ok.at(b, j + 1))
                act.activation(z[:, 2 * j:2 * j + 2, :], z[:, 2 * j:2 * j + 2, :], ACT.Tanh,
                               scale=0.5).then_inc(tt_ok.sem, 1)

            run_all("act", act, {"h_eT": h_eT, "h_proj": h_proj, "h_gates": h_gates, "h_k": h_k, "h_og": h_og,
                                 "h_sg": h_sg, "h_dc": h_dc, "h_ex": h_ex, "c_relu": c_relu, "c_exp": c_exp, "c_hoT": c_hoT,
                                 "t_xnT": t_xnT, "f_enc": f_enc, "f_route": f_route, "f_top": f_top, "h_qbd": h_qbd,
                                 "x_out": x_out, "x_c2s": x_c2s, "x_dec": x_dec})

        @block.vector
        def _(dve):
            dve.wait_ge(mults, 2)
            dve.tensor_tensor(hx[:], mulc[:], mulp[:], ALU.bitwise_xor).then_inc(hashed, 1)
            dve.wait_ge(hashed, 1)
            dve.tensor_scalar(hlo[:], hx[:], MOD, None, ALU.bitwise_and).then_inc(hashed, 1)
            dve.tensor_scalar(hhi[:], hx[:], 18, None, ALU.arith_shift_right).then_inc(hashed, 1)
            dve.wait_ge(hashed, 3)
            dve.tensor_tensor(hf[:], hlo[:], hhi[:], ALU.add).then_inc(hashed, 1)
            dve.wait_ge(hashed, 4)
            dve.tensor_scalar(hfix[:], hf[:], 0.0, float(MOD), ALU.is_lt, ALU.mult).then_inc(hashed, 1)
            dve.wait_ge(hashed, 5)
            dve.tensor_tensor(hf[:], hf[:], hfix[:], ALU.add).then_inc(hashed, 1)
            dve.wait_ge(hashed, 6)
            dve.tensor_scalar(hfix[:], hf[:], float(MOD), -float(MOD), ALU.is_ge, ALU.mult).then_inc(hashed, 1)
            dve.wait_ge(hashed, 7)
            dve.tensor_tensor(hf[:], hf[:], hfix[:], ALU.add).then_inc(hashed, 1)
            dve.wait_ge(hash_t, 1)
            dve.tensor_copy(idxf[:], X[0][:, 0:P]).then_inc(hashed, 1)
            dve.wait_ge(hashed, 9)
            dve.memset(idxf[0:1, 0:P:NT], float(MOD)).then_inc(hashed, 1)
            dve.wait_ge(hashed, 10)
            dve.tensor_copy(idx[:], idxf[:]).then_inc(idx_ok, 1)
            dve.wait_ge(loaded, LOADED)
            dve.tensor_scalar(wfold[:, CH:CV], projT[:], scale[:, 0:1], None, ALU.mult).then_inc(prep, 1)
            dve.wait_ge(prep, 1)
            dve.bn_stats(bst[:, 0, :], wfold[:, CH:CV]).then_inc(prep, 1)
            dve.wait_ge(prep, 2)
            dve.bn_aggr(mv[:, 0, :], bst[:, 0, :]).then_inc(prep, 1)
            dve.wait_ge(prep, 3)
            dve.tensor_scalar(projTc[:], wfold[:, CH:CV], mv[:, 0, 0:1], None, ALU.subtract).then_inc(prep, 1)
            dve.tensor_copy(blockmask[:], bc(headmask[:], (P, NH, DV1))).then_inc(prep, 1)
            dve.tensor_scalar(encb[:], encb[:], 0.5, None, ALU.mult).then_inc(prep, 1)
            dve.tensor_scalar(c2sb[:], c2sb[:], 0.5, None, ALU.mult).then_inc(prep, 1)
            dve.tensor_scalar(bfi[:], bfi[:], 1.0 / CAP, None, ALU.mult).then_inc(prep, 1)
            dve.tensor_scalar(be1n[:], be1n[:], -1.0, None, ALU.mult).then_inc(prep, 1)
            dve.tensor_scalar(woutT[:], woutT[:], 0.5, None, ALU.mult).then_inc(prep, 1)
            dve.tensor_scalar(s2cwh[:, :, 0:M], s2cw[:], 0.5, None, ALU.mult)
            dve.tensor_scalar(s2cwh[:, :, M:2 * M], s2cw[:], 0.5, None, ALU.mult).then_inc(prep, 1)
            dve.wait_ge(pprep, 1)
            dve.tensor_scalar(decw[:], decw[:], 0.5, None, ALU.mult).then_inc(prep, 1)
            dve.tensor_tensor(s2cb[:], X[1][:, 0:1], s2cb[:], ALU.add).then_inc(prep, 1)
            dve.tensor_tensor(decb[:], X[2][:, 0:D], decb[:], ALU.add).then_inc(prep, 1)
            dve.tensor_tensor(biasout[:], X[3][0:E, 0:M], be2[:], ALU.add).then_inc(prep, 1)
            dve.wait_ge(pprep, 2)
            dve.tensor_copy(projc[:], X[4][:, 0:2 * P].rearrange("p (t n) -> p t n", n=P)).then_inc(prep, 1)
            dve.wait_ge(pprep, 3)
            half_w = (CEND - CV) // 2
            dve.tensor_copy(wfold[:, CV:CV + half_w], Y[0][:, 0:half_w]).then_inc(prep, 1)
            dve.tensor_copy(wfold[:, CV + half_w:CEND], Y[1][:, 0:half_w]).then_inc(prep, 1)
            for dst, src in ((we1, we1raw), (rw1, rw1raw), (encwh, encwr), (c2swh, c2swr)):
                dve.tensor_copy(dst[:], src).then_inc(prep, 1)
            dve.wait_ge(prep, 18)
            dve.tensor_copy(wfh[:], wfold).then_inc(prep, 1)
            dve.wait_ge(prep, 23)
            for dst, src in ((we1, we1raw), (rw1, rw1raw)):
                dve.tensor_tensor(dst[M:2 * M], src[M:2 * M], dst[M:2 * M].bitcast(F32), ALU.subtract).then_inc(prep, 1)
            for dst, src, high in ((encwl, encwr, encwh), (c2swl, c2swr, c2swh), (wfl, wfold, wfh)):
                dve.tensor_tensor(dst[:], src, high[:].bitcast(F32), ALU.subtract).then_inc(prep, 1)

            def h_eT(b, u, half):
                dve.wait_ge(eT_ok.sem, eT_ok.at(b, 1))
                dve.tensor_tensor(eTl[:], X[0][:], eTh[:].bitcast(F32), ALU.subtract).then_inc(eT_ok.sem, 1)

            def h_proj(b, u, half, c):
                if c == 0:
                    dve.wait_ge(sgT_t.sem, sgT_t.at(b, 0))
                    dve.wait_ge(u_t.sem, u_t.at(b, 0))
                dve.wait_ge(kg_t.sem, kg_t.at(b, c + 1))
                dve.tensor_copy(kg[:, c, :], X[2][:, 0:NKG]).then_inc(kg_ok.sem, 1)

            def h_st(b, u, half):
                dve.wait_ge(hv_ok.sem, hv_ok.at(b, 4))
                for c in range(NT):
                    ins = dve.bn_stats(bst[:, c, :], hh[:, u, c, :])
                ins.then_inc(st1.sem, 1)
                dve.wait_ge(st1.sem, st1.at(b, 1))
                dve.sem_inc(passed, 1)
                for c in range(NT):
                    ins = dve.bn_aggr(mv[:, c, :], bst[:, c, :])
                ins.then_inc(st1.sem, 1)
                dve.wait_ge(st1.sem, st1.at(b, 2))
                dve.wait_ge(rs_ok.sem, rs_ok.at(b, 0))
                dve.tensor_scalar(vareps[:], mv[:, :, 1], 1e-5, None, ALU.add).then_inc(st1.sem, 1)

            def h_fi(b, u, half):
                dve.wait_ge(rs_ok.sem, rs_ok.at(b, 1))
                dve.wait_ge(sg_ok.sem, sg_ok.at(b, 0))
                dve.tensor_scalar(rsh[:], rs[:, u], 0.5, None, ALU.mult).then_inc(fi_ok.sem, 1)
                dve.wait_ge(kg_ok.sem, kg_ok.at(b, 4))
                dve.wait_ge(fiT_t.sem, fiT_t.at(b, 0))
                for k in range(2):
                    ins = dve.tensor_tensor(fi[:, k], kg[:, :, CF - CO + k * NH:CF - CO + (k + 1) * NH],
                                            bc(rs[:, u, :], (P, NT, NH)), ALU.mult)
                ins.then_inc(fi_ok.sem, 1)

            def h_q(b, u, half):
                dve.wait_ge(qk_t.sem, qk_t.at(b, 1))
                dve.wait_ge(int_t.sem, int_t.at(b, 0))
                dve.tensor_copy(qT[:], X[2][:]).then_inc(qT_ok.sem, 1)

            Gv = G[:, :].rearrange("p (c t) -> p c t", t=P)
            exv = ex[:, :].rearrange("p (c t) -> p c t", t=P)

            def h_F(b, u, half):
                dve.wait_ge(fi8_ok.sem, fi8_ok.at(b, 1))
                dve.tensor_scalar(fi8[:], fi8[:], CAP, None, ALU.mult).then_inc(scan.sem, 1)
                dve.wait_ge(scan.sem, scan.at(b, 1))
                dve.tensor_tensor_scan(Fs[:], notstart[:], fi8[:, 0, :], 0.0, ALU.mult, ALU.add).then_inc(scan.sem, 1)
                dve.wait_ge(scan.sem, scan.at(b, 2))
                dve.wait_ge(exT_t.sem, exT_t.at(b, 0))
                dve.tensor_tensor(ex[0:NH, :], fi8[:, 1, :], Fs[:], ALU.subtract).then_inc(scan.sem, 1)

            def h_G(b, u, half, c):
                t, last = slice(c * P, (c + 1) * P), (c + 1) * P
                dve.wait_ge(scan.sem, scan.at(b, 3 + 2 * c))
                if c == 0:
                    dve.wait_ge(gd_in.sem, gd_in.at(b, 0))
                dve.tensor_tensor_scan(G[:, t], ex[0:NH, t], ex[0:NH, t], mst[:, c:c + 1], ALU.max,
                                       ALU.max).then_inc(scan.sem, 1)
                dve.wait_ge(scan.sem, scan.at(b, 4 + 2 * c))
                dve.tensor_tensor(mst[:, c + 1:c + 2], G[:, last - 1:last], Fs[:, last - 1:last],
                                  ALU.add).then_inc(scan.sem, 1)

            def h_ex(b, u, half):
                dve.wait_ge(scan.sem, scan.at(b, 11))
                dve.wait_ge(dc_ok.sem, dc_ok.at(b, 0))
                dve.tensor_tensor(dcin[:], mst[:, 0:NT], Gv[:, :, P - 1], ALU.subtract).then_inc(scan.sem, 1)
                dve.tensor_tensor(exv[64:64 + NH], bc(mst[:, 0:NT], (NH, NT, P)), Gv,
                                  ALU.subtract).then_inc(scan.sem, 1)
                dve.tensor_tensor(exv[96:96 + NH], exv[0:NH], bc(Gv[:, :, P - 1], (NH, NT, P)),
                                  ALU.subtract).then_inc(scan.sem, 1)
                dve.scalar_tensor_tensor(out=ex[32:32 + NH, :], in0=G[:], scalar=-1.0, in1=Fs[:],
                                         op0=ALU.mult, op1=ALU.subtract).then_inc(scan.sem, 1)

            def c_p(b, u, half, n):
                c, j = n // 2, n % 2
                dve.wait_ge(s_t.sem, s_t.at(b, n + 1))
                dve.wait_ge(dm_ok.sem, dm_ok.at(b, c + 1))
                w = slice(j * 512, (j + 1) * 512)
                dve.tensor_tensor(W[:, c % 2, w], X[j][:], W[:, c % 2, w], ALU.mult).then_inc(p_ok.sem, 1)

            flat = "p h d -> p (h d)"

            def c_int(b, u, half, c):
                dve.wait_ge(int_t.sem, int_t.at(b, c))
                dve.wait_ge(num_ok.sem, num_ok.at(b, c))
                dve.tensor_tensor(tmpI[:], X[2][:, 0:NH * DV1].rearrange("p (h d) -> p h d", d=DV1),
                                  bc(exs[:, c, 32:32 + NH], (P, NH, DV1)), ALU.mult).then_inc(tmpi_ok.sem, 1)

            def c_u(b, u, half, c):
                dve.wait_ge(u_t.sem, u_t.at(b, c + 1))
                upd = X[0][:, 0:NH * DV1].rearrange("p (h d) -> p h d", d=DV1)
                if c == 0:
                    dve.wait_ge(int_t.sem, int_t.at(b, 0))
                    dve.tensor_tensor(cbd[:], upd, blockmask[:], ALU.mult).then_inc(cbd_ok.sem, 1)
                    return
                dve.wait_ge(cbd_ok.sem, cbd_ok.at(b, c))
                dve.tensor_tensor(tmpU[:], upd, blockmask[:], ALU.mult).then_inc(tmpu_ok.sem, 1)
                dve.wait_ge(tmpu_ok.sem, tmpu_ok.at(b, c))
                dve.wait_ge(int_t.sem, int_t.at(b, c))
                dve.scalar_tensor_tensor(out=cbd[:].rearrange(flat), in0=cbd[:].rearrange(flat),
                                         scalar=dcol[:, c:c + 1], in1=tmpU[:].rearrange(flat),
                                         op0=ALU.mult, op1=ALU.add).then_inc(cbd_ok.sem, 1)

            def c_num(b, u, half, c):
                dve.wait_ge(num_t.sem, num_t.at(b, c + 1))
                new = X[2][:, 0:NH * DV1]
                if c == 0:
                    dve.tensor_copy(num[:, c].rearrange(flat), new).then_inc(num_ok.sem, 1)
                else:
                    dve.wait_ge(tmpi_ok.sem, tmpi_ok.at(b, c))
                    dve.tensor_tensor(num[:, c].rearrange(flat), new, tmpI[:].rearrange(flat),
                                      ALU.add).then_inc(num_ok.sem, 1)

            def c_den(b, u, half):
                n = 0

                def step(ins):
                    nonlocal n
                    ins.then_inc(nrm.sem, 1)
                    n += 1
                    if n < 6:
                        dve.wait_ge(nrm.sem, nrm.at(b, n))

                dve.wait_ge(num_ok.sem, num_ok.at(b, 4))
                rsb = bc(rs[:, u, :], (P, NT, NH))
                step(dve.tensor_tensor(den[:], num[:, :, :, DV], rsb, ALU.mult))
                step(dve.scalar_tensor_tensor(out=den[:], in0=den[:], scalar=-1.0, in1=den[:],
                                              op0=ALU.mult, op1=ALU.max))
                step(dve.scalar_tensor_tensor(out=den[:], in0=den[:], scalar=DQK ** -0.5, in1=exs[:, :, 0:NH],
                                              op0=ALU.mult, op1=ALU.max))
                step(dve.tensor_scalar(den[:], den[:], 1e-6, None, ALU.add))
                step(dve.reciprocal(den[:], den[:]))
                step(dve.scalar_tensor_tensor(out=den[:], in0=den[:], scalar=DQK ** -0.5, in1=rsb,
                                              op0=ALU.mult, op1=ALU.mult))

            def c_hm(b, u, half):
                dve.wait_ge(nrm.sem, nrm.at(b, 6))
                dve.wait_ge(xnT_t.sem, xnT_t.at(b, 0))
                for c in range(NT):
                    ins = dve.tensor_tensor(hm[:, c].rearrange("p (h d) -> p h d", d=DV), num[:, c, :, 0:DV],
                                            bc(den[:, c], (P, NH, DV)), ALU.mult)
                ins.then_inc(nrm.sem, 1)
                dve.wait_ge(nrm.sem, nrm.at(b, 7))
                for c in range(NT):
                    ins = dve.bn_stats(bst2[:, c, :], hm[:, c, :])
                ins.then_inc(nrm.sem, 1)
                dve.wait_ge(nrm.sem, nrm.at(b, 8))
                dve.sem_inc(passed, 1)
                for c in range(NT):
                    ins = dve.bn_aggr(mv2[:, c, :], bst2[:, c, :])
                ins.then_inc(nrm.sem, 1)
                dve.wait_ge(nrm.sem, nrm.at(b, 9))
                dve.tensor_scalar(vareps2[:], mv2[:, :, 1], 1e-6, None, ALU.add).then_inc(nrm.sem, 1)

            def c_norm(b, u, half):
                dve.wait_ge(rs2_ok.sem, rs2_ok.at(b, 1))
                for c in range(NT):
                    ins = dve.tensor_scalar(hm[:, c, :], hm[:, c, :], mv2[:, c, 0:1], rs2[:, c:c + 1],
                                            ALU.subtract, ALU.mult)
                ins.then_inc(hn_ok.sem, 1)

            def c_hoT(b, u, half, k):
                dve.wait_ge(hwT_ok.sem, hwT_ok.at(b, k + 1))
                dve.wait_ge(sgT_ok.sem, sgT_ok.at(b, 1))
                dve.scalar_tensor_tensor(out=hoT[:, k, :], in0=sgT[:, k, :], scalar=1.0, in1=hoT[:, k, :],
                                         op0=ALU.add, op1=ALU.mult).then_inc(ho_ok.sem, 1)

            def t_y(b, u, half, j):
                dve.wait_ge(y_t.sem, y_t.at(b, j + 1))
                if not (isinstance(b, int) and b < 2):
                    dve.wait_ge(out_ok.sem, out_ok.at(b - 1, 0))
                dve.tensor_tensor(h2[:, u, 2 * j:2 * j + 2, :], X[3 + j][:, :].rearrange("p (c d) -> p c d", d=D),
                                  hh[:, u, 2 * j:2 * j + 2, :], ALU.add).then_inc(h2_ok.sem, 1)

            def t_st(b, u, half):
                dve.wait_ge(h2_ok.sem, h2_ok.at(b, 2))
                for c in range(NT):
                    ins = dve.bn_stats(bst3[:, c, :], h2[:, u, c, :])
                ins.then_inc(st3.sem, 1)
                dve.wait_ge(st3.sem, st3.at(b, 1))
                dve.sem_inc(passed, 1)
                for c in range(NT):
                    ins = dve.bn_aggr(mv3[:, c, :], bst3[:, c, :])
                ins.then_inc(st3.sem, 1)
                dve.wait_ge(st3.sem, st3.at(b, 2))
                dve.tensor_scalar(vareps3[:], mv3[:, :, 1], 1e-5, None, ALU.add).then_inc(st3.sem, 1)

            def t_xn(b, u, half):
                dve.wait_ge(rs3_ok.sem, rs3_ok.at(b, 1))
                dve.wait_ge(hoT_t.sem, hoT_t.at(b, 2))
                for c in range(NT):
                    ins = dve.tensor_scalar(hm[:, c, :], h2[:, u, c, :], mv3[:, c, 0:1], rs3[:, c:c + 1],
                                            ALU.subtract, ALU.mult)
                ins.then_inc(xn_ok.sem, 1)

            def t_xnT(b, u, half, k):
                dve.wait_ge(xnTa.sem, xnTa.at(b, k + 1))
                dve.tensor_tensor(xnTl[:, k, :], X[3 + k][:], xnTh[:, k, :].bitcast(F32), ALU.subtract).then_inc(xnTd.sem, 1)

            def f_s2c(b, u, half):
                dve.wait_ge(s2c_t.sem, s2c_t.at(b, 1))
                dve.wait_ge(w1_t.sem, w1_t.at(b, 0))
                dve.tensor_scalar(conth[:], X[3][:], s2cb[:, 0:1], None, ALU.add).then_inc(cont_ok.sem, 1)
                dve.wait_ge(cont_ok.sem, cont_ok.at(b, 1))
                dve.scalar_tensor_tensor(out=contl[:], in0=X[3][:], scalar=s2cb[:, 0:1], in1=conth[:].bitcast(F32),
                                         op0=ALU.add, op1=ALU.subtract).then_inc(cont_ok.sem, 1)

            def f_top(b, u, half):
                dve.wait_ge(r2_t.sem, r2_t.at(b, 1))
                dve.tensor_tensor(lg[:], X[3][:, 0:NT * E].rearrange("p (c x) -> p c x", x=E),
                                  bc1(rb2[:], (P, NT, E)), ALU.add).then_inc(top.sem, 1)
                dve.wait_ge(top.sem, top.at(b, 1))
                dve.sem_inc(passed, 1)
                for c in range(NT):
                    ins = dve.max(mx8[:, c, :], lg[:, c, :])
                ins.then_inc(top.sem, 1)
                dve.wait_ge(top.sem, top.at(b, 2))
                dve.wait_ge(e2_ok.sem, e2_ok.at(b, 0))
                dve.tensor_tensor(dl[:], mx8[:, :, 1], mx8[:, :, 0], ALU.subtract).then_inc(top.sem, 1)
                dve.sem_inc(passed, 1)
                for c in range(NT):
                    ins = dve.max_index(ix8[:, c, :], mx8[:, c, :], lg[:, c, :])
                ins.then_inc(top.sem, 1)
                dve.wait_ge(top.sem, top.at(b, 4))
                dve.tensor_copy(ixf[:], ix8[:, :, 0:2]).then_inc(top.sem, 1)
                dve.wait_ge(top.sem, top.at(b, 5))
                iot = bc1(iota8[:], (P, NT, E))
                dve.tensor_tensor(eq0[:], iot, bc(ixf[:, :, 0], (P, NT, E)), ALU.is_equal).then_inc(top.sem, 1)
                dve.tensor_tensor(eq1[:], iot, bc(ixf[:, :, 1], (P, NT, E)), ALU.is_equal).then_inc(top.sem, 1)

            def f_gate(b, u, half):
                dve.wait_ge(e2_ok.sem, e2_ok.at(b, 1))
                dve.tensor_scalar(s1[:], e2[:], 1.0, None, ALU.add).then_inc(top.sem, 1)
                dve.wait_ge(top.sem, top.at(b, 8))
                dve.reciprocal(w12[:, :, 0], s1[:]).then_inc(top.sem, 1)
                dve.wait_ge(top.sem, top.at(b, 9))
                dve.tensor_tensor(w12[:, :, 1], e2[:], w12[:, :, 0], ALU.mult).then_inc(top.sem, 1)
                dve.tensor_tensor(eq0[:], eq0[:], bc(w12[:, :, 0], (P, NT, E)), ALU.mult).then_inc(top.sem, 1)
                dve.wait_ge(top.sem, top.at(b, 10))
                dve.tensor_tensor(eq1[:], eq1[:], bc(w12[:, :, 1], (P, NT, E)), ALU.mult).then_inc(top.sem, 1)
                dve.wait_ge(top.sem, top.at(b, 12))
                dve.wait_ge(gT_t.sem, gT_t.at(b, 0))
                dve.tensor_tensor(g[:], eq0[:], eq1[:], ALU.add).then_inc(top.sem, 1)

            def f_gT(b, u, half):
                dve.wait_ge(gT_t.sem, gT_t.at(b, 1))
                dve.wait_ge(o_t.sem, o_t.at(b, 0))
                dve.wait_ge(gs_in.sem, gs_in.at(b, 0))
                dve.tensor_copy(gT[:], X[4][0:E, :]).then_inc(gT_ok.sem, 1)

            def x_exp(b, u, half, ch):
                dve.wait_ge(w1_t.sem, w1_t.at(b, ch + 1))
                dve.wait_ge(gb_in.sem, gb_in.at(b, 16))
                if ch < 4:
                    dve.wait_ge(dec_t.sem, dec_t.at(b, 0))
                else:
                    dve.wait_ge(w2_t.sem, w2_t.at(b, ch - 3))
                dve.scalar_tensor_tensor(out=hid[:, ch % 4, :], in0=Y[ch % 2][:], scalar=be1n[:, ch:ch + 1],
                                         in1=gb[:, ch // 2, :], op0=ALU.max, op1=ALU.mult).then_inc(hid_ok.sem, 1)

            def x_out(b, u, half):
                dve.wait_ge(oT_ok.sem, oT_ok.at(b, 1))
                dve.tensor_tensor(oTl[:], Y[2][:], oTh[:].bitcast(F32), ALU.subtract).then_inc(oT_ok.sem, 1)

            def x_dec(b, u, half, j):
                dve.wait_ge(dec_t.sem, dec_t.at(b, j + 1))
                if j == 0:
                    dve.wait_ge(stored[1 - u], (half + u) * 16)
                dve.tensor_tensor(z[:, 2 * j:2 * j + 2, :], Y[j][:, :].rearrange("p (c d) -> p c d", d=D),
                                  bc1(decb[:], (P, 2, D)), ALU.add).then_inc(z_ok.sem, 1)

            def l_st(b, u, half):
                dve.wait_ge(tt_ok.sem, tt_ok.at(b, 2))
                for c in range(NT):
                    ins = dve.bn_stats(bstf[:, c, :], z[:, c, :])
                ins.then_inc(st4.sem, 1)
                dve.wait_ge(st4.sem, st4.at(b, 1))
                dve.sem_inc(passed, 1)
                for c in range(NT):
                    ins = dve.bn_aggr(mvf[:, c, :], bstf[:, c, :])
                ins.then_inc(st4.sem, 1)
                dve.wait_ge(st4.sem, st4.at(b, 2))
                dve.tensor_scalar(vareps4[:], mvf[:, :, 1], 4e-5, None, ALU.add).then_inc(st4.sem, 1)

            def l_norm(b, u, half):
                dve.wait_ge(rs4_ok.sem, rs4_ok.at(b, 1))
                for c in range(NT):
                    ins = dve.tensor_scalar(z[:, c, :], z[:, c, :], mvf[:, c, 0:1], rs4[:, c:c + 1],
                                            ALU.subtract, ALU.mult)
                ins.then_inc(tn_ok.sem, 1)

            def l_sum(b, u, half):
                dve.wait_ge(gg_ok.sem, gg_ok.at(b, 2))
                dve.tensor_tensor(z[:], z[:], h2[:, u], ALU.add).then_inc(out_ok.sem, 1)

            run_all("dve", dve, {"h_proj": h_proj, "h_st": h_st, "h_fi": h_fi, "h_eT": h_eT, "h_q": h_q, "x_out": x_out, "h_F": h_F,
                                 "h_G": h_G, "h_ex": h_ex, "c_p": c_p, "c_int": c_int, "c_u": c_u, "c_num": c_num, "c_den": c_den,
                                 "c_hm": c_hm, "c_norm": c_norm, "c_hoT": c_hoT, "t_y": t_y, "t_st": t_st, "t_xn": t_xn,
                                 "t_xnT": t_xnT, "f_s2c": f_s2c, "f_top": f_top, "f_gate": f_gate, "f_gT": f_gT,
                                 "x_exp": x_exp, "x_dec": x_dec, "l_st": l_st, "l_norm": l_norm, "l_sum": l_sum})

        @block.tensor
        def _(pe):
            mm = pe.matmul
            pe.wait_ge(loaded, LOADED)
            pe.wait_ge(hashed, 8)
            pe.transpose(X[0][:, 0:P], hf[:], ident[:]).then_inc(hash_t, 1)
            pe.wait_ge(pconst, 6)
            for k in range(4):
                for x in range(2):
                    mm(X[1][x * M:(x + 1) * M, 0:1], s2cw[:, k, :], halves[:, 0:1], start=k == 0, stop=k == 3)
            for k in range(4):
                mm(X[2][:, 0:D], halves[:], decw[:, k, :], start=k == 0, stop=k == 3)
            pe.wait_ge(prep, 9)
            for ch in range(NCH):
                ins = mm(X[3][0:E, 0:M], be1pad[:, ch, :], we2[:, ch, :], start=ch == 0, stop=ch == NCH - 1)
            ins.then_inc(pprep, 1)
            for t in range(2):
                ins = pe.transpose(X[4][:, t * P:(t + 1) * P], projTc[:, t * P:(t + 1) * P], ident[:])
            ins.then_inc(pprep, 1)
            pe.wait_ge(prep, 16)
            half_w = (CEND - CV) // 2
            for j in range(2):
                for t in range(2):
                    ins = mm(Y[j][:, 0:half_w], projc[:, t, :], wall[:, t, j * half_w:(j + 1) * half_w],
                             start=t == 0, stop=t == 1)
            ins.then_inc(pprep, 1)
            pe.wait_ge(prep, PREPARED)

            def h_eT(b, u, half):
                pe.wait_ge(gathered[u], (half + 1) * 16 * NT)
                pe.wait_ge(p_ok.sem, p_ok.at(b, 0))
                for c in range(NT):
                    ins = pe.transpose(X[0][:, c * P:(c + 1) * P], e[:, u, c, :], ident[:])
                ins.then_inc(eT_t.sem, 1)

            def h_proj(b, u, half, c):
                if c == 0:
                    pe.wait_ge(eT_ok.sem, eT_ok.at(b, 2))
                    pe.wait_ge(p_ok.sem, p_ok.at(b, 0))
                    pe.wait_ge(num_ok.sem, num_ok.at(b, 0))
                th, tl = eTh[:, c * P:(c + 1) * P], eTl[:, c * P:(c + 1) * P]
                if c >= 2:
                    pe.wait_ge(hv_ok.sem, hv_ok.at(b, c - 1))
                mm3(mm, X[1 - c % 2][:], th, tl, wfh[:, CH:CO], wfl[:, CH:CO], True, True).then_inc(hv_t.sem, 1)
                if c >= 1:
                    pe.wait_ge(kg_ok.sem, kg_ok.at(b, c))
                mm3(mm, X[2][:, 0:NKG], th, tl, wfh[:, CO:CQ], wfl[:, CO:CQ], True, True).then_inc(kg_t.sem, 1)

            def h_gates(b, u, half):
                pe.wait_ge(fi_ok.sem, fi_ok.at(b, 2))
                pe.wait_ge(hv_ok.sem, hv_ok.at(b, 4))
                for k in range(2):
                    for c in range(NT):
                        ins = pe.transpose(X[k][0:NH, c * P:(c + 1) * P], fi[:, k, c, :], ident[:])
                ins.then_inc(fiT_t.sem, 1)

            def h_q(b, u, half):
                pe.wait_ge(kg_ok.sem, kg_ok.at(b, 4))
                mm3(mm, X[2][:], wfh[:, CQ:CEND], wfl[:, CQ:CEND], eTh[:], eTl[:], True, True).then_inc(qk_t.sem, 1)

            def h_k(b, u, half):
                pe.wait_ge(fi8_ok.sem, fi8_ok.at(b, 1))
                mm3(mm, X[0][:], wfh[:, CK:CQ], wfl[:, CK:CQ], eTh[:], eTl[:], True, True).then_inc(qk_t.sem, 1)

            def h_sg(b, u, half):
                pe.wait_ge(sg_ok.sem, sg_ok.at(b, 1))
                pe.wait_ge(kT_ok.sem, kT_ok.at(b, 1))
                for k in range(2):
                    for c in range(NT):
                        ins = pe.transpose(X[k][:, c * P:(c + 1) * P], kg[:, c, k * P:(k + 1) * P], ident[:])
                ins.then_inc(sgT_t.sem, 1)

            def h_ex(b, u, half):
                pe.wait_ge(scan.sem, scan.at(b, 15))
                pe.wait_ge(qT_ok.sem, qT_ok.at(b, 1))
                pe.wait_ge(sgT_ok.sem, sgT_ok.at(b, 1))
                for c in range(NT):
                    pe.transpose(X[2][:, c * P:c * P + 104], ex[0:104, c * P:(c + 1) * P], ident[0:104, 0:104])
                pe.wait_ge(dc_ok.sem, dc_ok.at(b, 1))
                mm(X[0][:, 0:NT], headsel[:], dc8[:], start=True, stop=True).then_inc(exT_t.sem, 1)

            def c_s(b, u, half, n):
                c, j = n // 2, n % 2
                if n == 0:
                    pe.wait_ge(qbd_ok.sem, qbd_ok.at(b, 4))
                    pe.wait_ge(exs_ok.sem, exs_ok.at(b, 1))
                elif j == 1:
                    if c > 0:
                        pe.wait_ge(p_ok.sem, p_ok.at(b, n - 1))
                elif c == 1:
                    pe.wait_ge(cbd_ok.sem, cbd_ok.at(b, 1))
                else:
                    pe.wait_ge(tmpu_ok.sem, tmpu_ok.at(b, c - 1))
                mm(X[j][:], kT[:, c * P:(c + 1) * P], qbd[:, 4 * j:4 * j + 4, c * P:(c + 1) * P],
                   start=True, stop=True).then_inc(s_t.sem, 1)

            def c_u(b, u, half, c):
                pe.wait_ge(wv_ok.sem, wv_ok.at(b, c + 1))
                pe.wait_ge(p_ok.sem, p_ok.at(b, 2 * c + 1))
                mm(X[0][:, 0:NH * DV1], kg[:, c, CK - CO:CQ - CO], wv[:, c].rearrange("p h d -> p (h d)"),
                   start=True, stop=True).then_inc(u_t.sem, 1)

            def c_int(b, u, half, c):
                pe.wait_ge(cbd_ok.sem, cbd_ok.at(b, c))
                pe.wait_ge(num_ok.sem, num_ok.at(b, c))
                mm(X[2][:, 0:NH * DV1], qT[:, c * P:(c + 1) * P], cbd[:].rearrange("p h d -> p (h d)"),
                   start=True, stop=True).then_inc(int_t.sem, 1)

            def c_head(b, u, half, n):
                c, h = n // NH, n % NH
                if h == 0:
                    pe.wait_ge(p_ok.sem, p_ok.at(b, 2 * c + 2))
                    pe.wait_ge(vh_ok.sem, vh_ok.at(b, 1))
                    if c > 0:
                        pe.wait_ge(tmpi_ok.sem, tmpi_ok.at(b, c))
                ins = mm(X[2][:, h * DV1:(h + 1) * DV1], W[:, c % 2, h * P:(h + 1) * P], vh[:, c, h, :],
                         start=True, stop=True)
                if h == NH - 1:
                    ins.then_inc(num_t.sem, 1)

            def c_hoT(b, u, half):
                pe.wait_ge(hn_ok.sem, hn_ok.at(b, 1))
                pe.wait_ge(gT_ok.sem, gT_ok.at(b, 0))
                for k in range(2):
                    for c in range(NT):
                        ins = pe.transpose(X[3 + k][:, c * P:(c + 1) * P], hm[:, c, k * P:(k + 1) * P], ident[:])
                    ins.then_inc(hoT_t.sem, 1)

            def t_y(b, u, half, j):
                pe.wait_ge(ho_ok.sem, ho_ok.at(b, 2))
                for c in range(2):
                    for k in range(2):
                        ins = mm(X[3 + j][:, c * D:(c + 1) * D], hoT[:, k, (2 * j + c) * P:(2 * j + c + 1) * P],
                                 woutT[:, k, :], start=k == 0, stop=k == 1)
                ins.then_inc(y_t.sem, 1)

            def t_xnT(b, u, half):
                pe.wait_ge(xn_ok.sem, xn_ok.at(b, 1))
                for k in range(2):
                    for c in range(NT):
                        ins = pe.transpose(X[3 + k][:, c * P:(c + 1) * P], hm[:, c, k * P:(k + 1) * P], ident[:])
                    ins.then_inc(xnT_t.sem, 1)

            def f_enc(b, u, half, m):
                if m == 0:
                    pe.wait_ge(xnTd.sem, xnTd.at(b, 2))
                if m >= 2:
                    pe.wait_ge(enc_ok.sem, enc_ok.at(b, m - 1))
                for k in range(2):
                    w = slice(m * P, (m + 1) * P)
                    ins = mm3(mm, X[3 + m % 2][:], encwh[:, k, w], encwl[:, k, w], xnTh[:, k, :], xnTl[:, k, :], k == 0, k == 1)
                ins.then_inc(enc_t.sem, 1)

            def f_s2c(b, u, half):
                pe.wait_ge(enc_ok.sem, enc_ok.at(b, 4))
                for k in range(4):
                    ins = mm(X[3][:], s2cwh[:, k, :], sp[:, k, :], start=k == 0, stop=k == 3)
                ins.then_inc(s2c_t.sem, 1)

            def f_route(b, u, half):
                pe.wait_ge(cont_ok.sem, cont_ok.at(b, 2))
                mm(X[4][0:M, :], rw1[:], conth[:], start=True, stop=False)
                mm(X[4][0:M, :], rw1[:], contl[:], start=False, stop=True).then_inc(r1_t.sem, 1)

            def f_logit(b, u, half):
                pe.wait_ge(r1_ok.sem, r1_ok.at(b, 1))
                for c in range(NT):
                    ins = mm(X[3][:, c * E:(c + 1) * E], r1T[:, c * P:(c + 1) * P], rw2[:], start=True, stop=True)
                ins.then_inc(r2_t.sem, 1)

            def f_gT(b, u, half):
                pe.wait_ge(top.sem, top.at(b, 13))
                for c in range(NT):
                    ins = pe.transpose(X[4][0:E, c * P:(c + 1) * P], g[:, c, :], ident[:])
                ins.then_inc(gT_t.sem, 1)

            def x_exp(b, u, half, ch):
                if ch == 0:
                    pe.wait_ge(cont_ok.sem, cont_ok.at(b, 2))
                    pe.wait_ge(z_ok.sem, z_ok.at(b, 0))
                if ch >= 2:
                    pe.wait_ge(hid_ok.sem, hid_ok.at(b, ch - 1))
                w = we1[:, ch * P:(ch + 1) * P]
                mm(Y[ch % 2][:], w, conth[:], start=True, stop=False)
                mm(Y[ch % 2][:], w, contl[:], start=False, stop=True).then_inc(w1_t.sem, 1)

            def x_sec(b, u, half, j):
                if j == 0:
                    pe.wait_ge(gT_ok.sem, gT_ok.at(b, 1))
                    pe.wait_ge(oT_ok.sem, oT_ok.at(b, 0))
                    mm(Y[2][0:M, :], biasout[:], gT[:], start=True, stop=False).then_inc(o_t.sem, 1)
                pe.wait_ge(hid_ok.sem, hid_ok.at(b, 2 * j + 2))
                for ch in (2 * j, 2 * j + 1):
                    x = ch % 2 * M
                    mm(Y[2][x:x + M, :], we2[:, ch, :], hid[:, ch % 4, :], start=ch == 1,
                       stop=j == NCH // 2 - 1).then_inc(w2_t.sem, 1)

            def x_c2s(b, u, half, m):
                if m == 0:
                    pe.wait_ge(oT_ok.sem, oT_ok.at(b, 2))
                if m >= 2:
                    pe.wait_ge(c2s_ok.sem, c2s_ok.at(b, m - 1))
                w = slice(m * P, (m + 1) * P)
                mm3(mm, Y[m % 2][:], c2swh[:, w], c2swl[:, w], oTh[:], oTl[:], True, True).then_inc(c2s_t.sem, 1)

            def x_dec(b, u, half, j):
                pe.wait_ge(c2s_ok.sem, c2s_ok.at(b, 4))
                for c in range(2):
                    for k in range(4):
                        t = (2 * j + c) * P
                        ins = mm(Y[j][:, c * D:(c + 1) * D], hid[:, k, t:t + P], decw[:, k, :], start=k == 0, stop=k == 3)
                ins.then_inc(dec_t.sem, 1)

            run_all("pe", pe, {"h_eT": h_eT, "h_proj": h_proj, "h_gates": h_gates, "h_q": h_q, "h_k": h_k, "h_sg": h_sg,
                               "h_ex": h_ex, "c_s": c_s, "c_u": c_u, "c_int": c_int, "c_head": c_head, "c_hoT": c_hoT,
                               "t_y": t_y, "t_xnT": t_xnT, "f_enc": f_enc, "f_s2c": f_s2c, "f_route": f_route, "f_logit": f_logit,
                               "f_gT": f_gT, "x_exp": x_exp, "x_sec": x_sec, "x_c2s": x_c2s,
                               "x_dec": x_dec})


def kernel(**inputs):
    import numpy as np
    import concourse.bacc as bacc
    from concourse.bass_utils import run_bass_kernel_spmd

    a = {k: np.ascontiguousarray(v) for k, v in inputs.items()}
    f = np.float32

    def attn(n):
        return a["L0_attn_" + n]

    def ffn(n):
        return a["L0_ffn_" + n]

    x = a["x"].reshape(-1)
    be1 = ffn("be1").reshape(NCH, P)
    be1pad = np.zeros((P, NCH, E), f)
    for ch in range(NCH):
        be1pad[:, ch, ch // (HE // P)] = be1[ch]
    heads = np.repeat(np.eye(NH, dtype=f), DQK, axis=1)
    notstart = np.ones((1, S), f)
    notstart[:, ::P] = 0
    arrays = {
        "tok": x.reshape(TILES, P), "tokp": np.roll(x, 1).reshape(TILES, P),
        "emb": a["L0_tok_emb_weight"], "projT": a["L0_tok_proj_weight"].T, "scale": a["L0_tok_scale"].reshape(1, 1),
        "ident": np.eye(P, dtype=f), "headmask": heads.T, "headsel": heads, "notstart": notstart,
        "iota8": np.arange(E, dtype=f)[None],
        "wall": np.concatenate([attn(n) for n in ("Wv", "Wog", "Wf", "Wi", "Wk", "Wq")], axis=0).T,
        "bfi": np.stack([attn("bf"), attn("bi")], axis=1), "mixw": attn("ln_w").reshape(2, P).T,
        "mixb": attn("ln_b").reshape(2, P).T,
        "woutT": attn("Wout").T, "encw": ffn("enc_W"), "encb": ffn("enc_b").reshape(4, P).T,
        "s2cw": ffn("s2c_W"), "s2cb": ffn("s2c_b")[:, None], "rw1": ffn("rW1"), "rb1": ffn("rb1")[:, None],
        "rw2": ffn("rW2"), "rb2": ffn("rb2")[None], "we1": ffn("We1").transpose(1, 0, 2).reshape(M, E * HE),
        "be1": be1.T, "be1pad": be1pad.reshape(P, NCH * E),
        "we2": ffn("We2").reshape(NCH, P, M).transpose(1, 0, 2).reshape(P, NCH * M), "be2": ffn("be2"),
        "c2sw": ffn("c2s_W"), "c2sb": ffn("c2s_b").reshape(4, P).T, "decw": ffn("dec_W"), "decb": ffn("dec_b")[None],
        "lng": ffn("ln_g")[None], "lnb": ffn("ln_b")[None],
    }
    nc = bacc.Bacc("TRN2", target_bir_lowering=False, num_devices=1)
    feed, aps = {}, {}
    for name, arr in arrays.items():
        arr = np.ascontiguousarray(arr)
        feed["in_" + name] = arr
        aps[name] = nc.dram_tensor("in_" + name, arr.shape, mybir.dt.from_np(arr.dtype), kind="ExternalInput").ap()
    out = nc.dram_tensor("out", (NB * S, D), F32, kind="ExternalOutput").ap()
    tower(nc, aps, out)
    r = run_bass_kernel_spmd(nc, [feed], core_ids=[0])
    return r.results[0]["out"].reshape(NB, S, D)
```
